# Optimizing a Trainium2 kernel written in Bass

```python
import numpy as np
import jax
import jax.numpy as jnp

def _softmax(x, axis=-1):
    return jax.nn.softmax(x, axis=axis)

def _gelu(x):
    return jax.nn.gelu(x, approximate=True)

def _silu(x):
    return jax.nn.silu(x)

def _sigmoid(x):
    return jax.nn.sigmoid(x)

def _layernorm(x, axis=-1, eps=1e-05):
    m = jnp.mean(x, axis=axis, keepdims=True)
    v = jnp.var(x, axis=axis, keepdims=True)
    return (x - m) / jnp.sqrt(v + eps)

def _scatter_add(tgt, idx, src, axis=0):
    return tgt.at[idx].add(src)

def _segment_sum(src, seg, n):
    return jax.ops.segment_sum(src, seg, n)
kernel_name = 'mk_decoder_preln_d1_seqx_r8_756cb6'

def setup_inputs(seed: int=0):
    np.random.seed(seed)
    _w = jnp.asarray

    def _rec_inputs():
        import jax
        import jax.numpy as jnp
        _rk = jax.random.key(seed)
        x = 7.22e-05 + 1 * jax.random.normal(jax.random.fold_in(_rk, 1), (4, 256, 256), jnp.float32)
        _lenS = 256 - jax.random.randint(jax.random.fold_in(_rk, 7), (4,), 0, max(1, 256 // 4) + 1, jnp.int32)
        _lenS2 = 256 - jax.random.randint(jax.random.fold_in(_rk, 8), (4,), 0, max(1, 256 // 4) + 1, jnp.int32)
        _ctx_1024P = jax.random.normal(jax.random.fold_in(_rk, 11), (4, 16, 128), jnp.float32)
        _ctx_1024c = jax.random.dirichlet(jax.random.fold_in(_rk, 511), 0.3 * jnp.ones((16,), jnp.float32), (4, 256))
        _ctx_1024t = jnp.einsum('bsk,bkd->bsd', _ctx_1024c, _ctx_1024P)
        _ctx_1024t = _ctx_1024t * jax.lax.rsqrt(jnp.mean(jnp.square(_ctx_1024t)) + 1e-12) * 0.953939
        ctx_1024 = 2.81802e-05 + 1.00001 * (_ctx_1024t + 0.3 * jax.random.normal(jax.random.fold_in(_rk, 611), (4, 256, 128), jnp.float32))
        return (x, ctx_1024)
    x, ctx_1024 = _rec_inputs()

    def _L0_attn_setup():
        import jax, jax.numpy as jnp
        import numpy as np
        from jax import lax
        B, L, D = (2, 256, 256)
        H, DK, DV, K = (16, 128, 128, 4)
        Q_DIM = H * DK
        V_DIM = H * DV

        def silu(x):
            return x * jax.nn.sigmoid(x)

        def causal_dwconv(x, w, b):
            Kk = w.shape[1]
            xp = jnp.pad(x, ((0, 0), (Kk - 1, 0), (0, 0)))
            kern = w.T[:, None, :]
            y = lax.conv_general_dilated(xp, kern, window_strides=(1,), padding='VALID', dimension_numbers=('NWC', 'WIO', 'NWC'), feature_group_count=w.shape[0])
            return y + b

        def layernorm(x, w, b, eps=1e-05):
            m = jnp.mean(x, axis=-1, keepdims=True)
            var = jnp.mean((x - m) ** 2, axis=-1, keepdims=True)
            return (x - m) * lax.rsqrt(var + eps) * w + b
        key = jax.random.key(seed)
        ks = jax.random.split(key, 16)
        s = 0.02
        f32 = jnp.float32
        return {'hidden_states': jax.random.normal(ks[0], (B, L, D), f32), 'Wq': jax.random.normal(ks[1], (D, Q_DIM), f32) * s, 'Wk': jax.random.normal(ks[2], (D, Q_DIM), f32) * s, 'Wv': jax.random.normal(ks[3], (D, V_DIM), f32) * s, 'Wb': jax.random.normal(ks[4], (D, H), f32) * s, 'bb': jnp.full((H,), -2.0, f32), 'Wg': jax.random.normal(ks[5], (D, V_DIM), f32) * s, 'Wo': jax.random.normal(ks[6], (V_DIM, D), f32) * s, 'qconv_w': jax.random.normal(ks[7], (Q_DIM, K), f32) * 0.5, 'qconv_b': jnp.zeros((Q_DIM,), f32), 'kconv_w': jax.random.normal(ks[8], (Q_DIM, K), f32) * 0.5, 'kconv_b': jnp.zeros((Q_DIM,), f32), 'qn_w': jnp.ones((DK,), f32), 'qn_b': jnp.zeros((DK,), f32), 'kn_w': jnp.ones((DK,), f32), 'kn_b': jnp.zeros((DK,), f32)}
    _L0_attn_all = _L0_attn_setup()
    _L0_attn_in = {k: v for k, v in _L0_attn_all.items() if k in ('Wq', 'Wk', 'Wv', 'Wb', 'bb', 'Wg', 'Wo', 'qconv_w', 'qconv_b', 'kconv_w', 'kconv_b', 'qn_w', 'qn_b', 'kn_w', 'kn_b')}
    del _L0_attn_all

    def _L0_xattn_setup():
        import jax, jax.numpy as jnp
        import numpy as np
        key = jax.random.key(seed)
        ks = jax.random.split(key, 6)
        B, L, N, C, D = (8, 64, 256, 128, 128)
        return {'teacher_logits': jax.random.normal(ks[0], (B, L, N), dtype=jnp.float32), 'teacher_features': jax.random.normal(ks[1], (B, N, C), dtype=jnp.float32), 'Wq': jax.random.normal(ks[2], (D, C), dtype=jnp.float32) * (1.0 / np.sqrt(C)), 'bq': jnp.zeros((D,), dtype=jnp.float32), 'Wk': jax.random.normal(ks[3], (D, C), dtype=jnp.float32) * (1.0 / np.sqrt(C)), 'bk': jnp.zeros((D,), dtype=jnp.float32)}
    _L0_xattn_all = _L0_xattn_setup()
    _L0_xattn_in = {k: v for k, v in _L0_xattn_all.items() if k in ('Wq', 'bq', 'Wk', 'bk')}
    del _L0_xattn_all

    def _L0_ffn_setup():
        import jax, jax.numpy as jnp
        import numpy as np
        N_EXPERTS = 16
        TOP_K = 4
        N_GROUP = 4
        TOPK_GROUP = 2
        NORM_TOPK = True
        ROUTED_SCALE = 2.5
        H = 256
        F_MOE = 128
        F_SHARED = 256
        B, S = (2, 256)

        def _route(hidden, gate_weight, bias):
            T = hidden.shape[0]
            epg = N_EXPERTS // N_GROUP
            logits = hidden @ gate_weight.T
            scores = jax.nn.sigmoid(logits)
            scores_for_choice = scores + bias[None, :]
            grp = scores_for_choice.reshape(T, N_GROUP, epg)
            group_scores = jax.lax.top_k(grp, 2)[0].sum(-1)
            group_idx = jax.lax.top_k(group_scores, TOPK_GROUP)[1]
            group_mask = jax.nn.one_hot(group_idx, N_GROUP, dtype=jnp.bool_).any(1)
            score_mask = jnp.repeat(group_mask, epg, axis=-1)
            masked = jnp.where(score_mask, scores_for_choice, -jnp.inf)
            topk_idx = jax.lax.top_k(masked, TOP_K)[1]
            topk_weight = jnp.take_along_axis(scores, topk_idx, axis=1)
            return (topk_weight, topk_idx)

        def _swiglu(x, gw, uw, dw):
            return jax.nn.silu(x @ gw.T) * (x @ uw.T) @ dw.T
        key = jax.random.key(seed)
        ks = jax.random.split(key, 9)
        std = 0.02
        return {'hidden_states': jax.random.normal(ks[0], (B, S, H), jnp.float32), 'gate_weight': jax.random.normal(ks[1], (N_EXPERTS, H), jnp.float32) * std, 'e_score_correction_bias': jnp.zeros((N_EXPERTS,), jnp.float32), 'gate_w': jax.random.normal(ks[2], (N_EXPERTS, F_MOE, H), jnp.float32) * std, 'up_w': jax.random.normal(ks[3], (N_EXPERTS, F_MOE, H), jnp.float32) * std, 'down_w': jax.random.normal(ks[4], (N_EXPERTS, H, F_MOE), jnp.float32) * std, 'sh_gate_w': jax.random.normal(ks[5], (F_SHARED, H), jnp.float32) * std, 'sh_up_w': jax.random.normal(ks[6], (F_SHARED, H), jnp.float32) * std, 'sh_down_w': jax.random.normal(ks[7], (H, F_SHARED), jnp.float32) * std}
    _L0_ffn_all = _L0_ffn_setup()
    _L0_ffn_in = {k: v for k, v in _L0_ffn_all.items() if k in ('gate_weight', 'e_score_correction_bias', 'gate_w', 'up_w', 'down_w', 'sh_gate_w', 'sh_up_w', 'sh_down_w')}
    del _L0_ffn_all
    return {'x': x, 'ctx_1024': ctx_1024, 'L0_attn_Wq': _L0_attn_in['Wq'], 'L0_attn_Wk': _L0_attn_in['Wk'], 'L0_attn_Wv': _L0_attn_in['Wv'], 'L0_attn_Wb': _L0_attn_in['Wb'], 'L0_attn_bb': _L0_attn_in['bb'], 'L0_attn_Wg': _L0_attn_in['Wg'], 'L0_attn_Wo': _L0_attn_in['Wo'], 'L0_attn_qconv_w': _L0_attn_in['qconv_w'], 'L0_attn_qconv_b': _L0_attn_in['qconv_b'], 'L0_attn_kconv_w': _L0_attn_in['kconv_w'], 'L0_attn_kconv_b': _L0_attn_in['kconv_b'], 'L0_attn_qn_w': _L0_attn_in['qn_w'], 'L0_attn_qn_b': _L0_attn_in['qn_b'], 'L0_attn_kn_w': _L0_attn_in['kn_w'], 'L0_attn_kn_b': _L0_attn_in['kn_b'], 'L0_xattn_Wq': _L0_xattn_in['Wq'], 'L0_xattn_bq': _L0_xattn_in['bq'], 'L0_xattn_Wk': _L0_xattn_in['Wk'], 'L0_xattn_bk': _L0_xattn_in['bk'], 'L0_ffn_gate_weight': _L0_ffn_in['gate_weight'], 'L0_ffn_e_score_correction_bias': _L0_ffn_in['e_score_correction_bias'], 'L0_ffn_gate_w': _L0_ffn_in['gate_w'], 'L0_ffn_up_w': _L0_ffn_in['up_w'], 'L0_ffn_down_w': _L0_ffn_in['down_w'], 'L0_ffn_sh_gate_w': _L0_ffn_in['sh_gate_w'], 'L0_ffn_sh_up_w': _L0_ffn_in['sh_up_w'], 'L0_ffn_sh_down_w': _L0_ffn_in['sh_down_w']}

def reference(x, ctx_1024, L0_attn_Wq, L0_attn_Wk, L0_attn_Wv, L0_attn_Wb, L0_attn_bb, L0_attn_Wg, L0_attn_Wo, L0_attn_qconv_w, L0_attn_qconv_b, L0_attn_kconv_w, L0_attn_kconv_b, L0_attn_qn_w, L0_attn_qn_b, L0_attn_kn_w, L0_attn_kn_b, L0_xattn_Wq, L0_xattn_bq, L0_xattn_Wk, L0_xattn_bk, L0_ffn_gate_weight, L0_ffn_e_score_correction_bias, L0_ffn_gate_w, L0_ffn_up_w, L0_ffn_down_w, L0_ffn_sh_gate_w, L0_ffn_sh_up_w, L0_ffn_sh_down_w):
    import jax
    import jax.numpy as jnp

    def _L0_attn_ref(hidden_states, Wq, Wk, Wv, Wb, bb, Wg, Wo, qconv_w, qconv_b, kconv_w, kconv_b, qn_w, qn_b, kn_w, kn_b):
        import jax, jax.numpy as jnp
        import numpy as np
        from jax import lax
        B, L, D = (2, 256, 256)
        H, DK, DV, K = (16, 128, 128, 4)
        Q_DIM = H * DK
        V_DIM = H * DV

        def silu(x):
            return x * jax.nn.sigmoid(x)

        def causal_dwconv(x, w, b):
            Kk = w.shape[1]
            xp = jnp.pad(x, ((0, 0), (Kk - 1, 0), (0, 0)))
            kern = w.T[:, None, :]
            y = lax.conv_general_dilated(xp, kern, window_strides=(1,), padding='VALID', dimension_numbers=('NWC', 'WIO', 'NWC'), feature_group_count=w.shape[0])
            return y + b

        def layernorm(x, w, b, eps=1e-05):
            m = jnp.mean(x, axis=-1, keepdims=True)
            var = jnp.mean((x - m) ** 2, axis=-1, keepdims=True)
            return (x - m) * lax.rsqrt(var + eps) * w + b
        Bs, Ls, Ds = hidden_states.shape
        q = hidden_states @ Wq
        k = hidden_states @ Wk
        v = hidden_states @ Wv
        beta = jax.nn.sigmoid(hidden_states @ Wb + bb)
        gate = silu(hidden_states @ Wg)
        q = silu(causal_dwconv(q, qconv_w, qconv_b))
        k = silu(causal_dwconv(k, kconv_w, kconv_b))
        q = layernorm(q.reshape(Bs, Ls, H, DK), qn_w, qn_b)
        k = layernorm(k.reshape(Bs, Ls, H, DK), kn_w, kn_b)
        v = v.reshape(Bs, Ls, H, DV)
        qs = q.transpose(1, 0, 2, 3)
        ks_ = k.transpose(1, 0, 2, 3)
        vs = v.transpose(1, 0, 2, 3)
        bs = beta.transpose(1, 0, 2)
        S0 = jnp.zeros((Bs, H, DV, DK), hidden_states.dtype)

        def step(S, inp):
            q_t, k_t, v_t, b_t = inp
            b = b_t[..., None, None]
            S = (1.0 - b) * S + b * (v_t[..., :, None] * k_t[..., None, :])
            o_t = jnp.einsum('bhvk,bhk->bhv', S, q_t)
            return (S, o_t)
        _, os = lax.scan(step, S0, (qs, ks_, vs, bs))
        o = os.transpose(1, 0, 2, 3).reshape(Bs, Ls, H * DV)
        o = o * gate
        return o @ Wo

    def _L0_xattn_ref(teacher_logits, teacher_features, Wq, bq, Wk, bk):
        import jax, jax.numpy as jnp
        import numpy as np
        query = jnp.einsum('bnc,dc->bnd', teacher_features, Wq) + bq
        key = jnp.einsum('bnc,dc->bnd', teacher_features, Wk) + bk
        energy = jnp.einsum('bnd,bmd->bnm', query, key)
        attention = jax.nn.softmax(energy, axis=-1)
        x_m = jnp.einsum('bln,bmn->blm', teacher_logits, attention)
        return x_m

    def _L0_ffn_ref(hidden_states, gate_weight, e_score_correction_bias, gate_w, up_w, down_w, sh_gate_w, sh_up_w, sh_down_w):
        import jax, jax.numpy as jnp
        import numpy as np
        N_EXPERTS = 16
        TOP_K = 4
        N_GROUP = 4
        TOPK_GROUP = 2
        NORM_TOPK = True
        ROUTED_SCALE = 2.5
        H = 256
        F_MOE = 128
        F_SHARED = 256
        B, S = (2, 256)

        def _route(hidden, gate_weight, bias):
            T = hidden.shape[0]
            epg = N_EXPERTS // N_GROUP
            logits = hidden @ gate_weight.T
            scores = jax.nn.sigmoid(logits)
            scores_for_choice = scores + bias[None, :]
            grp = scores_for_choice.reshape(T, N_GROUP, epg)
            group_scores = jax.lax.top_k(grp, 2)[0].sum(-1)
            group_idx = jax.lax.top_k(group_scores, TOPK_GROUP)[1]
            group_mask = jax.nn.one_hot(group_idx, N_GROUP, dtype=jnp.bool_).any(1)
            score_mask = jnp.repeat(group_mask, epg, axis=-1)
            masked = jnp.where(score_mask, scores_for_choice, -jnp.inf)
            topk_idx = jax.lax.top_k(masked, TOP_K)[1]
            topk_weight = jnp.take_along_axis(scores, topk_idx, axis=1)
            return (topk_weight, topk_idx)

        def _swiglu(x, gw, uw, dw):
            return jax.nn.silu(x @ gw.T) * (x @ uw.T) @ dw.T
        Bh, Sh, Hh = hidden_states.shape
        hidden = hidden_states.reshape(-1, Hh)
        topk_weight, topk_idx = _route(hidden, gate_weight, e_score_correction_bias)
        if NORM_TOPK:
            topk_weight = topk_weight / (topk_weight.sum(-1, keepdims=True) + 1e-20)
        topk_weight = topk_weight * ROUTED_SCALE
        one_hot = jax.nn.one_hot(topk_idx, N_EXPERTS, dtype=topk_weight.dtype)
        weight_matrix = (one_hot * topk_weight[..., None]).sum(1)
        g = jnp.einsum('th,nfh->ntf', hidden, gate_w)
        u = jnp.einsum('th,nfh->ntf', hidden, up_w)
        act = jax.nn.silu(g) * u
        routed = jnp.einsum('ntf,nhf,tn->th', act, down_w, weight_matrix)
        out = routed + _swiglu(hidden, sh_gate_w, sh_up_w, sh_down_w)
        return out.reshape(Bh, Sh, Hh)
    x = x + _L0_attn_ref(_layernorm(x, axis=-1), L0_attn_Wq, L0_attn_Wk, L0_attn_Wv, L0_attn_Wb, L0_attn_bb, L0_attn_Wg, L0_attn_Wo, L0_attn_qconv_w, L0_attn_qconv_b, L0_attn_kconv_w, L0_attn_kconv_b, L0_attn_qn_w, L0_attn_qn_b, L0_attn_kn_w, L0_attn_kn_b)
    x = x + _L0_xattn_ref(_layernorm(x, axis=-1), ctx_1024, L0_xattn_Wq, L0_xattn_bq, L0_xattn_Wk, L0_xattn_bk)
    x = x + _L0_ffn_ref(_layernorm(x, axis=-1), L0_ffn_gate_weight, L0_ffn_e_score_correction_bias, L0_ffn_gate_w, L0_ffn_up_w, L0_ffn_down_w, L0_ffn_sh_gate_w, L0_ffn_sh_up_w, L0_ffn_sh_down_w)
    return x

_drawn_inputs = setup_inputs


def setup_inputs(seed=0):
    import zlib

    import numpy as np

    out = dict(_drawn_inputs(seed))
    spreads = {'L0_attn_bb': (-2.0, 0.2),
     'L0_attn_qconv_b': (0.0, 0.1),
     'L0_attn_kconv_b': (0.0, 0.1),
     'L0_attn_qn_w': (1.0, 0.2),
     'L0_attn_qn_b': (0.0, 0.568),
     'L0_attn_kn_w': (1.0, 0.2),
     'L0_attn_kn_b': (0.0, 0.549),
     'L0_xattn_bq': (0.0, 0.1),
     'L0_xattn_bk': (0.0, 0.8),
     'L0_ffn_e_score_correction_bias': (0.0, 0.77)}
    factors = {'L0_ffn_gate_weight': 6.628,
     'L0_ffn_gate_w': 4.971,
     'L0_ffn_up_w': 4.928,
     'L0_ffn_down_w': 4.917,
     'L0_ffn_sh_gate_w': 4.424,
     'L0_ffn_sh_up_w': 4.385,
     'L0_ffn_sh_down_w': 4.374}
    for name, (base, spread) in spreads.items():
        noise = np.random.default_rng([zlib.crc32(name.encode()), seed]).standard_normal(out[name].shape)
        drawn = base * np.exp(spread * noise) if base else spread * noise
        out[name] = jnp.asarray(drawn.astype(out[name].dtype))
    for name, factor in factors.items():
        out[name] = (out[name] * factor).astype(out[name].dtype)
    return out
```

```python
from contextlib import ExitStack

import concourse.bass as bass
from concourse import mybir

F32 = mybir.dt.float32
F32R = mybir.dt.float32r
I32 = mybir.dt.int32
ALU = mybir.AluOpType
ACT = mybir.ActivationFunctionType
AX = mybir.AxisListType

P = 128
B, L, D = 4, 256, 256
T = B * L
TT = T // P
KT = D // P
N = 512
NCH = T // N
BPC = N // L
H = 16
G = 4
NG = H // G
TAPS = 4
PRM = TAPS + 3
DW = L + P
E_ROUTED, E_SHARED = 16, 2
E_ALL = E_ROUTED + E_SHARED
EG = 4
EPG = E_ROUTED // EG
TOPK_GROUP, TOP_K = 2, 4
ROUTED_SCALE = 2.5
EPS = 1e-5
RSQRT_SEED = 1597463007.0
VERY_NEGATIVE = -3.0e38

C_HEAD = B + NCH
C_GROUP = G * C_HEAD + TT + TT // 2


def c_scores(g, k):
    return TT + C_GROUP * g + C_HEAD * k


def c_outputs(g, k):
    return c_scores(g, k) + B


def c_values(g):
    return TT + C_GROUP * g + C_HEAD * G


def c_project(g):
    return c_values(g) + TT


def head(g, k):
    if isinstance(g, int):
        n = G * g + k
        return n // G, n % G
    return g, k


def units(g, k, per, more=0):
    return g * (G * per) + (k * per + more)


def uses(g, k, ring):
    return g * (G // ring) + (k // ring + 1)


class Steps:

    def __init__(self, eng, sem, body=0):
        self.eng, self.sem, self.n, self.g, self.body = eng, sem, 0, 0, body

    def did(self, ins):
        ins.then_inc(self.sem, 1)
        self.n += 1
        return self.n

    def after(self, n):
        if self.n and n:
            self.eng.wait_ge(self.sem, self.g * self.body + n)

    def enter(self, g):
        self.g, self.start = g, self.n

    def leave(self, rounds):
        assert self.n - self.start == self.body, (self.n - self.start, self.body)
        self.g, self.n = 0, self.n + self.body * (rounds - 1)


def decoder_layer(nc, x_in, ctx_in, xw_in, xb_in, wb_in, bb_in, wh_in, prm_in, wv_in, wo_in,
                  rw_in, rb_in, we_in, ident_in, tie_in, out):
    obet_rows = nc.dram_tensor("obet_rows", [H, B * DW], F32).ap()
    route_rows = nc.dram_tensor("route_rows", [E_ROUTED, T], F32).ap()

    ctx = ExitStack()
    with ctx:
        def sb(name, cols, dt=F32, parts=P):
            return ctx.enter_context(nc.sbuf_tensor(name, [parts, cols], dt))

        def sem(name):
            return ctx.enter_context(nc.semaphore(name))

        ident = sb("ident", P)
        tie = sb("tie", E_ROUTED * E_ROUTED + EG * EG)
        x = sb("x", TT * D)
        xT_hi = sb("xT_hi", KT * T, F32R)
        xT_lo = sb("xT_lo", KT * T, F32R)
        xT = sb("xT", KT * T)
        attT = sb("attT", KT * T)
        dmask = sb("dmask", B * DW)
        beta_tok = sb("beta_tok", TT * H)
        w_raw = sb("w_raw", 2 * 3 * D)
        w_hi = sb("w_hi", 2 * 3 * D, F32R)
        w_lo = sb("w_lo", 2 * 3 * D, F32R)
        prm = sb("prm", G * 2 * PRM)
        wv_raw = sb("wv_raw", KT * N)
        wv_hi = sb("wv_hi", KT * N, F32R)
        wv_lo = sb("wv_lo", KT * N, F32R)
        wo = sb("wo", G * D)
        obet = sb("obet", 2 * B * DW)
        raw = sb("raw", 2 * T)
        tap0 = sb("tap0", 2 * T)
        conv = sb("conv", 2 * T)
        tok = sb("tok", 2 * T)
        qk = sb("qk", 2 * T)
        gate = sb("gate", 2 * T)
        decay = sb("decay", B * DW)
        probs = sb("probs", B * DW)
        gated = sb("gated", G * T)
        values = sb("values", TT * N)
        stats = sb("stats", 16 * 6)
        rstd = sb("rstd", 16)
        nmr = sb("nmr", 16)
        s_sum, s_dif, s_var, s_y, s_t = (sb(f"nw{i}", 16) for i in range(5))
        small = sb("small", 64)
        ctxT = raw[:, 0:T]
        xw = raw[:, T:T + 2 * P]
        qctx, kctx = conv[:, 0:T], conv[:, T:2 * T]
        att = tok
        x_norm = values[:, 0:TT * D]
        wb = gate[:, 0:KT * H]
        bb = gate[0:H, 64:65]
        xb = gate[:, 66:68]
        betaT = gated[0:H, 0:T]
        obetT = gated[0:H, T:T + B * DW]
        rw = obet[:, 0:KT * H]
        rb = obet[:, 64:64 + H]
        score = obet[:, 128:256]
        choice = obet[:, 256:384]
        masked = obet[:, 384:512]
        rank = obet[:, 512:640]
        weight = obet[:, 640:768]
        gpair = obet[:, 768:768 + 6 * 32]
        gmask = obet[:, 960:992]
        denom = obet[:, 992:1008]
        cmp_a, cmp_b = raw, conv
        routeT = gated[0:E_ROUTED, 0:T]
        wbc = gated[:, 2 * T:4 * T]
        silu_g = tok
        prod = qk
        act_w = gate
        act_hi = sb("act_hi", T, F32R)
        act_lo = sb("act_lo", T, F32R)

        bank = [ctx.enter_context(nc.psum_tensor(f"bank{i}", [P, N], F32)) for i in range(8)]
        a_ring, t_ring, c_ring = bank[0:2], bank[2:6], bank[6:8]
        e_ring, y_acc = bank[0:4], bank[4:8]

        ld = {n: sem("ld_" + n) for n in
              ("const", "x", "ctx", "beta", "router", "wv", "wo", "obet_rows", "route_rows", "out")}
        ld_w = [sem(f"ld_w{i}") for i in range(2)]
        ld_prm = [sem(f"ld_prm{i}") for i in range(G)]
        ld_obet = [sem(f"ld_obet{i}") for i in range(2)]
        ld_we = [sem(f"ld_we{i}") for i in range(2)]
        ld_route = [sem(f"ld_route{i}") for i in range(2)]
        a_full, a_drained = sem("a_full"), sem("a_drained")
        t_full, t_drained = sem("t_full"), sem("t_drained")
        c_full, c_drained = sem("c_full"), sem("c_drained")
        w_hi_ready, w_lo_ready = sem("w_hi_ready"), sem("w_lo_ready")
        wv_hi_ready, wv_lo_ready = sem("wv_hi_ready"), sem("wv_lo_ready")
        taps_done, conv_done, silu_done = sem("taps_done"), sem("conv_done"), sem("silu_done")
        rstd_ready = sem("rstd_ready")
        decay_ready = sem("decay_ready")
        dve_step = sem("dve_step")
        ln_rstd, ln_norm = sem("ln_rstd"), sem("ln_norm")
        ln_full, ln_copied, ln_split = sem("ln_full"), sem("ln_copied"), sem("ln_split")
        x_qk_full, x_qk_ready = sem("x_qk_full"), sem("x_qk_ready")
        x_energy, x_max, x_exp = sem("x_energy"), sem("x_max"), sem("x_exp")
        x_soft, x_attT_full, x_attT_ready = sem("x_soft"), sem("x_attT_full"), sem("x_attT_ready")
        x_mix_full, x_mixed = sem("x_mix_full"), sem("x_mixed")
        b_full, b_ready, b_tok_full, b_tok_ready = (
            sem("b_full"), sem("b_ready"), sem("b_tok_full"), sem("b_tok_ready"))
        obet_ready, dmask_ready = sem("obet_ready"), sem("dmask_ready")
        r_full, r_score, r_ready, r_tr_full, r_tr_ready = (
            sem("r_full"), sem("r_score"), sem("r_ready"), sem("r_tr_full"), sem("r_tr_ready"))
        r_cmp = sem("r_cmp")
        ones_ready = sem("ones_ready")
        e_full, g_silu, u_prod = sem("e_full"), sem("g_silu"), sem("u_prod")
        e_weighted, e_hi, e_lo = sem("e_weighted"), sem("e_hi"), sem("e_lo")
        e_down = sem("e_down")
        y_full, y_added = sem("y_full"), sem("y_added")

        block = ctx.enter_context(nc.Block())

        @block.sync
        def _(sp):
            sp.dma_start(ctxT, ctx_in).then_inc(ld["ctx"], 16)
            sp.dma_start(xw, xw_in).then_inc(ld["ctx"], 16)
            sp.dma_start(xb, xb_in).then_inc(ld["ctx"], 16)
            sp.dma_start(x[:, :], x_in).then_inc(ld["x"], 16)
            sp.dma_start(ident[:, :], ident_in).then_inc(ld["const"], 16)
            sp.dma_start(wb, wb_in).then_inc(ld["beta"], 16)
            sp.dma_start(bb, bb_in).then_inc(ld["beta"], 16)
            sp.dma_start(wv_raw[:, :], wv_in[0, :, :]).then_inc(ld["wv"], 16)
            sp.dma_start(wo[:, :], wo_in[0, :, :]).then_inc(ld["wo"], 16)
            sp.dma_start(tie[:, :], tie_in).then_inc(ld["const"], 16)

            def load_weights(g, k):
                s = k % 2
                if not (isinstance(g, int) and G * g + k < 2):
                    sp.wait_ge(w_hi_ready, units(g, k, 1, -1))
                    sp.wait_ge(w_lo_ready, units(g, k, 1, -1))
                n = G * g + k
                sp.dma_start(w_raw[:, s * 3 * D:(s + 1) * 3 * D],
                             wh_in[bass.ds(n, 1), :, :].rearrange("a p c -> (a p) c")).then_inc(ld_w[s], 16)

            def load_params(g, k):
                s = k % G
                if not (isinstance(g, int) and G * g + k < G):
                    sp.wait_ge(t_drained, units(g, k - G + 1, 16 // 2))
                n = G * g + k
                sp.dma_start(prm[:, s * 2 * PRM:(s + 1) * 2 * PRM],
                             prm_in[bass.ds(n, 1), :, :].rearrange("a p c -> (a p) c")).then_inc(ld_prm[s], 16)

            def load_obet(g, k):
                s = k % 2
                if not (isinstance(g, int) and G * g + k < 2):
                    sp.wait_ge(decay_ready, units(g, k, 1, -1))
                n = G * g + k
                sp.dma_start(obet[:, s * B * DW:(s + 1) * B * DW],
                             obet_rows[bass.ds(n, 1), :].broadcast_to([P, B * DW])).then_inc(ld_obet[s], 16)

            for n in range(2):
                load_weights(0, n)
            for n in range(G):
                load_params(0, n)
            sp.wait_ge(obet_ready, 2)
            sp.dma_start(obet_rows, obetT).then_inc(ld["obet_rows"], 16)
            sp.wait_ge(ld["obet_rows"], 16)
            for n in range(2):
                load_obet(0, n)

            def step(g, k):
                n = G * g + k if isinstance(g, int) else None
                if n is None or n + 2 < H:
                    load_weights(g, k + 2)
                if n is None or n + 4 < H:
                    load_params(g, k + 4)
                if n is None or n + 2 < H:
                    load_obet(g, k + 2)
                if k == 1 and (n is None or g < NG - 1):
                    sp.wait_ge(wv_hi_ready, g + 1)
                    sp.wait_ge(wv_lo_ready, g + 1)
                    sp.dma_start(wv_raw[:, :], wv_in[bass.ds(g + 1, 1), :, :].rearrange("a p c -> (a p) c")
                                 ).then_inc(ld["wv"], 16)
                if k == 0 and n is None:
                    pass

            with sp.Fori(0, NG - 1) as g:
                for k in range(G):
                    step(g, k)
                sp.wait_ge(c_full, c_project(g) + TT // 2)
                sp.dma_start(wo[:, :], wo_in[bass.ds(g + 1, 1), :, :].rearrange("a p c -> (a p) c")
                             ).then_inc(ld["wo"], 16)
            for k in range(G):
                step(NG - 1, k)

            def load_expert(e):
                sp.dma_start(w_raw[:, (e_slot := e[1]) * 3 * D:(e_slot + 1) * 3 * D],
                             we_in[bass.ds(e[0], 1), :, :].rearrange("a p c -> (a p) c")
                             ).then_inc(ld_we[e_slot], 16)

            for s in range(2):
                sp.wait_ge(w_hi_ready, H)
                sp.wait_ge(w_lo_ready, H)
                load_expert((s, s))
            sp.wait_ge(decay_ready, H)
            sp.dma_start(rw, rw_in).then_inc(ld["router"], 16)
            sp.dma_start(rb, rb_in.broadcast_to([P, E_ROUTED])).then_inc(ld["router"], 16)
            for s in range(2):
                sp.wait_ge(w_hi_ready, H + 1 + s)
                sp.wait_ge(w_lo_ready, H + 1 + s)
                load_expert((2 + s, s))
            sp.wait_ge(r_tr_ready, NCH)
            sp.dma_start(route_rows, routeT).then_inc(ld["route_rows"], 16)
            sp.wait_ge(ld["route_rows"], 16)

            def load_route(e, s, before):
                sp.wait_ge(e_weighted, before)
                sp.dma_start(wbc[:, s * T:(s + 1) * T],
                             route_rows[bass.ds(e, 1), :].broadcast_to([P, T])).then_inc(ld_route[s], 16)

            for s in range(2):
                load_route(s, s, NCH * (s + 1))
            with sp.Fori(0, E_ROUTED // 2 - 1) as r:
                for s in range(2):
                    sp.wait_ge(w_hi_ready, r * 2 + (H + 3 + s))
                    sp.wait_ge(w_lo_ready, r * 2 + (H + 3 + s))
                    load_expert((r * 2 + (4 + s), s))
                    load_route(r * 2 + (2 + s), s, r * (2 * NCH) + NCH * (3 + s))
            for u in range(TT // 2):
                sp.wait_ge(y_added, u + 1)
                sp.dma_start(out[:, u * N:(u + 1) * N], x[:, u * N:(u + 1) * N]).then_inc(ld["out"], 16)
            sp.wait_ge(ld["out"], 16 * (TT // 2))

        @block.gpsimd
        def _(pool):
            def split_low(g, k):
                s = k % 2
                pool.wait_ge(w_hi_ready, units(g, k, 1, 1))
                if not (isinstance(g, int) and G * g + k < 2):
                    pool.wait_ge(a_full, units(g, k - 1, 6))
                w = slice(s * 3 * D, (s + 1) * 3 * D)
                nc.gpsimd.tensor_tensor(w_lo[:, w], w_raw[:, w], w_hi[:, w].bitcast(F32),
                                        ALU.subtract).then_inc(w_lo_ready, 1)

            def split_values(g):
                pool.wait_ge(wv_hi_ready, g + 1)
                nc.gpsimd.tensor_tensor(wv_lo[:, :], wv_raw[:, :], wv_hi[:, :].bitcast(F32),
                                        ALU.subtract).then_inc(wv_lo_ready, 1)

            def last_tap(g, k):
                for u in range(2 * NCH):
                    pool.wait_ge(taps_done, units(g, k, 4, u + 1))
                    y = conv[:, u * N:(u + 1) * N].rearrange("p (b t) -> p b t", b=BPC)[:, :, TAPS - 1:L]
                    r = tap0[:, u * N:(u + 1) * N].rearrange("p (b t) -> p b t", b=BPC)[:, :, 0:L - TAPS + 1]
                    nc.gpsimd.tensor_tensor(y, r, y, ALU.add).then_inc(conv_done, 1)

            split_values(0)
            split_low(0, 0)
            split_low(0, 1)
            last_tap(0, 0)
            last_tap(0, 1)

            def step(g, k):
                n = G * g + k if isinstance(g, int) else None
                if n is None or n + 2 < H:
                    split_low(*head(g, k + 2))
                if n is None or n + 2 < H:
                    last_tap(*head(g, k + 2))
                if k == 1 and (n is None or g < NG - 1):
                    pool.wait_ge(c_full, c_values(g - 1) + TT if not isinstance(g, int) or g else TT)
                    split_values(g + 1)

            with pool.Fori(0, NG - 1) as g:
                for k in range(G):
                    step(g, k)
            for k in range(G):
                step(NG - 1, k)

            def expert_low(n, s):
                w = slice(s * 3 * D, (s + 1) * 3 * D)
                pool.wait_ge(w_hi_ready, n + H)
                nc.gpsimd.tensor_tensor(w_lo[:, w], w_raw[:, w], w_hi[:, w].bitcast(F32),
                                        ALU.subtract).then_inc(w_lo_ready, 1)

            def weigh(n, s, first):
                for c in range(NCH):
                    pool.wait_ge(u_prod, (n - 1) * NCH + c + 1)
                    if not first:
                        pool.wait_ge(e_hi, (n - 2) * NCH + c + 1)
                        pool.wait_ge(e_lo, (n - 2) * NCH + c + 1)
                    cc = slice(c * N, (c + 1) * N)
                    nc.gpsimd.tensor_tensor(act_w[:, cc], prod[:, cc], wbc[:, s * T + c * N:s * T + (c + 1) * N],
                                            ALU.mult).then_inc(e_weighted, 1)

            pool.wait_ge(c_drained, c_values(NG - 1) + TT // 2)
            nc.gpsimd.memset(wbc, 1.0).then_inc(ones_ready, 1)
            pool.wait_ge(ones_ready, 1)
            expert_low(1, 0)
            expert_low(2, 1)
            weigh(1, 0, True)
            weigh(2, 1, False)
            with pool.Fori(0, E_ROUTED // 2) as r:
                for s in range(2):
                    pool.wait_ge(e_down, r * 2 + (1 + s))
                    expert_low(r * 2 + (3 + s), s)
                    pool.wait_ge(ld_route[s], r * 16 + 16)
                    weigh(r * 2 + (3 + s), s, False)

        @block.scalar
        def _(act):
            def stream_norm(i, split):
                act.wait_ge(ln_rstd, i + 1)
                for t in range(TT):
                    nc.scalar.activation(x_norm[:, t * D:(t + 1) * D], x[:, t * D:(t + 1) * D],
                                         ACT.Identity, scale=rstd[:, t:t + 1],
                                         bias=nmr[:, t:t + 1]).then_inc(ln_norm, 1)
                for u in range(KT * NCH):
                    act.wait_ge(ln_full, i * KT * NCH + u + 1)
                    nc.scalar.activation(xT[:, u * N:(u + 1) * N], bank[u][:, :],
                                         ACT.Copy).then_inc(ln_copied, 1)

            act.wait_ge(ld["ctx"], 48)
            for u in range(2 * NCH):
                act.wait_ge(x_qk_full, u + 1)
                nc.scalar.activation(conv[:, u * N:(u + 1) * N], bank[4 + u][:, :], ACT.Identity,
                                     bias=xb[:, u // NCH:u // NCH + 1]).then_inc(x_qk_ready, 1)
            for t in range(TT):
                act.wait_ge(x_max, 2 * (t // 2) + 2)
                nc.scalar.activation(att[:, t * L:(t + 1) * L],
                                     bank[4 + t // 2][:, (t % 2) * L:(t % 2 + 1) * L], ACT.Exp,
                                     bias=small[:, t:t + 1],
                                     accum_out=small[:, 8 + t:9 + t]).then_inc(x_exp, 1)
            stream_norm(0, True)
            act.wait_ge(ld["beta"], 32)
            for c in range(NCH):
                act.wait_ge(b_full, c + 1)
                nc.scalar.activation(betaT[:, c * N:(c + 1) * N], bank[c][0:H, :], ACT.Sigmoid,
                                     bias=bb).then_inc(b_ready, 1)

            def high(g, k):
                s = k % 2
                w = slice(s * 3 * D, (s + 1) * 3 * D)
                act.wait_ge(ld_w[s], uses(g, k, 2) * 16)
                if not (isinstance(g, int) and G * g + k < 2):
                    act.wait_ge(a_full, units(g, k - 1, 6))
                nc.scalar.activation(w_hi[:, w], w_raw[:, w], ACT.Copy).then_inc(w_hi_ready, 1)

            def high_values(g):
                act.wait_ge(ld["wv"], g * 16 + 16)
                nc.scalar.activation(wv_hi[:, :], wv_raw[:, :], ACT.Copy).then_inc(wv_hi_ready, 1)

            def raw_qk(g, k):
                act.wait_ge(ld_prm[k % G], uses(g, k, G) * 16)
                for u in range(2 * NCH):
                    act.wait_ge(a_full, units(g, k, 6, u + 1))
                    if not (isinstance(g, int) and G * g + k < 1):
                        act.wait_ge(conv_done, units(g, k - 1, 4, u + 1))
                    o = (k % G) * 2 * PRM + (u // NCH) * PRM
                    nc.scalar.activation(raw[:, u * N:(u + 1) * N], a_ring[u % 2][:, :], ACT.Copy)
                    nc.scalar.activation(tap0[:, u * N:(u + 1) * N], a_ring[u % 2][:, :], ACT.Copy,
                                         scale=prm[:, o:o + 1]).then_inc(a_drained, 1)

            def gates(g, k):
                for c in range(NCH):
                    act.wait_ge(a_full, units(g, k, 6, 4 + c + 1))
                    if not (isinstance(g, int) and G * g + k < 2):
                        gg, kk = head(g, k - 2) if isinstance(g, int) else (g, k - 2)
                        act.wait_ge(c_drained, c_outputs(gg, kk) + NCH)
                    nc.scalar.activation(gate[:, (k % 2) * T + c * N:(k % 2) * T + (c + 1) * N],
                                         a_ring[c % 2][:, :], ACT.Silu).then_inc(a_drained, 1)

            def silu(g, k):
                for u in range(2 * NCH):
                    act.wait_ge(conv_done, units(g, k, 4, u + 1))
                    c = conv[:, u * N:(u + 1) * N]
                    nc.scalar.activation(c, c, ACT.Silu).then_inc(silu_done, 1)

            def normalise(g, k):
                act.wait_ge(rstd_ready, units(g, k, 1, 1))
                for u in range(2 * NCH):
                    act.wait_ge(t_full, units(g, k, 8, u + 1))
                    if not (isinstance(g, int) and G * g + k < 1):
                        act.wait_ge(t_full, units(g, k - 1, 8, 4 + u + 1))
                    for i in range(G):
                        t = u * G + i
                        ins = nc.scalar.activation(tok[:, t * P:(t + 1) * P], t_ring[u][:, i * P:(i + 1) * P],
                                                   ACT.Identity, scale=rstd[:, t:t + 1], bias=nmr[:, t:t + 1])
                    ins.then_inc(t_drained, 1)

            def affine(g, k):
                for u in range(2 * NCH):
                    o = (k % G) * 2 * PRM + (u // NCH) * PRM + TAPS + 1
                    act.wait_ge(t_full, units(g, k, 8, 4 + u + 1))
                    if not (isinstance(g, int) and G * g + k < 1):
                        gg, kk = head(g, k - 1) if isinstance(g, int) else (g, k - 1)
                        act.wait_ge(c_full, c_scores(gg, kk) + B)
                    nc.scalar.activation(qk[:, u * N:(u + 1) * N], t_ring[u][:, :], ACT.Identity,
                                         scale=prm[:, o:o + 1], bias=prm[:, o + 1:o + 2]).then_inc(t_drained, 1)

            high_values(0)
            high(0, 0)
            high(0, 1)
            raw_qk(0, 0)
            gates(0, 0)
            silu(0, 0)
            raw_qk(0, 1)
            normalise(0, 0)
            affine(0, 0)
            gates(0, 1)
            silu(0, 1)

            def step(g, k):
                n = G * g + k if isinstance(g, int) else None
                if n is None or n + 2 < H:
                    high(*head(g, k + 2))
                    raw_qk(*head(g, k + 2))
                if n is None or n + 1 < H:
                    normalise(*head(g, k + 1))
                    affine(*head(g, k + 1))
                if n is None or n + 2 < H:
                    gates(*head(g, k + 2))
                    silu(*head(g, k + 2))
                if k == 1 and (n is None or g < NG - 1):
                    act.wait_ge(c_full, c_values(g - 1) + TT if not isinstance(g, int) or g else TT)
                    high_values(g + 1)

            with act.Fori(0, NG - 1) as g:
                for k in range(G):
                    step(g, k)
            for k in range(G):
                step(NG - 1, k)

            def expert_high(n, s, wait_down):
                w = slice(s * 3 * D, (s + 1) * 3 * D)
                act.wait_ge(ld_we[s], wait_down * 16 + 16 if not isinstance(wait_down, int) else 16 * (wait_down + 1))
                nc.scalar.activation(w_hi[:, w], w_raw[:, w], ACT.Copy).then_inc(w_hi_ready, 1)

            def gate_silu(n, first):
                for c in range(NCH):
                    act.wait_ge(e_full, (n - 1) * 4 + 2 * c + 1)
                    if not first:
                        act.wait_ge(u_prod, (n - 2) * NCH + c + 1)
                    cc = slice(c * N, (c + 1) * N)
                    nc.scalar.activation(silu_g[:, cc], e_ring[2 * c][:, :], ACT.Silu).then_inc(g_silu, 1)

            def act_high(n, first):
                for c in range(NCH):
                    act.wait_ge(e_weighted, (n - 1) * NCH + c + 1)
                    if not first:
                        act.wait_ge(e_down, n - 1)
                    cc = slice(c * N, (c + 1) * N)
                    nc.scalar.activation(act_hi[:, cc], act_w[:, cc], ACT.Copy).then_inc(e_hi, 1)

            act.wait_ge(a_full, 6 * H)
            expert_high(1, 0, 0)
            expert_high(2, 1, 0)
            stream_norm(1, False)
            stream_norm(2, True)
            for c in range(1):
                act.wait_ge(r_full, 1)
                nc.scalar.activation(score, bank[4][:, 0:TT * E_ROUTED], ACT.Sigmoid).then_inc(r_score, 1)
            gate_silu(1, True)
            act_high(1, True)
            gate_silu(2, False)
            act_high(2, False)
            for c in range(NCH):
                act.wait_ge(r_tr_full, c + 1)
                nc.scalar.activation(routeT[:, c * N:(c + 1) * N], y_acc[2 + c][0:E_ROUTED, :] if False else bank[c][0:E_ROUTED, :],
                                     ACT.Copy).then_inc(r_tr_ready, 1)
            with act.Fori(0, E_ROUTED // 2) as r:
                for s in range(2):
                    act.wait_ge(e_down, r * 2 + (1 + s))
                    expert_high(r * 2 + (3 + s), s, r + 1)
                    gate_silu(r * 2 + (3 + s), False)
                    act_high(r * 2 + (3 + s), False)

        @block.vector
        def _(dve):
            steps = Steps(dve, dve_step, body=G * 23)

            def norm_factors(tiles, width):
                st = stats[:, 0:6 * tiles].rearrange("p (t s) -> p s t", s=6)
                me, m2e, mo, m2o = st[:, 1, :], st[:, 2, :], st[:, 4, :], st[:, 5, :]
                c = slice(0, tiles)
                dif = steps.did(nc.vector.tensor_tensor(s_dif[:, c], me, mo, ALU.subtract))
                nc.vector.tensor_tensor(s_sum[:, c], me, mo, ALU.add)
                nc.vector.tensor_tensor(s_var[:, c], m2e, m2o, ALU.add)
                steps.after(dif)
                a = steps.did(nc.vector.tensor_tensor(s_t[:, c], s_dif[:, c], s_dif[:, c], ALU.mult))
                steps.after(a)
                a = steps.did(nc.vector.scalar_tensor_tensor(
                    out=s_var[:, c], in0=s_t[:, c], scalar=width / 4.0, in1=s_var[:, c],
                    op0=ALU.mult, op1=ALU.add))
                steps.after(a)
                a = steps.did(nc.vector.tensor_scalar(s_var[:, c], s_var[:, c], 1.0 / width, EPS,
                                                      ALU.mult, ALU.add))
                steps.after(a)
                a = steps.did(nc.vector.tensor_scalar(
                    s_y[:, c].bitcast(I32), s_var[:, c].bitcast(I32), -0.5, RSQRT_SEED,
                    ALU.mult, ALU.add))
                for i in range(3):
                    steps.after(a)
                    a = steps.did(nc.vector.tensor_tensor(s_t[:, c], s_y[:, c], s_y[:, c], ALU.mult))
                    steps.after(a)
                    a = steps.did(nc.vector.scalar_tensor_tensor(
                        out=s_t[:, c], in0=s_t[:, c], scalar=-0.5, in1=s_var[:, c],
                        op0=ALU.mult, op1=ALU.mult))
                    steps.after(a)
                    y = rstd if i == 2 else s_y
                    a = steps.did(nc.vector.scalar_tensor_tensor(
                        out=y[:, c], in0=s_t[:, c], scalar=1.5, in1=s_y[:, c],
                        op0=ALU.add, op1=ALU.mult))
                steps.after(a)
                return nc.vector.scalar_tensor_tensor(
                    out=nmr[:, c], in0=s_sum[:, c], scalar=-0.5, in1=rstd[:, c],
                    op0=ALU.mult, op1=ALU.mult)

            def stream_stats():
                for t in range(TT):
                    ins = nc.vector.bn_stats(stats[:, 6 * t:6 * t + 6], x[:, t * D:(t + 1) * D])
                steps.after(steps.did(ins))
                norm_factors(TT, D).then_inc(ln_rstd, 1)

            def stream_split(i, n):
                for u in range(KT * NCH):
                    uu = slice(u * N, (u + 1) * N)
                    dve.wait_ge(ln_copied, i * KT * NCH + u + 1)
                    a = steps.did(nc.vector.tensor_copy(xT_hi[:, uu], xT[:, uu]))
                    steps.after(a)
                    nc.vector.tensor_tensor(xT_lo[:, uu], xT[:, uu], xT_hi[:, uu].bitcast(F32),
                                            ALU.subtract).then_inc(ln_split, 1)

            dve.wait_ge(ld["x"], 16)
            stream_stats()
            dve.wait_ge(ld["const"], 32)
            a = steps.did(nc.vector.memset(dmask[:, :], 0.0))
            steps.after(a)
            dm = dmask[:, :].rearrange("p (b c) -> p b c", b=B)
            for b in range(B):
                nc.vector.tensor_copy(dm[:, b, 0:P], ident[:, :])
                ins = nc.vector.tensor_copy(dm[:, b, L:L + P], ident[:, :])
            ins.then_inc(dmask_ready, 1)
            for t in range(TT):
                dve.wait_ge(x_energy, t // 2 + 1)
                nc.vector.tensor_reduce(small[:, t:t + 1], bank[4 + t // 2][:, (t % 2) * L:(t % 2 + 1) * L],
                                        op=ALU.max, axis=AX.X, negate=True).then_inc(x_max, 1)
            dve.wait_ge(x_exp, TT)
            a = steps.did(nc.vector.reciprocal(small[:, 16:16 + TT], small[:, 8:8 + TT]))
            steps.after(a)
            for t in range(TT):
                nc.vector.tensor_scalar(att[:, t * L:(t + 1) * L], att[:, t * L:(t + 1) * L],
                                        small[:, 16 + t:17 + t], None, ALU.mult).then_inc(x_soft, 1)
            for u in range(KT * NCH):
                dve.wait_ge(x_attT_full, u + 1)
                nc.vector.tensor_copy(attT[:, u * N:(u + 1) * N], bank[4 + u][:, :]).then_inc(x_attT_ready, 1)
            stream_split(0, 0)
            a = steps.did(nc.vector.memset(obetT, 0.0))
            dve.wait_ge(b_ready, NCH)
            steps.after(a)
            bt = betaT.rearrange("h (b t) -> h b t", b=B)
            ob = obetT.rearrange("h (b c) -> h b c", b=B)
            nc.vector.tensor_scalar(ob[:, :, 1:L], bt[:, :, 1:L], -1.0, 1.0, ALU.mult,
                                    ALU.add).then_inc(obet_ready, 1)
            nc.vector.tensor_scalar(ob[:, :, L + 1:DW], bt[:, :, P + 1:L], -1.0, 1.0, ALU.mult,
                                    ALU.add).then_inc(obet_ready, 1)
            dve.wait_ge(b_tok_full, 1)
            nc.vector.tensor_copy(beta_tok[:, :], bank[2][:, 0:TT * H]).then_inc(b_tok_ready, 1)
            dve.wait_ge(b_tok_ready, 1)
            bt_v = beta_tok[:, :].rearrange("p (t h) -> p t h", t=TT)

            def scale_values(g, first):
                for t in range(TT):
                    at = t if first else c_values(g) + t
                    dve.wait_ge(c_full, at + 1)
                    gg = 0 if first else g + 1
                    nc.vector.tensor_tensor(
                        values[:, t * N:(t + 1) * N].rearrange("p (h c) -> p h c", h=G),
                        c_ring[t % 2][:, :].rearrange("p (h c) -> p h c", h=G),
                        bt_v[:, t, bass.ds(gg * G, G)].unsqueeze(2).broadcast_to([P, G, P]),
                        ALU.mult).then_inc(c_drained, 1)

            def head_decay(g, k):
                s = k % 2
                dve.wait_ge(ld_obet[s], uses(g, k, 2) * 16)
                if not (isinstance(g, int) and G * g + k < 1):
                    gg, kk = head(g, k - 1) if isinstance(g, int) else (g, k - 1)
                    dve.wait_ge(c_drained, c_scores(gg, kk) + B)
                nc.vector.tensor_tensor_scan(decay[:, :], obet[:, s * B * DW:(s + 1) * B * DW],
                                             dmask[:, :], 0.0, ALU.mult, ALU.add).then_inc(decay_ready, 1)

            def head_stats(g, k):
                for u in range(2 * NCH):
                    dve.wait_ge(t_full, units(g, k, 8, u + 1))
                    for i in range(G):
                        t = u * G + i
                        ins = nc.vector.bn_stats(stats[:, 6 * t:6 * t + 6], t_ring[u][:, i * P:(i + 1) * P])
                if not (isinstance(g, int) and G * g + k < 1):
                    dve.wait_ge(t_drained, units(g, k - 1, 8, 4))
                steps.after(steps.did(ins))
                norm_factors(2 * TT, P).then_inc(rstd_ready, 1)

            def taps(g, k, part):
                o = (k % G) * 2 * PRM + part * PRM
                if part == 0:
                    dve.wait_ge(ld_prm[k % G], uses(g, k, G) * 16)
                made = []
                for u in (2 * part, 2 * part + 1):
                    dve.wait_ge(a_drained, units(g, k, 6, u + 1))
                    if not (isinstance(g, int) and G * g + k < 1):
                        dve.wait_ge(t_full, units(g, k - 1, 8, u + 1))
                    made.append(steps.did(nc.vector.tensor_scalar(
                        conv[:, u * N:(u + 1) * N], raw[:, u * N:(u + 1) * N],
                        prm[:, o + 3:o + 4], prm[:, o + 4:o + 5], ALU.mult, ALU.add)))
                for back in (1, 2):
                    for i, u in enumerate((2 * part, 2 * part + 1)):
                        y = conv[:, u * N:(u + 1) * N].rearrange("p (b t) -> p b t", b=BPC)[:, :, back:L]
                        r = raw[:, u * N:(u + 1) * N].rearrange("p (b t) -> p b t", b=BPC)[:, :, 0:L - back]
                        steps.after(made[i])
                        ins = nc.vector.scalar_tensor_tensor(
                            out=y, in0=r, scalar=prm[:, o + 3 - back:o + 4 - back], in1=y,
                            op0=ALU.mult, op1=ALU.add)
                        if back == 2:
                            ins.then_inc(taps_done, 1)
                        else:
                            made[i] = steps.did(ins)

            def decayed(g, k):
                dve.wait_ge(decay_ready, units(g, k, 1, 1))
                for b in range(B):
                    dve.wait_ge(c_full, c_scores(g, k) + (b + 1))
                    bb_ = slice(b * DW, (b + 1) * DW)
                    nc.vector.tensor_tensor(probs[:, bb_], c_ring[b % 2][:, 0:DW], decay[:, bb_],
                                            ALU.mult).then_inc(c_drained, 1)

            def gated_out(g, k):
                if not (isinstance(g, int) and g < 1):
                    dve.wait_ge(c_full, c_project(g - 1) + TT // 2)
                dve.wait_ge(a_drained, units(g, k, 6, 6))
                for c in range(NCH):
                    dve.wait_ge(c_full, c_outputs(g, k) + (c + 1))
                    nc.vector.tensor_tensor(gated[:, k * T + c * N:k * T + (c + 1) * N], c_ring[c % 2][:, :],
                                            gate[:, (k % 2) * T + c * N:(k % 2) * T + (c + 1) * N],
                                            ALU.mult).then_inc(c_drained, 1)

            def add_projection(g):
                for u in range(TT // 2):
                    dve.wait_ge(c_full, c_project(g) + (u + 1))
                    xs = x[:, u * N:(u + 1) * N]
                    nc.vector.tensor_tensor(xs, c_ring[u % 2][:, :], xs, ALU.add).then_inc(c_drained, 1)

            scale_values(0, True)
            taps(0, 0, 0)
            taps(0, 0, 1)
            head_decay(0, 0)
            head_stats(0, 0)
            taps(0, 1, 0)
            taps(0, 1, 1)

            def step(g, k):
                n = G * g + k if isinstance(g, int) else None
                if n is None or n + 1 < H:
                    head_stats(*head(g, k + 1))
                if n is None or n + 2 < H:
                    taps(*head(g, k + 2), 0)
                decayed(g, k)
                if n is None or n + 2 < H:
                    taps(*head(g, k + 2), 1)
                gated_out(g, k)
                if n is None or n + 1 < H:
                    head_decay(*head(g, k + 1))
                if k == G - 1:
                    if n is None or g < NG - 1:
                        scale_values(g, False)
                        add_projection(g)
                    else:
                        for u in range(TT // 2):
                            dve.wait_ge(c_full, c_values(g) + (u + 1))
                            xs = x[:, u * N:(u + 1) * N]
                            nc.vector.tensor_tensor(xs, c_ring[u % 2][:, :], xs, ALU.add).then_inc(c_drained, 1)

            dve.wait_ge(c_drained, TT)
            with dve.Fori(0, NG - 1) as g:
                steps.enter(g)
                for k in range(G):
                    step(g, k)
            steps.leave(NG - 1)
            for k in range(G):
                step(NG - 1, k)
            dve.wait_ge(c_drained, c_values(NG - 1) + TT // 2)
            stream_stats()
            for u in range(TT // 2):
                dve.wait_ge(x_mix_full, u + 1)
                xs = x[:, u * N:(u + 1) * N]
                nc.vector.tensor_tensor(xs, bank[4 + u][:, :], xs, ALU.add).then_inc(x_mixed, 1)
            dve.wait_ge(x_mixed, TT // 2)
            stream_stats()
            stream_split(2, 1)

            def u_times(n, first):
                for c in range(NCH):
                    dve.wait_ge(e_full, (n - 1) * 4 + 2 * c + 2)
                    dve.wait_ge(g_silu, (n - 1) * NCH + c + 1)
                    if not first:
                        dve.wait_ge(e_weighted, (n - 2) * NCH + c + 1)
                    cc = slice(c * N, (c + 1) * N)
                    nc.vector.tensor_tensor(prod[:, cc], e_ring[2 * c + 1][:, :], silu_g[:, cc],
                                            ALU.mult).then_inc(u_prod, 1)

            def act_low(n, first):
                for c in range(NCH):
                    dve.wait_ge(e_hi, (n - 1) * NCH + c + 1)
                    cc = slice(c * N, (c + 1) * N)
                    nc.vector.tensor_tensor(act_lo[:, cc], act_w[:, cc], act_hi[:, cc].bitcast(F32),
                                            ALU.subtract).then_inc(e_lo, 1)

            u_times(1, True)
            act_low(1, True)

            t8 = lambda ap, n: ap.rearrange("p (t e) -> p t e", t=TT)
            sc3 = choice.rearrange("p (t e) -> p t e", t=TT)
            dve.wait_ge(r_score, 1)
            dve.wait_ge(ld["router"], 32)

            def op(ins):
                steps.after(steps.did(ins))

            op(nc.vector.tensor_tensor(sc3, score.rearrange("p (t e) -> p t e", t=TT),
                                       rb.unsqueeze(1).broadcast_to([P, TT, E_ROUTED]), ALU.add))
            c4 = choice.rearrange("p (q e) -> p e q", e=EPG)
            hi1, lo1, hi2, lo2, top, sec = (gpair[:, i * 32:(i + 1) * 32] for i in range(6))
            op(nc.vector.tensor_tensor(hi1, c4[:, 0, :], c4[:, 1, :], ALU.max))
            op(nc.vector.tensor_tensor(lo1, c4[:, 0, :], c4[:, 1, :], ALU.min))
            op(nc.vector.tensor_tensor(hi2, c4[:, 2, :], c4[:, 3, :], ALU.max))
            op(nc.vector.tensor_tensor(lo2, c4[:, 2, :], c4[:, 3, :], ALU.min))
            op(nc.vector.tensor_tensor(top, hi1, hi2, ALU.max))
            op(nc.vector.tensor_tensor(sec, hi1, hi2, ALU.min))
            op(nc.vector.tensor_tensor(lo1, lo1, lo2, ALU.max))
            op(nc.vector.tensor_tensor(sec, sec, lo1, ALU.max))
            op(nc.vector.tensor_tensor(top, top, sec, ALU.add))

            def ranks(dst, src, n, tri):
                v = src.rearrange("p (t e) -> p t e", t=TT)
                other = v.unsqueeze(2).broadcast_to([P, TT, n, n])
                own = v.unsqueeze(3).broadcast_to([P, TT, n, n])
                a = cmp_a[:, 0:TT * n * n].rearrange("p (t e f) -> p t e f", t=TT, e=n)
                b = cmp_b[:, 0:TT * n * n].rearrange("p (t e f) -> p t e f", t=TT, e=n)
                mask = tri.rearrange("p (e f) -> p e f", e=n).unsqueeze(1).broadcast_to([P, TT, n, n])
                op(nc.vector.tensor_tensor(b, other, own, ALU.is_equal))
                op(nc.vector.tensor_tensor(b, b, mask, ALU.mult))
                op(nc.vector.tensor_tensor(a, other, own, ALU.is_gt))
                op(nc.vector.tensor_tensor(a, a, b, ALU.add))
                op(nc.vector.tensor_reduce(dst.rearrange("p (t e) -> p t e", t=TT), a, op=ALU.add, axis=AX.X))

            ranks(gmask, top, EG, tie[:, E_ROUTED * E_ROUTED:])
            op(nc.vector.tensor_scalar(gmask, gmask, TOPK_GROUP - 0.5, None, ALU.is_lt))
            gm4 = gmask.unsqueeze(2).broadcast_to([P, TT * EG, EPG])
            m4 = masked.rearrange("p (q e) -> p q e", e=EPG)
            op(nc.vector.tensor_tensor(m4, choice.rearrange("p (q e) -> p q e", e=EPG), gm4, ALU.mult))
            op(nc.vector.tensor_scalar(gmask, gmask, -VERY_NEGATIVE, VERY_NEGATIVE, ALU.mult, ALU.add))
            op(nc.vector.tensor_tensor(m4, m4, gm4, ALU.add))
            ranks(rank, masked, E_ROUTED, tie[:, 0:E_ROUTED * E_ROUTED])
            op(nc.vector.tensor_scalar(rank, rank, TOP_K - 0.5, None, ALU.is_lt))
            op(nc.vector.tensor_tensor(weight, rank, score, ALU.mult))
            w3 = weight.rearrange("p (t e) -> p t e", t=TT)
            dn = denom[:, 0:TT]
            op(nc.vector.tensor_reduce(dn, w3, op=ALU.add, axis=AX.X))
            op(nc.vector.tensor_scalar(dn, dn, 1e-20, None, ALU.add))
            op(nc.vector.reciprocal(dn, dn))
            op(nc.vector.tensor_tensor(w3, w3, dn.unsqueeze(2).broadcast_to([P, TT, E_ROUTED]), ALU.mult))
            nc.vector.tensor_scalar(weight, weight, ROUTED_SCALE, None, ALU.mult).then_inc(r_ready, 1)

            u_times(2, False)
            act_low(2, False)
            with dve.Fori(0, E_ROUTED // 2) as r:
                for s in range(2):
                    u_times(r * 2 + (3 + s), False)
                    dve.wait_ge(e_down, r * 2 + (2 + s))
                    act_low(r * 2 + (3 + s), False)
            for u in range(TT // 2):
                dve.wait_ge(y_full, u + 1)
                xs = x[:, u * N:(u + 1) * N]
                nc.vector.tensor_tensor(xs, y_acc[u][:, :], xs, ALU.add).then_inc(y_added, 1)

        @block.tensor
        def _(pe):
            def mm(o, l, r, start, stop):
                return nc.tensor.matmul(o, l, r, start=start, stop=stop)

            def mm3(o, l_hi, l_lo, r_hi, r_lo, start, stop, loose=False):
                nc.tensor.matmul(o, l_hi, r_lo, start=start, stop=False, skip_group_check=loose)
                nc.tensor.matmul(o, l_lo, r_hi, start=False, stop=False, skip_group_check=loose)
                return nc.tensor.matmul(o, l_hi, r_hi, start=False, stop=stop, skip_group_check=loose)

            def stream_transpose(i):
                for u in range(KT * NCH):
                    kt, c = divmod(u, NCH)
                    for j in range(G):
                        t = c * G + j
                        pe.wait_ge(ln_norm, i * TT + t + 1)
                        ins = nc.tensor.transpose(bank[u][:, j * P:(j + 1) * P],
                                                  x_norm[:, t * D + kt * P:t * D + (kt + 1) * P], ident[:, :])
                    ins.then_inc(ln_full, 1)

            pe.wait_ge(ld["ctx"], 48)
            for u in range(2 * NCH):
                s, c = divmod(u, NCH)
                mm(bank[4 + u][:, :], xw[:, s * P:(s + 1) * P], ctxT[:, c * N:(c + 1) * N],
                   True, True).then_inc(x_qk_full, 1)
            pe.wait_ge(x_qk_ready, 2 * NCH)
            for t in range(TT):
                b = t // KT
                ins = mm(bank[4 + t // 2][:, (t % 2) * L:(t % 2 + 1) * L], qctx[:, t * P:(t + 1) * P],
                         kctx[:, b * L:(b + 1) * L], True, True)
                if t % 2:
                    ins.then_inc(x_energy, 1)
            pe.wait_ge(ld["const"], 32)
            pe.wait_ge(x_soft, TT)
            for u in range(KT * NCH):
                nt, c = divmod(u, NCH)
                for j in range(G):
                    t = c * G + j
                    ins = nc.tensor.transpose(bank[4 + u][:, j * P:(j + 1) * P],
                                              att[:, t * L + nt * P:t * L + (nt + 1) * P], ident[:, :])
                ins.then_inc(x_attT_full, 1)
            stream_transpose(0)
            pe.wait_ge(ld["beta"], 32)
            pe.wait_ge(ln_copied, KT * NCH)
            for c in range(NCH):
                for kt in range(KT):
                    ins = mm(bank[c][0:H, :], wb[:, kt * H:(kt + 1) * H],
                             xT[:, kt * T + c * N:kt * T + (c + 1) * N], kt == 0, kt == KT - 1)
                ins.then_inc(b_full, 1)
            pe.wait_ge(b_ready, NCH)
            for t in range(TT):
                ins = nc.tensor.transpose(bank[2][:, t * H:(t + 1) * H], betaT[:, t * P:(t + 1) * P],
                                          ident[0:H, 0:H])
            ins.then_inc(b_tok_full, 1)

            def xs_(t_, kt, a, b):
                return t_[:, kt * T + a:kt * T + b]

            def values_of(g, first):
                pe.wait_ge(wv_lo_ready, 1 if first else g + 2)
                for t in range(TT):
                    at = t if first else c_values(g) + t
                    if not first or t >= 2:
                        pe.wait_ge(c_drained, at - 1)
                    for kt in range(KT):
                        w = slice(kt * N, (kt + 1) * N)
                        ins = mm3(c_ring[t % 2][:, :], xs_(xT_hi, kt, t * P, (t + 1) * P),
                                  xs_(xT_lo, kt, t * P, (t + 1) * P), wv_hi[:, w], wv_lo[:, w],
                                  kt == 0, kt == KT - 1)
                    ins.then_inc(c_full, 1)

            def project_in(g, k, what):
                s = k % 2
                if what == 0:
                    pe.wait_ge(w_lo_ready, units(g, k, 1, 1))
                for c in range(NCH):
                    u = what * NCH + c
                    if not (isinstance(g, int) and G * g + k < 1 and u < 2):
                        pe.wait_ge(a_drained, units(g, k, 6, u - 1))
                    for kt in range(KT):
                        o = s * 3 * D + what * D + kt * P
                        ins = mm3(a_ring[c % 2][:, :], w_hi[:, o:o + P], w_lo[:, o:o + P],
                                  xs_(xT_hi, kt, c * N, (c + 1) * N), xs_(xT_lo, kt, c * N, (c + 1) * N),
                                  kt == 0, kt == KT - 1)
                    ins.then_inc(a_full, 1)

            def to_tokens(g, k):
                for u in range(2 * NCH):
                    pe.wait_ge(silu_done, units(g, k, 4, u + 1))
                    if not (isinstance(g, int) and G * g + k < 1):
                        pe.wait_ge(t_drained, units(g, k, 8, u - 3))
                    for i in range(G):
                        t = u * G + i
                        ins = nc.tensor.transpose(t_ring[u][:, i * P:(i + 1) * P], conv[:, t * P:(t + 1) * P],
                                                  ident[:, :])
                    ins.then_inc(t_full, 1)

            def to_features(g, k):
                for u in range(2 * NCH):
                    pe.wait_ge(t_drained, units(g, k, 8, u + 1))
                    for i in range(G):
                        t = u * G + i
                        ins = nc.tensor.transpose(t_ring[u][:, i * P:(i + 1) * P], tok[:, t * P:(t + 1) * P],
                                                  ident[:, :])
                    ins.then_inc(t_full, 1)

            def attend(g, k):
                pe.wait_ge(t_drained, units(g, k, 8, 8))
                for b in range(B):
                    pe.wait_ge(c_drained, c_scores(g, k) + (b - 1))
                    q0, k0 = b * L, T + b * L
                    mm(c_ring[b % 2][:, 0:L], qk[:, k0:k0 + P], qk[:, q0:q0 + L], True, True)
                    mm(c_ring[b % 2][:, L:DW], qk[:, k0 + P:k0 + L], qk[:, q0 + P:q0 + L],
                       True, True).then_inc(c_full, 1)
                for c in range(NCH):
                    for i in range(BPC):
                        b = c * BPC + i
                        pe.wait_ge(c_drained, c_scores(g, k) + (c * BPC + i + 1 if c else max(i + 1, BPC + 1 + 1)))
                        v0 = values[:, (2 * b) * N + k * P:(2 * b) * N + (k + 1) * P]
                        v1 = values[:, (2 * b + 1) * N + k * P:(2 * b + 1) * N + (k + 1) * P]
                        o = c_ring[c % 2]
                        mm(o[:, i * L:(i + 1) * L], v0, probs[:, b * DW:b * DW + L], True, False)
                        ins = mm(o[:, i * L + P:(i + 1) * L], v1, probs[:, b * DW + L:(b + 1) * DW], False, True)
                    ins.then_inc(c_full, 1)

            def project_out(g, at):
                pe.wait_ge(ld["wo"], g * 16 + 16)
                pe.wait_ge(c_drained, c_outputs(g, G - 1) + NCH)
                for u in range(TT // 2):
                    pe.wait_ge(c_drained, at + (u - 1))
                    for i in range(2):
                        t = 2 * u + i
                        for h in range(G):
                            ins = mm(c_ring[u % 2][:, i * D:(i + 1) * D],
                                     gated[:, h * T + t * P:h * T + (t + 1) * P],
                                     wo[:, h * D:(h + 1) * D], h == 0, h == G - 1)
                    ins.then_inc(c_full, 1)

            pe.wait_ge(ln_split, KT * NCH)
            values_of(0, True)
            for what in range(3):
                project_in(0, 0, what)
            pe.wait_ge(b_tok_ready, 1)
            to_tokens(0, 0)
            project_in(0, 1, 0)
            project_in(0, 1, 1)
            to_features(0, 0)
            project_in(0, 1, 2)

            def step(g, k):
                n = G * g + k if isinstance(g, int) else None
                if n is None or n + 1 < H:
                    to_tokens(*head(g, k + 1))
                if n is None or n + 2 < H:
                    project_in(*head(g, k + 2), 0)
                    project_in(*head(g, k + 2), 1)
                attend(g, k)
                if n is None or n + 1 < H:
                    to_features(*head(g, k + 1))
                if n is None or n + 2 < H:
                    project_in(*head(g, k + 2), 2)
                if k == G - 1:
                    if n is None or g < NG - 1:
                        values_of(g, False)
                        project_out(g, c_project(g))
                    else:
                        project_out(g, c_values(g))

            with pe.Fori(0, NG - 1) as g:
                for k in range(G):
                    step(g, k)
            for k in range(G):
                step(NG - 1, k)

            stream_transpose(1)
            pe.wait_ge(x_attT_ready, KT * NCH)
            pe.wait_ge(ln_copied, 2 * KT * NCH)
            for u in range(TT // 2):
                for i in range(2):
                    t = 2 * u + i
                    for nt in range(KT):
                        ins = mm(bank[4 + u][:, i * D:(i + 1) * D], xT[:, nt * T + t * P:nt * T + (t + 1) * P],
                                 attT[:, nt * T + (t // KT) * L:nt * T + (t // KT + 1) * L],
                                 nt == 0, nt == KT - 1)
                ins.then_inc(x_mix_full, 1)
            stream_transpose(2)
            pe.wait_ge(ld["router"], 32)
            pe.wait_ge(ln_copied, 3 * KT * NCH)
            for t in range(TT):
                for kt in range(KT):
                    ins = mm(bank[4][:, t * E_ROUTED:(t + 1) * E_ROUTED],
                             xT[:, kt * T + t * P:kt * T + (t + 1) * P], rw[:, kt * H:(kt + 1) * H],
                             kt == 0, kt == KT - 1)
            ins.then_inc(r_full, 1)

            def gate_up(n, s, first):
                pe.wait_ge(w_lo_ready, n + H)
                for c in range(NCH):
                    for j in range(2):
                        if not first:
                            pe.wait_ge(g_silu if j == 0 else u_prod, (n - 2) * NCH + c + 1)
                        for kt in range(KT):
                            o = s * 3 * D + j * D + kt * P
                            ins = mm3(e_ring[2 * c + j][:, :], w_hi[:, o:o + P], w_lo[:, o:o + P],
                                      xs_(xT_hi, kt, c * N, (c + 1) * N), xs_(xT_lo, kt, c * N, (c + 1) * N),
                                      kt == 0, kt == KT - 1)
                        ins.then_inc(e_full, 1)

            def down(n, s, first, last):
                o = s * 3 * D + 2 * D
                for t in range(TT):
                    if t % G == 0:
                        pe.wait_ge(e_lo, (n - 1) * NCH + t // G + 1)
                    tt = slice(t * P, (t + 1) * P)
                    ins = mm3(y_acc[t // 2][:, (t % 2) * D:(t % 2 + 1) * D], act_hi[:, tt], act_lo[:, tt],
                              w_hi[:, o:o + D], w_lo[:, o:o + D], first and t % 2 == 0, last, loose=True)
                    if last and t % 2:
                        ins.then_inc(y_full, 1)
                if not last:
                    ins.then_inc(e_down, 1)

            pe.wait_ge(ln_split, 2 * KT * NCH)
            gate_up(1, 0, True)
            pe.wait_ge(r_score, 1)
            gate_up(2, 1, False)
            down(1, 0, True, False)
            pe.wait_ge(r_ready, 1)
            pe.wait_ge(g_silu, 2 * NCH)
            pe.wait_ge(u_prod, 2 * NCH)
            for c in range(NCH):
                for j in range(G):
                    t = c * G + j
                    ins = nc.tensor.transpose(bank[c][0:E_ROUTED, j * P:(j + 1) * P],
                                              weight[:, t * E_ROUTED:(t + 1) * E_ROUTED], ident[:, :])
                ins.then_inc(r_tr_full, 1)
            down(2, 1, False, False)
            pe.wait_ge(r_tr_ready, NCH)
            with pe.Fori(0, E_ROUTED // 2 - 1) as r:
                for s in range(2):
                    gate_up(r * 2 + (3 + s), s, False)
                    down(r * 2 + (3 + s), s, False, False)
            gate_up(E_ALL - 1, 0, False)
            down(E_ALL - 1, 0, False, False)
            gate_up(E_ALL, 1, False)
            down(E_ALL, 1, False, True)


def kernel(**inputs):
    import numpy as np
    import concourse.bacc as bacc
    from concourse.bass_utils import run_bass_kernel_spmd

    a = {k: np.asarray(v) for k, v in inputs.items()}

    def tiles(w):
        return w.reshape(KT, P, -1).transpose(1, 0, 2)

    def tokens(v):
        return v.reshape(TT, P, D).transpose(1, 0, 2).reshape(P, TT * D)

    heads = [tiles(a[f"L0_attn_{n}"]).reshape(P, KT, H, P).transpose(2, 0, 1, 3) for n in ("Wq", "Wk", "Wg")]
    wh = np.stack(heads, axis=2).reshape(H, P, 3 * D)
    prm = []
    for n in "qk":
        cw = a[f"L0_attn_{n}conv_w"].reshape(H, P, TAPS)
        cb = a[f"L0_attn_{n}conv_b"].reshape(H, P, 1)
        nw, nb = (np.broadcast_to(a[f"L0_attn_{n}n_{s}"].reshape(1, P, 1), (H, P, 1)) for s in "wb")
        prm += [cw, cb, nw, nb]
    prm = np.concatenate(prm, axis=2)
    wv = tiles(a["L0_attn_Wv"]).reshape(P, KT, NG, N).transpose(2, 0, 1, 3).reshape(NG, P, KT * N)
    wo = a["L0_attn_Wo"].reshape(NG, G, P, D).transpose(0, 2, 1, 3).reshape(NG, P, G * D)

    def up(w):
        return w.reshape(-1, P, KT, P).transpose(0, 3, 2, 1).reshape(-1, P, D)

    gw = np.concatenate([up(a["L0_ffn_sh_gate_w"]), up(a["L0_ffn_gate_w"])])
    uw = np.concatenate([up(a["L0_ffn_sh_up_w"]), up(a["L0_ffn_up_w"])])
    dw = np.concatenate([a["L0_ffn_sh_down_w"].reshape(D, E_SHARED, P).transpose(1, 2, 0),
                         a["L0_ffn_down_w"].transpose(0, 2, 1)])
    we = np.concatenate([gw, uw, dw], axis=2)
    lower = [np.broadcast_to(np.tril(np.ones((n, n), np.float32), -1).reshape(1, n * n), (P, n * n))
             for n in (E_ROUTED, EG)]
    arrays = {
        "x": tokens(a["x"]),
        "ctx": a["ctx_1024"].reshape(T, P).T,
        "xw": np.concatenate([a["L0_xattn_Wq"].T, a["L0_xattn_Wk"].T], axis=1),
        "xb": np.stack([a["L0_xattn_bq"], a["L0_xattn_bk"]], axis=1),
        "wb": tiles(a["L0_attn_Wb"]).reshape(P, KT * H),
        "bb": a["L0_attn_bb"].reshape(H, 1),
        "wh": wh, "prm": prm, "wv": wv, "wo": wo,
        "rw": tiles(a["L0_ffn_gate_weight"].T).reshape(P, KT * E_ROUTED),
        "rb": a["L0_ffn_e_score_correction_bias"].reshape(1, E_ROUTED),
        "we": we,
        "ident": np.eye(P, dtype=np.float32),
        "tie": np.concatenate(lower, axis=1),
    }
    arrays = {f"in_{k}": np.ascontiguousarray(v) for k, v in arrays.items()}
    nc = bacc.Bacc("TRN2", target_bir_lowering=False, num_devices=1)
    args = [nc.dram_tensor(k, v.shape, mybir.dt.from_np(v.dtype), kind="ExternalInput").ap()
            for k, v in arrays.items()]
    out = nc.dram_tensor("out_x", [P, TT * D], F32, kind="ExternalOutput").ap()
    decoder_layer(nc, *args, out)
    r = run_bass_kernel_spmd(nc, [arrays], core_ids=[0])
    got = np.asarray(r.results[0]["out_x"])
    return got.reshape(P, TT, D).transpose(1, 0, 2).reshape(B, L, D)
```

```python
from contextlib import ExitStack

import concourse.bass as bass
from concourse import mybir

F32 = mybir.dt.float32
F32R = mybir.dt.float32r
I32 = mybir.dt.int32
ALU = mybir.AluOpType
ACT = mybir.ActivationFunctionType
AX = mybir.AxisListType

P = 128
B, L, D = 4, 256, 256
T = B * L
TT = T // P
KT = D // P
N = 512
NCH = T // N
BPC = N // L
H = 16
G = 4
NG = H // G
TAPS = 4
PRM = TAPS + 3
DW = L + P
E_ROUTED, E_SHARED = 16, 2
E_ALL = E_ROUTED + E_SHARED
EG = 4
EPG = E_ROUTED // EG
TOPK_GROUP, TOP_K = 2, 4
ROUTED_SCALE = 2.5
EPS = 1e-5
RSQRT_SEED = 1597463007.0
VERY_NEGATIVE = -3.0e38

C_HEAD = B + NCH
C_GROUP = G * C_HEAD + TT + TT // 2


def c_scores(g, k):
    return C_GROUP * g + (TT + C_GROUP * (k // G) + C_HEAD * (k % G))


def c_outputs(g, k):
    return c_scores(g, k) + B


def c_values(g):
    return TT + C_GROUP * g + C_HEAD * G


def c_project(g):
    return c_values(g) + TT


def head(g, k):
    return (g + k // G if k // G else g), k % G


def units(g, k, per, more=0):
    return g * (G * per) + (k * per + more)


def uses(g, k, ring):
    return g * (G // ring) + (k // ring + 1)


class Steps:

    def __init__(self, eng, sem, body=0):
        self.eng, self.sem, self.n, self.g, self.body = eng, sem, 0, 0, body

    def did(self, ins):
        ins.then_inc(self.sem, 1)
        self.n += 1
        return self.n

    def after(self, n):
        if self.n and n:
            self.eng.wait_ge(self.sem, self.g * self.body + n)

    def enter(self, g):
        self.g, self.start = g, self.n

    def leave(self, rounds):
        assert self.n - self.start == self.body, (self.n - self.start, self.body)
        self.g, self.n = 0, self.n + self.body * (rounds - 1)


def decoder_layer(nc, x_in, ctx_in, xw_in, xb_in, wb_in, bb_in, wh_in, prm_in, wv_in, wo_in,
                  rw_in, rb_in, we_in, ident_in, tie_in, out):
    obet_rows = nc.dram_tensor("obet_rows", [H, B * DW], F32).ap()
    route_rows = nc.dram_tensor("route_rows", [E_ROUTED, T], F32).ap()

    ctx = ExitStack()
    with ctx:
        def sb(name, cols, dt=F32, parts=P):
            return ctx.enter_context(nc.sbuf_tensor(name, [parts, cols], dt))

        def sem(name):
            return ctx.enter_context(nc.semaphore(name))

        ident = sb("ident", P)
        tie = sb("tie", E_ROUTED * E_ROUTED + EG * EG)
        x = sb("x", TT * D)
        xT_hi = sb("xT_hi", KT * T, F32R)
        xT_lo = sb("xT_lo", KT * T, F32R)
        attT = sb("attT", KT * T)
        dmask = sb("dmask", B * DW)
        beta_tok = sb("beta_tok", TT * H)
        w_raw = sb("w_raw", 2 * 3 * D)
        w_hi = sb("w_hi", 2 * 3 * D, F32R)
        w_lo = sb("w_lo", 2 * 3 * D, F32R)
        prm = sb("prm", G * 2 * PRM)
        wv_raw = sb("wv_raw", KT * N)
        wv_hi = sb("wv_hi", KT * N, F32R)
        wv_lo = sb("wv_lo", KT * N, F32R)
        wo = sb("wo", G * D)
        obet = sb("obet", 2 * B * DW)
        raw = sb("raw", 2 * T)
        tap0 = sb("tap0", 2 * T)
        conv = sb("conv", 2 * T)
        tok = sb("tok", 2 * T)
        qk = sb("qk", 2 * T)
        gate = sb("gate", G * T)
        decay = sb("decay", B * DW)
        probs = sb("probs", B * DW)
        gated = sb("gated", G * T)
        values = sb("values", TT * N)
        stats = sb("stats", 16 * 6)
        rstd = sb("rstd", 16)
        nmr = sb("nmr", 16)
        s_sum, s_dif, s_var, s_y, s_t = (sb(f"nw{i}", 16) for i in range(5))
        small = sb("small", 64)
        xT = qk
        ctxT = raw[:, 0:T]
        xw = raw[:, T:T + 2 * P]
        qctx, kctx = conv[:, 0:T], conv[:, T:2 * T]
        att = tok
        x_norm = values[:, 0:TT * D]
        wb = gate[:, 0:KT * H]
        bb = gate[0:H, 64:65]
        xb = gate[:, 66:68]
        betaT = gated[0:H, 0:T]
        obetT = gated[0:H, T:T + B * DW]
        rw = obet[:, 0:KT * H]
        rb = obet[:, 64:64 + H]
        score = obet[:, 128:256]
        choice = obet[:, 256:384]
        masked = obet[:, 384:512]
        rank = obet[:, 512:640]
        weight = obet[:, 640:768]
        gpair = obet[:, 768:768 + 6 * 32]
        gmask = obet[:, 960:992]
        denom = obet[:, 992:1008]
        cmp_a, cmp_b = raw, conv
        routeT = gated[0:E_ROUTED, 0:T]
        wbc = gated[:, 2 * T:4 * T]
        silu_g = tok
        prod = qk
        act_w = gate
        act_hi = sb("act_hi", T, F32R)
        act_lo = sb("act_lo", T, F32R)

        bank = [ctx.enter_context(nc.psum_tensor(f"bank{i}", [P, N], F32)) for i in range(8)]
        a_ring, t_ring, c_ring = bank[0:2], bank[2:6], bank[6:8]
        e_ring, y_acc = bank[0:4], bank[4:8]

        ld = {n: sem("ld_" + n) for n in
              ("const", "x", "ctx", "beta", "router", "wv", "wo", "obet_rows", "route_rows", "out")}
        ld_w = [sem(f"ld_w{i}") for i in range(2)]
        ld_prm = [sem(f"ld_prm{i}") for i in range(G)]
        ld_obet = [sem(f"ld_obet{i}") for i in range(2)]
        ld_we = [sem(f"ld_we{i}") for i in range(2)]
        ld_route = [sem(f"ld_route{i}") for i in range(2)]
        a_full, a_drained = sem("a_full"), sem("a_drained")
        t_full, t_drained = sem("t_full"), sem("t_drained")
        c_full, c_drained = sem("c_full"), sem("c_drained")
        w_hi_ready, w_lo_ready = sem("w_hi_ready"), sem("w_lo_ready")
        wv_hi_ready, wv_lo_ready = sem("wv_hi_ready"), sem("wv_lo_ready")
        down_hi_ready, down_lo_ready = sem("down_hi_ready"), sem("down_lo_ready")
        taps_done, conv_done, silu_done = sem("taps_done"), sem("conv_done"), sem("silu_done")
        rstd_ready = sem("rstd_ready")
        decay_ready = sem("decay_ready")
        dve_step = sem("dve_step")
        ln_rstd, ln_norm = sem("ln_rstd"), sem("ln_norm")
        ln_full, ln_copied, ln_split = sem("ln_full"), sem("ln_copied"), sem("ln_split")
        x_qk_full, x_qk_ready = sem("x_qk_full"), sem("x_qk_ready")
        x_energy, x_max, x_exp = sem("x_energy"), sem("x_max"), sem("x_exp")
        x_soft, x_attT_full, x_attT_ready = sem("x_soft"), sem("x_attT_full"), sem("x_attT_ready")
        x_mix_full, x_mixed = sem("x_mix_full"), sem("x_mixed")
        b_full, b_ready, b_tok_full, b_tok_ready = (
            sem("b_full"), sem("b_ready"), sem("b_tok_full"), sem("b_tok_ready"))
        obet_ready, dmask_ready = sem("obet_ready"), sem("dmask_ready")
        r_full, r_score, r_ready, r_tr_full, r_tr_ready = (
            sem("r_full"), sem("r_score"), sem("r_ready"), sem("r_tr_full"), sem("r_tr_ready"))
        r_cmp = sem("r_cmp")
        ones_ready = sem("ones_ready")
        e_full, g_silu, u_prod = sem("e_full"), sem("g_silu"), sem("u_prod")
        e_weighted, e_hi, e_lo = sem("e_weighted"), sem("e_hi"), sem("e_lo")
        e_down = sem("e_down")
        y_full, y_added = sem("y_full"), sem("y_added")

        block = ctx.enter_context(nc.Block())

        @block.sync
        def _(sp):
            sp.dma_start(ctxT, ctx_in).then_inc(ld["ctx"], 16)
            sp.dma_start(xw, xw_in).then_inc(ld["ctx"], 16)
            sp.dma_start(xb, xb_in).then_inc(ld["ctx"], 16)
            sp.dma_start(x[:, :], x_in).then_inc(ld["x"], 16)
            sp.dma_start(ident[:, :], ident_in).then_inc(ld["const"], 16)
            sp.dma_start(wb, wb_in).then_inc(ld["beta"], 16)
            sp.dma_start(bb, bb_in).then_inc(ld["beta"], 16)
            sp.dma_start(wv_raw[:, :], wv_in[0, :, :]).then_inc(ld["wv"], 16)
            sp.dma_start(wo[:, :], wo_in[0, :, :]).then_inc(ld["wo"], 16)
            sp.dma_start(tie[:, :], tie_in).then_inc(ld["const"], 16)

            def load_weights(g, k):
                s = k % 2
                if not (isinstance(g, int) and G * g + k < 2):
                    sp.wait_ge(w_hi_ready, units(g, k, 1, -1))
                    sp.wait_ge(w_lo_ready, units(g, k, 1, -1))
                n = G * g + k
                sp.dma_start(w_raw[:, s * 3 * D:(s + 1) * 3 * D],
                             wh_in[bass.ds(n, 1), :, :].rearrange("a p c -> (a p) c")).then_inc(ld_w[s], 16)

            def load_params(g, k):
                s = k % G
                if not (isinstance(g, int) and G * g + k < G):
                    sp.wait_ge(t_drained, units(g, k - G + 1, 16 // 2))
                n = G * g + k
                sp.dma_start(prm[:, s * 2 * PRM:(s + 1) * 2 * PRM],
                             prm_in[bass.ds(n, 1), :, :].rearrange("a p c -> (a p) c")).then_inc(ld_prm[s], 16)

            def load_obet(g, k):
                s = k % 2
                if not (isinstance(g, int) and G * g + k < 2):
                    sp.wait_ge(decay_ready, units(g, k, 1, -1))
                n = G * g + k
                sp.dma_start(obet[:, s * B * DW:(s + 1) * B * DW],
                             obet_rows[bass.ds(n, 1), :].broadcast_to([P, B * DW])).then_inc(ld_obet[s], 16)

            for n in range(2):
                load_weights(0, n)
            for n in range(3):
                load_params(0, n)
            load_weights(0, 2)
            sp.wait_ge(obet_ready, 2)
            sp.dma_start(obet_rows, obetT).then_inc(ld["obet_rows"], 16)
            sp.wait_ge(ld["obet_rows"], 16)
            for n in range(2):
                load_obet(0, n)

            def step(g, k):
                n = G * g + k if isinstance(g, int) else None
                if n is None or n + 3 < H:
                    load_weights(g, k + 3)
                if n is None or n + 3 < H:
                    load_params(g, k + 3)
                if n is None or n + 2 < H:
                    load_obet(g, k + 2)
                if k == 1 and (n is None or g < NG - 1):
                    sp.wait_ge(wv_hi_ready, g + 1)
                    sp.wait_ge(wv_lo_ready, g + 1)
                    sp.dma_start(wv_raw[:, :], wv_in[bass.ds(g + 1, 1), :, :].rearrange("a p c -> (a p) c")
                                 ).then_inc(ld["wv"], 16)

            step(0, 0)
            with sp.Fori(0, NG - 1) as g:
                for k in range(1, G):
                    step(g, k)
                step(g + 1, 0)
                sp.wait_ge(c_full, c_project(g) + TT // 2)
                sp.dma_start(wo[:, :], wo_in[bass.ds(g + 1, 1), :, :].rearrange("a p c -> (a p) c")
                             ).then_inc(ld["wo"], 16)
            for k in range(1, G):
                step(NG - 1, k)

            def load_expert(e, s):
                sp.dma_start(w_raw[:, s * 3 * D:(s + 1) * 3 * D],
                             we_in[bass.ds(e, 1), :, :].rearrange("a p c -> (a p) c")).then_inc(ld_we[s], 16)

            def expert_split(n):
                sp.wait_ge(down_lo_ready, n)

            for s in range(2):
                sp.wait_ge(w_hi_ready, H)
                sp.wait_ge(w_lo_ready, H)
                load_expert(s, s)
            sp.wait_ge(decay_ready, H)
            sp.dma_start(rw, rw_in).then_inc(ld["router"], 16)
            sp.dma_start(rb, rb_in.broadcast_to([P, E_ROUTED])).then_inc(ld["router"], 16)
            for s in range(2):
                expert_split(1 + s)
                load_expert(2 + s, s)
            sp.wait_ge(r_tr_ready, NCH)
            sp.dma_start(route_rows, routeT).then_inc(ld["route_rows"], 16)
            sp.wait_ge(ld["route_rows"], 16)

            def load_route(e, s, before):
                sp.wait_ge(e_weighted, before)
                sp.dma_start(wbc[:, s * T:(s + 1) * T],
                             route_rows[bass.ds(e, 1), :].broadcast_to([P, T])).then_inc(ld_route[s], 16)

            for s in range(2):
                load_route(s, s, NCH * (s + 1))
            with sp.Fori(0, E_ROUTED // 2 - 1) as r:
                for s in range(2):
                    expert_split(r * 2 + (3 + s))
                    load_expert(r * 2 + (4 + s), s)
                    load_route(r * 2 + (2 + s), s, r * (2 * NCH) + NCH * (3 + s))
            for u in range(TT // 2):
                sp.wait_ge(y_added, u + 1)
                sp.dma_start(out[:, u * N:(u + 1) * N], x[:, u * N:(u + 1) * N]).then_inc(ld["out"], 16)
            sp.wait_ge(ld["out"], 16 * (TT // 2))

        @block.gpsimd
        def _(pool):
            def split_low(g, k):
                s = k % 2
                pool.wait_ge(w_hi_ready, units(g, k, 1, 1))
                if not (isinstance(g, int) and G * g + k < 2):
                    pool.wait_ge(a_full, units(g, k - 1, 6))
                w = slice(s * 3 * D, (s + 1) * 3 * D)
                nc.gpsimd.tensor_tensor(w_lo[:, w], w_raw[:, w], w_hi[:, w].bitcast(F32),
                                        ALU.subtract).then_inc(w_lo_ready, 1)

            def split_values(g):
                pool.wait_ge(wv_hi_ready, g + 1)
                nc.gpsimd.tensor_tensor(wv_lo[:, :], wv_raw[:, :], wv_hi[:, :].bitcast(F32),
                                        ALU.subtract).then_inc(wv_lo_ready, 1)

            def last_tap(g, k):
                for u in range(2 * NCH):
                    pool.wait_ge(taps_done, units(g, k, 4, u + 1))
                    y = conv[:, u * N:(u + 1) * N].rearrange("p (b t) -> p b t", b=BPC)[:, :, TAPS - 1:L]
                    r = tap0[:, u * N:(u + 1) * N].rearrange("p (b t) -> p b t", b=BPC)[:, :, 0:L - TAPS + 1]
                    nc.gpsimd.tensor_tensor(y, r, y, ALU.add).then_inc(conv_done, 1)

            split_low(0, 0)
            split_values(0)
            split_low(0, 1)
            last_tap(0, 0)
            split_low(0, 2)
            last_tap(0, 1)

            def step(g, k):
                n = G * g + k if isinstance(g, int) else None
                if n is None or n + 3 < H:
                    split_low(*head(g, k + 3))
                if n is None or n + 2 < H:
                    last_tap(*head(g, k + 2))
                if k == 1 and (n is None or g < NG - 1):
                    pool.wait_ge(c_full, c_scores(g, 0))
                    split_values(g + 1)

            step(0, 0)
            with pool.Fori(0, NG - 1) as g:
                for k in range(1, G):
                    step(g, k)
                step(g + 1, 0)
            for k in range(1, G):
                step(NG - 1, k)

            def gate_up_low(n, s):
                w = slice(s * 3 * D, s * 3 * D + 2 * D)
                pool.wait_ge(w_hi_ready, n + H)
                nc.gpsimd.tensor_tensor(w_lo[:, w], w_raw[:, w], w_hi[:, w].bitcast(F32),
                                        ALU.subtract).then_inc(w_lo_ready, 1)

            def down_low(n, s):
                w = slice(s * 3 * D + 2 * D, (s + 1) * 3 * D)
                pool.wait_ge(down_hi_ready, n)
                nc.gpsimd.tensor_tensor(w_lo[:, w], w_raw[:, w], w_hi[:, w].bitcast(F32),
                                        ALU.subtract).then_inc(down_lo_ready, 1)

            def weigh(n, s, first):
                for c in range(NCH):
                    pool.wait_ge(u_prod, (n - 1) * NCH + c + 1)
                    if not first:
                        pool.wait_ge(e_hi, (n - 2) * NCH + c + 1)
                        pool.wait_ge(e_lo, (n - 2) * NCH + c + 1)
                    cc = slice(c * N, (c + 1) * N)
                    nc.gpsimd.tensor_tensor(act_w[:, cc], prod[:, cc], wbc[:, s * T + c * N:s * T + (c + 1) * N],
                                            ALU.mult).then_inc(e_weighted, 1)

            pool.wait_ge(c_drained, c_values(NG - 1) + TT // 2)
            nc.gpsimd.memset(wbc, 1.0).then_inc(ones_ready, 1)
            pool.wait_ge(ones_ready, 1)
            for n in (1, 2):
                gate_up_low(n, n - 1)
                down_low(n, n - 1)
            weigh(1, 0, True)
            gate_up_low(3, 0)
            weigh(2, 1, False)
            gate_up_low(4, 1)
            down_low(3, 0)

            def step(n, s, left=2):
                pool.wait_ge(ld_route[s], (n - 1 - s) * 8)
                weigh(n, s, False)
                if left > 1:
                    gate_up_low(n + 2, s)
                if left > 0:
                    down_low(n + 1, 1 - s)

            with pool.Fori(0, E_ROUTED // 2 - 1) as r:
                for s in range(2):
                    step(r * 2 + (3 + s), s)
            step(E_ALL - 1, 0, 1)
            step(E_ALL, 1, 0)

        @block.scalar
        def _(act):
            def stream_norm(i, split):
                act.wait_ge(ln_rstd, i + 1)
                for t in range(TT):
                    nc.scalar.activation(x_norm[:, t * D:(t + 1) * D], x[:, t * D:(t + 1) * D],
                                         ACT.Identity, scale=rstd[:, t:t + 1],
                                         bias=nmr[:, t:t + 1]).then_inc(ln_norm, 1)
                for u in range(KT * NCH):
                    act.wait_ge(ln_full, i * KT * NCH + u + 1)
                    nc.scalar.activation(xT[:, u * N:(u + 1) * N], bank[u][:, :],
                                         ACT.Copy).then_inc(ln_copied, 1)

            act.wait_ge(ld["ctx"], 48)
            for u in range(2 * NCH):
                act.wait_ge(x_qk_full, u + 1)
                nc.scalar.activation(conv[:, u * N:(u + 1) * N], bank[4 + u][:, :], ACT.Identity,
                                     bias=xb[:, u // NCH:u // NCH + 1]).then_inc(x_qk_ready, 1)
            for t in range(TT):
                act.wait_ge(x_max, 2 * (t // 2) + 2)
                nc.scalar.activation(att[:, t * L:(t + 1) * L],
                                     bank[4 + t // 2][:, (t % 2) * L:(t % 2 + 1) * L], ACT.Exp,
                                     bias=small[:, t:t + 1],
                                     accum_out=small[:, 8 + t:9 + t]).then_inc(x_exp, 1)
            stream_norm(0, True)
            act.wait_ge(ld["beta"], 32)
            for c in range(NCH):
                act.wait_ge(b_full, c + 1)
                nc.scalar.activation(betaT[:, c * N:(c + 1) * N], bank[c][0:H, :], ACT.Sigmoid,
                                     bias=bb).then_inc(b_ready, 1)

            def high(g, k):
                s = k % 2
                w = slice(s * 3 * D, (s + 1) * 3 * D)
                act.wait_ge(ld_w[s], uses(g, k, 2) * 16)
                if not (isinstance(g, int) and G * g + k < 2):
                    act.wait_ge(a_full, units(g, k - 1, 6))
                nc.scalar.activation(w_hi[:, w], w_raw[:, w], ACT.Copy).then_inc(w_hi_ready, 1)

            def high_values(g):
                act.wait_ge(ld["wv"], g * 16 + 16)
                nc.scalar.activation(wv_hi[:, :], wv_raw[:, :], ACT.Copy).then_inc(wv_hi_ready, 1)

            def raw_qk(g, k):
                act.wait_ge(ld_prm[k % G], uses(g, k, G) * 16)
                for u in range(2 * NCH):
                    act.wait_ge(a_full, units(g, k, 6, u + 1))
                    if not (isinstance(g, int) and G * g + k < 1):
                        act.wait_ge(conv_done, units(g, k - 1, 4, u + 1))
                    o = (k % G) * 2 * PRM + (u // NCH) * PRM
                    nc.scalar.activation(raw[:, u * N:(u + 1) * N], a_ring[u % 2][:, :], ACT.Copy)
                    nc.scalar.activation(tap0[:, u * N:(u + 1) * N], a_ring[u % 2][:, :], ACT.Copy,
                                         scale=prm[:, o:o + 1]).then_inc(a_drained, 1)

            def gates(g, k):
                for c in range(NCH):
                    act.wait_ge(a_full, units(g, k, 6, 4 + c + 1))
                    if not (isinstance(g, int) and G * g + k < G - 1):
                        act.wait_ge(c_full, c_scores(g, k - G + 1) + B)
                    nc.scalar.activation(gate[:, (k % G) * T + c * N:(k % G) * T + (c + 1) * N],
                                         a_ring[c % 2][:, :], ACT.Silu).then_inc(a_drained, 1)

            def silu(g, k, part):
                for u in (2 * part, 2 * part + 1):
                    act.wait_ge(conv_done, units(g, k, 4, u + 1))
                    c = conv[:, u * N:(u + 1) * N]
                    nc.scalar.activation(c, c, ACT.Silu).then_inc(silu_done, 1)

            def normalise(g, k):
                act.wait_ge(rstd_ready, units(g, k, 1, 1))
                for u in range(2 * NCH):
                    act.wait_ge(t_full, units(g, k, 8, u + 1))
                    if not (isinstance(g, int) and G * g + k < 1):
                        act.wait_ge(t_full, units(g, k - 1, 8, 4 + u + 1))
                    for i in range(G):
                        t = u * G + i
                        ins = nc.scalar.activation(tok[:, t * P:(t + 1) * P], t_ring[u][:, i * P:(i + 1) * P],
                                                   ACT.Identity, scale=rstd[:, t:t + 1], bias=nmr[:, t:t + 1])
                    ins.then_inc(t_drained, 1)

            def affine(g, k):
                for u in range(2 * NCH):
                    o = (k % G) * 2 * PRM + (u // NCH) * PRM + TAPS + 1
                    act.wait_ge(t_full, units(g, k, 8, 4 + u + 1))
                    if not (isinstance(g, int) and G * g + k < 1):
                        act.wait_ge(c_full, c_scores(g, k - 1) + B)
                    nc.scalar.activation(qk[:, u * N:(u + 1) * N], t_ring[u][:, :], ACT.Identity,
                                         scale=prm[:, o:o + 1], bias=prm[:, o + 1:o + 2]).then_inc(t_drained, 1)

            high(0, 0)
            high_values(0)
            high(0, 1)
            raw_qk(0, 0)
            gates(0, 0)
            silu(0, 0, 0)
            silu(0, 0, 1)
            high(0, 2)
            raw_qk(0, 1)
            gates(0, 1)
            normalise(0, 0)
            silu(0, 1, 0)

            def step(g, k):
                n = G * g + k if isinstance(g, int) else None
                affine(g, k)
                if n is None or n + 1 < H:
                    silu(*head(g, k + 1), 1)
                if n is None or n + 2 < H:
                    raw_qk(*head(g, k + 2))
                if n is None or n + 3 < H:
                    high(*head(g, k + 3))
                if n is None or n + 1 < H:
                    normalise(*head(g, k + 1))
                if n is None or n + 2 < H:
                    gates(*head(g, k + 2))
                    silu(*head(g, k + 2), 0)
                if k == 1 and (n is None or g < NG - 1):
                    act.wait_ge(c_full, c_scores(g, 0))
                    high_values(g + 1)

            step(0, 0)
            with act.Fori(0, NG - 1) as g:
                for k in range(1, G):
                    step(g, k)
                step(g + 1, 0)
            for k in range(1, G):
                step(NG - 1, k)

            def gate_up_high(n, s, first=False):
                act.wait_ge(ld_we[s], n * 8 + (1 - s) * 8)
                if not first:
                    act.wait_ge(e_full, n * 4 - 8)
                w = slice(s * 3 * D, s * 3 * D + 2 * D)
                nc.scalar.activation(w_hi[:, w], w_raw[:, w], ACT.Copy).then_inc(w_hi_ready, 1)

            def down_high(n, s, first=False):
                act.wait_ge(ld_we[s], n * 8 + (1 - s) * 8)
                if not first:
                    act.wait_ge(e_down, n - 2)
                w = slice(s * 3 * D + 2 * D, (s + 1) * 3 * D)
                nc.scalar.activation(w_hi[:, w], w_raw[:, w], ACT.Copy).then_inc(down_hi_ready, 1)

            def gate_silu(n, first):
                for c in range(NCH):
                    act.wait_ge(e_full, (n - 1) * 4 + 2 * c + 1)
                    if not first:
                        act.wait_ge(u_prod, (n - 2) * NCH + c + 1)
                    cc = slice(c * N, (c + 1) * N)
                    nc.scalar.activation(silu_g[:, cc], e_ring[2 * c][:, :], ACT.Silu).then_inc(g_silu, 1)

            def act_high(n, first):
                for c in range(NCH):
                    act.wait_ge(e_weighted, (n - 1) * NCH + c + 1)
                    if not first:
                        act.wait_ge(e_down, n - 1)
                    cc = slice(c * N, (c + 1) * N)
                    nc.scalar.activation(act_hi[:, cc], act_w[:, cc], ACT.Copy).then_inc(e_hi, 1)

            act.wait_ge(a_full, 6 * H)
            for n in (1, 2):
                gate_up_high(n, n - 1, True)
                down_high(n, n - 1, True)
            stream_norm(1, False)
            stream_norm(2, True)
            for c in range(1):
                act.wait_ge(r_full, 1)
                nc.scalar.activation(score, bank[4][:, 0:TT * E_ROUTED], ACT.Sigmoid).then_inc(r_score, 1)
            gate_silu(1, True)
            gate_up_high(3, 0)
            act_high(1, True)
            gate_silu(2, False)
            for c in range(NCH):
                act.wait_ge(r_tr_full, c + 1)
                nc.scalar.activation(routeT[:, c * N:(c + 1) * N], y_acc[c][0:E_ROUTED, :],
                                     ACT.Copy).then_inc(r_tr_ready, 1)
            gate_up_high(4, 1)
            act_high(2, False)
            down_high(3, 0)

            def step(n, s, left=2):
                gate_silu(n, False)
                if left > 1:
                    gate_up_high(n + 2, s)
                act_high(n, False)
                if left > 0:
                    down_high(n + 1, 1 - s)

            with act.Fori(0, E_ROUTED // 2 - 1) as r:
                for s in range(2):
                    step(r * 2 + (3 + s), s)
            step(E_ALL - 1, 0, 1)
            step(E_ALL, 1, 0)

        @block.vector
        def _(dve):
            steps = Steps(dve, dve_step, body=G * 23)

            def norm_factors(tiles, width):
                st = stats[:, 0:6 * tiles].rearrange("p (t s) -> p s t", s=6)
                me, m2e, mo, m2o = st[:, 1, :], st[:, 2, :], st[:, 4, :], st[:, 5, :]
                c = slice(0, tiles)
                dif = steps.did(nc.vector.tensor_tensor(s_dif[:, c], me, mo, ALU.subtract))
                nc.vector.tensor_tensor(s_sum[:, c], me, mo, ALU.add)
                nc.vector.tensor_tensor(s_var[:, c], m2e, m2o, ALU.add)
                steps.after(dif)
                a = steps.did(nc.vector.tensor_tensor(s_t[:, c], s_dif[:, c], s_dif[:, c], ALU.mult))
                steps.after(a)
                a = steps.did(nc.vector.scalar_tensor_tensor(
                    out=s_var[:, c], in0=s_t[:, c], scalar=width / 4.0, in1=s_var[:, c],
                    op0=ALU.mult, op1=ALU.add))
                steps.after(a)
                a = steps.did(nc.vector.tensor_scalar(s_var[:, c], s_var[:, c], 1.0 / width, EPS,
                                                      ALU.mult, ALU.add))
                steps.after(a)
                a = steps.did(nc.vector.tensor_scalar(
                    s_y[:, c].bitcast(I32), s_var[:, c].bitcast(I32), -0.5, RSQRT_SEED,
                    ALU.mult, ALU.add))
                for i in range(3):
                    steps.after(a)
                    a = steps.did(nc.vector.tensor_tensor(s_t[:, c], s_y[:, c], s_y[:, c], ALU.mult))
                    steps.after(a)
                    a = steps.did(nc.vector.scalar_tensor_tensor(
                        out=s_t[:, c], in0=s_t[:, c], scalar=-0.5, in1=s_var[:, c],
                        op0=ALU.mult, op1=ALU.mult))
                    steps.after(a)
                    y = rstd if i == 2 else s_y
                    a = steps.did(nc.vector.scalar_tensor_tensor(
                        out=y[:, c], in0=s_t[:, c], scalar=1.5, in1=s_y[:, c],
                        op0=ALU.add, op1=ALU.mult))
                steps.after(a)
                return nc.vector.scalar_tensor_tensor(
                    out=nmr[:, c], in0=s_sum[:, c], scalar=-0.5, in1=rstd[:, c],
                    op0=ALU.mult, op1=ALU.mult)

            def stream_stats():
                for t in range(TT):
                    ins = nc.vector.bn_stats(stats[:, 6 * t:6 * t + 6], x[:, t * D:(t + 1) * D])
                steps.after(steps.did(ins))
                norm_factors(TT, D).then_inc(ln_rstd, 1)

            def stream_split(i, n):
                for u in range(KT * NCH):
                    uu = slice(u * N, (u + 1) * N)
                    dve.wait_ge(ln_copied, i * KT * NCH + u + 1)
                    a = steps.did(nc.vector.tensor_copy(xT_hi[:, uu], xT[:, uu]))
                    steps.after(a)
                    nc.vector.tensor_tensor(xT_lo[:, uu], xT[:, uu], xT_hi[:, uu].bitcast(F32),
                                            ALU.subtract).then_inc(ln_split, 1)

            dve.wait_ge(ld["x"], 16)
            stream_stats()
            dve.wait_ge(ld["const"], 32)
            a = steps.did(nc.vector.memset(dmask[:, :], 0.0))
            steps.after(a)
            dm = dmask[:, :].rearrange("p (b c) -> p b c", b=B)
            for b in range(B):
                nc.vector.tensor_copy(dm[:, b, 0:P], ident[:, :])
                ins = nc.vector.tensor_copy(dm[:, b, L:L + P], ident[:, :])
            ins.then_inc(dmask_ready, 1)
            for t in range(TT):
                dve.wait_ge(x_energy, t // 2 + 1)
                nc.vector.tensor_reduce(small[:, t:t + 1], bank[4 + t // 2][:, (t % 2) * L:(t % 2 + 1) * L],
                                        op=ALU.max, axis=AX.X, negate=True).then_inc(x_max, 1)
            dve.wait_ge(x_exp, TT)
            a = steps.did(nc.vector.reciprocal(small[:, 16:16 + TT], small[:, 8:8 + TT]))
            steps.after(a)
            for t in range(TT):
                nc.vector.tensor_scalar(att[:, t * L:(t + 1) * L], att[:, t * L:(t + 1) * L],
                                        small[:, 16 + t:17 + t], None, ALU.mult).then_inc(x_soft, 1)
            for u in range(KT * NCH):
                dve.wait_ge(x_attT_full, u + 1)
                nc.vector.tensor_copy(attT[:, u * N:(u + 1) * N], bank[4 + u][:, :]).then_inc(x_attT_ready, 1)
            stream_split(0, 0)
            a = steps.did(nc.vector.memset(obetT, 0.0))
            dve.wait_ge(b_ready, NCH)
            steps.after(a)
            bt = betaT.rearrange("h (b t) -> h b t", b=B)
            ob = obetT.rearrange("h (b c) -> h b c", b=B)
            nc.vector.tensor_scalar(ob[:, :, 1:L], bt[:, :, 1:L], -1.0, 1.0, ALU.mult,
                                    ALU.add).then_inc(obet_ready, 1)
            nc.vector.tensor_scalar(ob[:, :, L + 1:DW], bt[:, :, P + 1:L], -1.0, 1.0, ALU.mult,
                                    ALU.add).then_inc(obet_ready, 1)
            dve.wait_ge(b_tok_full, 1)
            nc.vector.tensor_copy(beta_tok[:, :], bank[2][:, 0:TT * H]).then_inc(b_tok_ready, 1)
            dve.wait_ge(b_tok_ready, 1)
            bt_v = beta_tok[:, :].rearrange("p (t h) -> p t h", t=TT)

            def scale_values(g, first):
                for t in range(TT):
                    at = t if first else c_values(g) + t
                    dve.wait_ge(c_full, at + 1)
                    gg = 0 if first else g + 1
                    nc.vector.tensor_tensor(
                        values[:, t * N:(t + 1) * N].rearrange("p (h c) -> p h c", h=G),
                        c_ring[t % 2][:, :].rearrange("p (h c) -> p h c", h=G),
                        bt_v[:, t, bass.ds(gg * G, G)].unsqueeze(2).broadcast_to([P, G, P]),
                        ALU.mult).then_inc(c_drained, 1)

            def head_decay(g, k):
                s = k % 2
                dve.wait_ge(ld_obet[s], uses(g, k, 2) * 16)
                if not (isinstance(g, int) and G * g + k < 1):
                    dve.wait_ge(c_drained, c_scores(g, k - 1) + B)
                nc.vector.tensor_tensor_scan(decay[:, :], obet[:, s * B * DW:(s + 1) * B * DW],
                                             dmask[:, :], 0.0, ALU.mult, ALU.add).then_inc(decay_ready, 1)

            def head_stats(g, k, part):
                for u in (2 * part, 2 * part + 1):
                    dve.wait_ge(t_full, units(g, k, 8, u + 1))
                    for i in range(G):
                        t = u * G + i
                        ins = nc.vector.bn_stats(stats[:, 6 * t:6 * t + 6], t_ring[u][:, i * P:(i + 1) * P])
                if part == 0:
                    return
                steps.after(steps.did(ins))
                if not (isinstance(g, int) and G * g + k < 1):
                    dve.wait_ge(t_drained, units(g, k - 1, 8, 4))

            def head_factors():
                norm_factors(2 * TT, P).then_inc(rstd_ready, 1)

            def taps(g, k, part):
                o = (k % G) * 2 * PRM + part * PRM
                if part == 0:
                    dve.wait_ge(ld_prm[k % G], uses(g, k, G) * 16)
                made = []
                for u in (2 * part, 2 * part + 1):
                    dve.wait_ge(a_drained, units(g, k, 6, u + 1))
                    if not (isinstance(g, int) and G * g + k < 1):
                        dve.wait_ge(t_full, units(g, k - 1, 8, u + 1))
                    made.append(steps.did(nc.vector.tensor_scalar(
                        conv[:, u * N:(u + 1) * N], raw[:, u * N:(u + 1) * N],
                        prm[:, o + 3:o + 4], prm[:, o + 4:o + 5], ALU.mult, ALU.add)))
                for back in (1, 2):
                    for i, u in enumerate((2 * part, 2 * part + 1)):
                        y = conv[:, u * N:(u + 1) * N].rearrange("p (b t) -> p b t", b=BPC)[:, :, back:L]
                        r = raw[:, u * N:(u + 1) * N].rearrange("p (b t) -> p b t", b=BPC)[:, :, 0:L - back]
                        steps.after(made[i])
                        ins = nc.vector.scalar_tensor_tensor(
                            out=y, in0=r, scalar=prm[:, o + 3 - back:o + 4 - back], in1=y,
                            op0=ALU.mult, op1=ALU.add)
                        if back == 2:
                            ins.then_inc(taps_done, 1)
                        else:
                            made[i] = steps.did(ins)

            def decayed(g, k, part):
                dve.wait_ge(decay_ready, units(g, k, 1, 1))
                for b in (2 * part, 2 * part + 1):
                    dve.wait_ge(c_full, c_scores(g, k) + (b + 1))
                    bb_ = slice(b * DW, (b + 1) * DW)
                    nc.vector.tensor_tensor(probs[:, bb_], c_ring[b % 2][:, 0:DW], decay[:, bb_],
                                            ALU.mult).then_inc(c_drained, 1)

            def gated_out(g, k):
                dve.wait_ge(c_full, c_scores(g, 0))
                dve.wait_ge(a_drained, units(g, k, 6, 6))
                for c in range(NCH):
                    dve.wait_ge(c_full, c_outputs(g, k) + (c + 1))
                    nc.vector.tensor_tensor(gated[:, k * T + c * N:k * T + (c + 1) * N], c_ring[c % 2][:, :],
                                            gate[:, k * T + c * N:k * T + (c + 1) * N],
                                            ALU.mult).then_inc(c_drained, 1)

            def add_projection(at, some):
                for u in some:
                    dve.wait_ge(c_full, at + (u + 1))
                    xs = x[:, u * N:(u + 1) * N]
                    nc.vector.tensor_tensor(xs, c_ring[u % 2][:, :], xs, ALU.add).then_inc(c_drained, 1)

            taps(0, 0, 0)
            taps(0, 0, 1)
            scale_values(0, True)
            head_decay(0, 0)
            head_stats(0, 0, 0)
            head_stats(0, 0, 1)
            head_factors()
            taps(0, 1, 0)
            taps(0, 1, 1)

            def step(g, k):
                n = G * g + k if isinstance(g, int) else None
                if n is None or n + 1 < H:
                    head_stats(*head(g, k + 1), 0)
                    head_stats(*head(g, k + 1), 1)
                    head_factors()
                if k == 0 and n != 0:
                    at = c_project(g - 1)
                    add_projection(at, (0,))
                    taps(*head(g, k + 2), 0)
                    add_projection(at, (1,))
                    taps(*head(g, k + 2), 1)
                    add_projection(at, (2, 3))
                    decayed(g, k, 0)
                    decayed(g, k, 1)
                else:
                    decayed(g, k, 0)
                    decayed(g, k, 1)
                    if n is None or n + 2 < H:
                        taps(*head(g, k + 2), 0)
                        taps(*head(g, k + 2), 1)
                gated_out(g, k)
                if n is None or n + 1 < H:
                    head_decay(*head(g, k + 1))
                if k == G - 1:
                    if n is None or g < NG - 1:
                        scale_values(g, False)
                    else:
                        add_projection(c_values(g), range(TT // 2))

            dve.wait_ge(c_drained, TT)
            step(0, 0)
            with dve.Fori(0, NG - 1) as g:
                steps.enter(g)
                for k in range(1, G):
                    step(g, k)
                step(g + 1, 0)
            steps.leave(NG - 1)
            for k in range(1, G):
                step(NG - 1, k)
            dve.wait_ge(c_drained, c_values(NG - 1) + TT // 2)
            stream_stats()
            for u in range(TT // 2):
                dve.wait_ge(x_mix_full, u + 1)
                xs = x[:, u * N:(u + 1) * N]
                nc.vector.tensor_tensor(xs, bank[4 + u][:, :], xs, ALU.add).then_inc(x_mixed, 1)
            dve.wait_ge(x_mixed, TT // 2)
            stream_stats()
            stream_split(2, 1)

            def u_times(n, first):
                for c in range(NCH):
                    dve.wait_ge(e_full, (n - 1) * 4 + 2 * c + 2)
                    dve.wait_ge(g_silu, (n - 1) * NCH + c + 1)
                    if not first:
                        dve.wait_ge(e_weighted, (n - 2) * NCH + c + 1)
                    cc = slice(c * N, (c + 1) * N)
                    nc.vector.tensor_tensor(prod[:, cc], e_ring[2 * c + 1][:, :], silu_g[:, cc],
                                            ALU.mult).then_inc(u_prod, 1)

            def act_low(n):
                for c in range(NCH):
                    dve.wait_ge(e_hi, (n - 1) * NCH + c + 1)
                    cc = slice(c * N, (c + 1) * N)
                    nc.vector.tensor_tensor(act_lo[:, cc], act_w[:, cc], act_hi[:, cc].bitcast(F32),
                                            ALU.subtract).then_inc(e_lo, 1)

            t8 = lambda ap, n: ap.rearrange("p (t e) -> p t e", t=TT)
            sc3 = choice.rearrange("p (t e) -> p t e", t=TT)
            dve.wait_ge(r_score, 1)
            dve.wait_ge(ld["router"], 32)

            def op(ins):
                steps.after(steps.did(ins))

            op(nc.vector.tensor_tensor(sc3, score.rearrange("p (t e) -> p t e", t=TT),
                                       rb.unsqueeze(1).broadcast_to([P, TT, E_ROUTED]), ALU.add))
            c4 = choice.rearrange("p (q e) -> p e q", e=EPG)
            hi1, lo1, hi2, lo2, top, sec = (gpair[:, i * 32:(i + 1) * 32] for i in range(6))
            op(nc.vector.tensor_tensor(hi1, c4[:, 0, :], c4[:, 1, :], ALU.max))
            op(nc.vector.tensor_tensor(lo1, c4[:, 0, :], c4[:, 1, :], ALU.min))
            op(nc.vector.tensor_tensor(hi2, c4[:, 2, :], c4[:, 3, :], ALU.max))
            op(nc.vector.tensor_tensor(lo2, c4[:, 2, :], c4[:, 3, :], ALU.min))
            op(nc.vector.tensor_tensor(top, hi1, hi2, ALU.max))
            op(nc.vector.tensor_tensor(sec, hi1, hi2, ALU.min))
            op(nc.vector.tensor_tensor(lo1, lo1, lo2, ALU.max))
            op(nc.vector.tensor_tensor(sec, sec, lo1, ALU.max))
            op(nc.vector.tensor_tensor(top, top, sec, ALU.add))

            def ranks(dst, src, n, tri):
                v = src.rearrange("p (t e) -> p t e", t=TT)
                other = v.unsqueeze(2).broadcast_to([P, TT, n, n])
                own = v.unsqueeze(3).broadcast_to([P, TT, n, n])
                a = cmp_a[:, 0:TT * n * n].rearrange("p (t e f) -> p t e f", t=TT, e=n)
                b = cmp_b[:, 0:TT * n * n].rearrange("p (t e f) -> p t e f", t=TT, e=n)
                mask = tri.rearrange("p (e f) -> p e f", e=n).unsqueeze(1).broadcast_to([P, TT, n, n])
                op(nc.vector.tensor_tensor(b, other, own, ALU.is_equal))
                op(nc.vector.tensor_tensor(b, b, mask, ALU.mult))
                op(nc.vector.tensor_tensor(a, other, own, ALU.is_gt))
                op(nc.vector.tensor_tensor(a, a, b, ALU.add))
                op(nc.vector.tensor_reduce(dst.rearrange("p (t e) -> p t e", t=TT), a, op=ALU.add, axis=AX.X))

            ranks(gmask, top, EG, tie[:, E_ROUTED * E_ROUTED:])
            op(nc.vector.tensor_scalar(gmask, gmask, TOPK_GROUP - 0.5, None, ALU.is_lt))
            gm4 = gmask.unsqueeze(2).broadcast_to([P, TT * EG, EPG])
            m4 = masked.rearrange("p (q e) -> p q e", e=EPG)
            op(nc.vector.tensor_tensor(m4, choice.rearrange("p (q e) -> p q e", e=EPG), gm4, ALU.mult))
            op(nc.vector.tensor_scalar(gmask, gmask, -VERY_NEGATIVE, VERY_NEGATIVE, ALU.mult, ALU.add))
            op(nc.vector.tensor_tensor(m4, m4, gm4, ALU.add))
            ranks(rank, masked, E_ROUTED, tie[:, 0:E_ROUTED * E_ROUTED])
            op(nc.vector.tensor_scalar(rank, rank, TOP_K - 0.5, None, ALU.is_lt))
            op(nc.vector.tensor_tensor(weight, rank, score, ALU.mult))
            w3 = weight.rearrange("p (t e) -> p t e", t=TT)
            dn = denom[:, 0:TT]
            op(nc.vector.tensor_reduce(dn, w3, op=ALU.add, axis=AX.X))
            op(nc.vector.tensor_scalar(dn, dn, 1e-20, None, ALU.add))
            op(nc.vector.reciprocal(dn, dn))
            op(nc.vector.tensor_tensor(w3, w3, dn.unsqueeze(2).broadcast_to([P, TT, E_ROUTED]), ALU.mult))
            nc.vector.tensor_scalar(weight, weight, ROUTED_SCALE, None, ALU.mult).then_inc(r_ready, 1)

            u_times(1, True)
            act_low(1)
            u_times(2, False)
            act_low(2)
            with dve.Fori(0, E_ROUTED // 2) as r:
                for s in range(2):
                    u_times(r * 2 + (3 + s), False)
                    act_low(r * 2 + (3 + s))
            for u in range(TT // 2):
                dve.wait_ge(y_full, u + 1)
                xs = x[:, u * N:(u + 1) * N]
                nc.vector.tensor_tensor(xs, y_acc[u][:, :], xs, ALU.add).then_inc(y_added, 1)

        @block.tensor
        def _(pe):
            def mm(o, l, r, start, stop):
                return nc.tensor.matmul(o, l, r, start=start, stop=stop)

            def mm3(o, l_hi, l_lo, r_hi, r_lo, start, stop, loose=False):
                nc.tensor.matmul(o, l_hi, r_lo, start=start, stop=False, skip_group_check=loose)
                nc.tensor.matmul(o, l_lo, r_hi, start=False, stop=False, skip_group_check=loose)
                return nc.tensor.matmul(o, l_hi, r_hi, start=False, stop=stop, skip_group_check=loose)

            def stream_transpose(i):
                for u in range(KT * NCH):
                    kt, c = divmod(u, NCH)
                    for j in range(G):
                        t = c * G + j
                        pe.wait_ge(ln_norm, i * TT + t + 1)
                        ins = nc.tensor.transpose(bank[u][:, j * P:(j + 1) * P],
                                                  x_norm[:, t * D + kt * P:t * D + (kt + 1) * P], ident[:, :])
                    ins.then_inc(ln_full, 1)

            pe.wait_ge(ld["ctx"], 48)
            for u in range(2 * NCH):
                s, c = divmod(u, NCH)
                mm(bank[4 + u][:, :], xw[:, s * P:(s + 1) * P], ctxT[:, c * N:(c + 1) * N],
                   True, True).then_inc(x_qk_full, 1)
            pe.wait_ge(x_qk_ready, 2 * NCH)
            for t in range(TT):
                b = t // KT
                ins = mm(bank[4 + t // 2][:, (t % 2) * L:(t % 2 + 1) * L], qctx[:, t * P:(t + 1) * P],
                         kctx[:, b * L:(b + 1) * L], True, True)
                if t % 2:
                    ins.then_inc(x_energy, 1)
            pe.wait_ge(ld["const"], 32)
            pe.wait_ge(x_soft, TT)
            for u in range(KT * NCH):
                nt, c = divmod(u, NCH)
                for j in range(G):
                    t = c * G + j
                    ins = nc.tensor.transpose(bank[4 + u][:, j * P:(j + 1) * P],
                                              att[:, t * L + nt * P:t * L + (nt + 1) * P], ident[:, :])
                ins.then_inc(x_attT_full, 1)
            stream_transpose(0)
            pe.wait_ge(ld["beta"], 32)
            pe.wait_ge(ln_copied, KT * NCH)
            for c in range(NCH):
                for kt in range(KT):
                    ins = mm(bank[c][0:H, :], wb[:, kt * H:(kt + 1) * H],
                             xT[:, kt * T + c * N:kt * T + (c + 1) * N], kt == 0, kt == KT - 1)
                ins.then_inc(b_full, 1)
            pe.wait_ge(b_ready, NCH)
            for t in range(TT):
                ins = nc.tensor.transpose(bank[2][:, t * H:(t + 1) * H], betaT[:, t * P:(t + 1) * P],
                                          ident[0:H, 0:H])
            ins.then_inc(b_tok_full, 1)

            def xs_(t_, kt, a, b):
                return t_[:, kt * T + a:kt * T + b]

            def values_of(g, first):
                pe.wait_ge(wv_lo_ready, 1 if first else g + 2)
                for t in range(TT):
                    at = t if first else c_values(g) + t
                    if not first or t >= 2:
                        pe.wait_ge(c_drained, at - 1)
                    for kt in range(KT):
                        w = slice(kt * N, (kt + 1) * N)
                        ins = mm3(c_ring[t % 2][:, :], xs_(xT_hi, kt, t * P, (t + 1) * P),
                                  xs_(xT_lo, kt, t * P, (t + 1) * P), wv_hi[:, w], wv_lo[:, w],
                                  kt == 0, kt == KT - 1)
                    ins.then_inc(c_full, 1)

            def project_in(g, k, what):
                s = k % 2
                if what == 0:
                    pe.wait_ge(w_lo_ready, units(g, k, 1, 1))
                for c in range(NCH):
                    u = what * NCH + c
                    if not (isinstance(g, int) and G * g + k < 1 and u < 2):
                        pe.wait_ge(a_drained, units(g, k, 6, u - 1))
                    for kt in range(KT):
                        o = s * 3 * D + what * D + kt * P
                        ins = mm3(a_ring[c % 2][:, :], w_hi[:, o:o + P], w_lo[:, o:o + P],
                                  xs_(xT_hi, kt, c * N, (c + 1) * N), xs_(xT_lo, kt, c * N, (c + 1) * N),
                                  kt == 0, kt == KT - 1)
                    ins.then_inc(a_full, 1)

            def to_tokens(g, k):
                for u in range(2 * NCH):
                    pe.wait_ge(silu_done, units(g, k, 4, u + 1))
                    if not (isinstance(g, int) and G * g + k < 1):
                        pe.wait_ge(t_drained, units(g, k, 8, u - 3))
                    for i in range(G):
                        t = u * G + i
                        ins = nc.tensor.transpose(t_ring[u][:, i * P:(i + 1) * P], conv[:, t * P:(t + 1) * P],
                                                  ident[:, :])
                    ins.then_inc(t_full, 1)

            def to_features(g, k):
                for u in range(2 * NCH):
                    pe.wait_ge(t_drained, units(g, k, 8, u + 1))
                    for i in range(G):
                        t = u * G + i
                        ins = nc.tensor.transpose(t_ring[u][:, i * P:(i + 1) * P], tok[:, t * P:(t + 1) * P],
                                                  ident[:, :])
                    ins.then_inc(t_full, 1)

            def scores(g, k, part):
                if part == 0:
                    pe.wait_ge(t_drained, units(g, k, 8, 8))
                for b in (2 * part, 2 * part + 1):
                    pe.wait_ge(c_drained, c_scores(g, k) + (b - 1))
                    q0, k0 = b * L, T + b * L
                    mm(c_ring[b % 2][:, 0:L], qk[:, k0:k0 + P], qk[:, q0:q0 + L], True, True)
                    mm(c_ring[b % 2][:, L:DW], qk[:, k0 + P:k0 + L], qk[:, q0 + P:q0 + L],
                       True, True).then_inc(c_full, 1)

            def outputs(g, k):
                for c in range(NCH):
                    for i in range(BPC):
                        b = c * BPC + i
                        pe.wait_ge(c_drained, c_scores(g, k) + max(b + 1, B - 1 + c))
                        v0 = values[:, (2 * b) * N + k * P:(2 * b) * N + (k + 1) * P]
                        v1 = values[:, (2 * b + 1) * N + k * P:(2 * b + 1) * N + (k + 1) * P]
                        o = c_ring[c % 2]
                        mm(o[:, i * L:(i + 1) * L], v0, probs[:, b * DW:b * DW + L], True, False)
                        ins = mm(o[:, i * L + P:(i + 1) * L], v1, probs[:, b * DW + L:(b + 1) * DW], False, True)
                    ins.then_inc(c_full, 1)

            def project_out(g, at):
                pe.wait_ge(ld["wo"], g * 16 + 16)
                pe.wait_ge(c_drained, c_outputs(g, G - 1) + NCH)
                for u in range(TT // 2):
                    pe.wait_ge(c_drained, at + (u - 1))
                    for i in range(2):
                        t = 2 * u + i
                        for h in range(G):
                            ins = mm(c_ring[u % 2][:, i * D:(i + 1) * D],
                                     gated[:, h * T + t * P:h * T + (t + 1) * P],
                                     wo[:, h * D:(h + 1) * D], h == 0, h == G - 1)
                    ins.then_inc(c_full, 1)

            pe.wait_ge(ln_split, KT * NCH)
            for what in range(3):
                project_in(0, 0, what)
            values_of(0, True)
            pe.wait_ge(b_tok_ready, 1)
            to_tokens(0, 0)
            for what in range(3):
                project_in(0, 1, what)

            def step(g, k):
                n = G * g + k if isinstance(g, int) else None
                to_features(g, k)
                if n is None or n + 2 < H:
                    project_in(*head(g, k + 2), 0)
                if n is None or n + 1 < H:
                    to_tokens(*head(g, k + 1))
                if n is None or n + 2 < H:
                    project_in(*head(g, k + 2), 1)
                if k == 0 and n != 0:
                    project_out(g - 1, c_project(g - 1))
                scores(g, k, 0)
                if n is None or n + 2 < H:
                    project_in(*head(g, k + 2), 2)
                scores(g, k, 1)
                outputs(g, k)
                if k == G - 1:
                    if n is None or g < NG - 1:
                        values_of(g, False)
                    else:
                        project_out(g, c_values(g))

            step(0, 0)
            with pe.Fori(0, NG - 1) as g:
                for k in range(1, G):
                    step(g, k)
                step(g + 1, 0)
            for k in range(1, G):
                step(NG - 1, k)

            stream_transpose(1)
            pe.wait_ge(x_attT_ready, KT * NCH)
            pe.wait_ge(ln_copied, 2 * KT * NCH)
            for u in range(TT // 2):
                for i in range(2):
                    t = 2 * u + i
                    for nt in range(KT):
                        ins = mm(bank[4 + u][:, i * D:(i + 1) * D], xT[:, nt * T + t * P:nt * T + (t + 1) * P],
                                 attT[:, nt * T + (t // KT) * L:nt * T + (t // KT + 1) * L],
                                 nt == 0, nt == KT - 1)
                ins.then_inc(x_mix_full, 1)
            stream_transpose(2)
            pe.wait_ge(ld["router"], 32)
            pe.wait_ge(ln_copied, 3 * KT * NCH)
            for t in range(TT):
                for kt in range(KT):
                    ins = mm(bank[4][:, t * E_ROUTED:(t + 1) * E_ROUTED],
                             xT[:, kt * T + t * P:kt * T + (t + 1) * P], rw[:, kt * H:(kt + 1) * H],
                             kt == 0, kt == KT - 1)
            ins.then_inc(r_full, 1)

            def gate_up(n, s, first):
                pe.wait_ge(w_lo_ready, n + H)
                for c in range(NCH):
                    for j in range(2):
                        if not first:
                            pe.wait_ge(g_silu if j == 0 else u_prod, (n - 2) * NCH + c + 1)
                        for kt in range(KT):
                            o = s * 3 * D + j * D + kt * P
                            ins = mm3(e_ring[2 * c + j][:, :], w_hi[:, o:o + P], w_lo[:, o:o + P],
                                      xs_(xT_hi, kt, c * N, (c + 1) * N), xs_(xT_lo, kt, c * N, (c + 1) * N),
                                      kt == 0, kt == KT - 1)
                        ins.then_inc(e_full, 1)

            def down(n, s, first, last):
                pe.wait_ge(down_lo_ready, n)
                o = s * 3 * D + 2 * D
                for t in range(TT):
                    if t % G == 0:
                        pe.wait_ge(e_lo, (n - 1) * NCH + t // G + 1)
                    tt = slice(t * P, (t + 1) * P)
                    ins = mm3(y_acc[t // 2][:, (t % 2) * D:(t % 2 + 1) * D], act_hi[:, tt], act_lo[:, tt],
                              w_hi[:, o:o + D], w_lo[:, o:o + D], first and t % 2 == 0, last, loose=True)
                    if last and t % 2:
                        ins.then_inc(y_full, 1)
                if not last:
                    ins.then_inc(e_down, 1)

            pe.wait_ge(ln_split, 2 * KT * NCH)
            gate_up(1, 0, True)
            gate_up(2, 1, False)
            pe.wait_ge(r_score, 1)
            pe.wait_ge(r_ready, 1)
            for c in range(NCH):
                for j in range(G):
                    t = c * G + j
                    ins = nc.tensor.transpose(y_acc[c][0:E_ROUTED, j * P:(j + 1) * P],
                                              weight[:, t * E_ROUTED:(t + 1) * E_ROUTED], ident[:, :])
                ins.then_inc(r_tr_full, 1)
            pe.wait_ge(r_tr_ready, NCH)
            down(1, 0, True, False)
            with pe.Fori(0, E_ROUTED // 2) as r:
                for s in range(2):
                    gate_up(r * 2 + (3 + s), s, False)
                    down(r * 2 + (2 + s), 1 - s, False, False)
            down(E_ALL, 1, False, True)


def kernel(**inputs):
    import numpy as np
    import concourse.bacc as bacc
    from concourse.bass_utils import run_bass_kernel_spmd

    a = {k: np.asarray(v) for k, v in inputs.items()}

    def tiles(w):
        return w.reshape(KT, P, -1).transpose(1, 0, 2)

    def tokens(v):
        return v.reshape(TT, P, D).transpose(1, 0, 2).reshape(P, TT * D)

    heads = [tiles(a[f"L0_attn_{n}"]).reshape(P, KT, H, P).transpose(2, 0, 1, 3) for n in ("Wq", "Wk", "Wg")]
    wh = np.stack(heads, axis=2).reshape(H, P, 3 * D)
    prm = []
    for n in "qk":
        cw = a[f"L0_attn_{n}conv_w"].reshape(H, P, TAPS)
        cb = a[f"L0_attn_{n}conv_b"].reshape(H, P, 1)
        nw, nb = (np.broadcast_to(a[f"L0_attn_{n}n_{s}"].reshape(1, P, 1), (H, P, 1)) for s in "wb")
        prm += [cw, cb, nw, nb]
    prm = np.concatenate(prm, axis=2)
    wv = tiles(a["L0_attn_Wv"]).reshape(P, KT, NG, N).transpose(2, 0, 1, 3).reshape(NG, P, KT * N)
    wo = a["L0_attn_Wo"].reshape(NG, G, P, D).transpose(0, 2, 1, 3).reshape(NG, P, G * D)

    def up(w):
        return w.reshape(-1, P, KT, P).transpose(0, 3, 2, 1).reshape(-1, P, D)

    gw = np.concatenate([up(a["L0_ffn_sh_gate_w"]), up(a["L0_ffn_gate_w"])])
    uw = np.concatenate([up(a["L0_ffn_sh_up_w"]), up(a["L0_ffn_up_w"])])
    dw = np.concatenate([a["L0_ffn_sh_down_w"].reshape(D, E_SHARED, P).transpose(1, 2, 0),
                         a["L0_ffn_down_w"].transpose(0, 2, 1)])
    we = np.concatenate([gw, uw, dw], axis=2)
    lower = [np.broadcast_to(np.tril(np.ones((n, n), np.float32), -1).reshape(1, n * n), (P, n * n))
             for n in (E_ROUTED, EG)]
    arrays = {
        "x": tokens(a["x"]),
        "ctx": a["ctx_1024"].reshape(T, P).T,
        "xw": np.concatenate([a["L0_xattn_Wq"].T, a["L0_xattn_Wk"].T], axis=1),
        "xb": np.stack([a["L0_xattn_bq"], a["L0_xattn_bk"]], axis=1),
        "wb": tiles(a["L0_attn_Wb"]).reshape(P, KT * H),
        "bb": a["L0_attn_bb"].reshape(H, 1),
        "wh": wh, "prm": prm, "wv": wv, "wo": wo,
        "rw": tiles(a["L0_ffn_gate_weight"].T).reshape(P, KT * E_ROUTED),
        "rb": a["L0_ffn_e_score_correction_bias"].reshape(1, E_ROUTED),
        "we": we,
        "ident": np.eye(P, dtype=np.float32),
        "tie": np.concatenate(lower, axis=1),
    }
    arrays = {f"in_{k}": np.ascontiguousarray(v) for k, v in arrays.items()}
    nc = bacc.Bacc("TRN2", target_bir_lowering=False, num_devices=1)
    args = [nc.dram_tensor(k, v.shape, mybir.dt.from_np(v.dtype), kind="ExternalInput").ap()
            for k, v in arrays.items()]
    out = nc.dram_tensor("out_x", [P, TT * D], F32, kind="ExternalOutput").ap()
    decoder_layer(nc, *args, out)
    r = run_bass_kernel_spmd(nc, [arrays], core_ids=[0])
    got = np.asarray(r.results[0]["out_x"])
    return got.reshape(P, TT, D).transpose(1, 0, 2).reshape(B, L, D)
```

```python
from contextlib import ExitStack

import concourse.bass as bass
from concourse import mybir

F32 = mybir.dt.float32
F32R = mybir.dt.float32r
I32 = mybir.dt.int32
ALU = mybir.AluOpType
ACT = mybir.ActivationFunctionType
AX = mybir.AxisListType

P = 128
B, L, D = 4, 256, 256
T = B * L
TT = T // P
KT = D // P
N = 512
NCH = T // N
BPC = N // L
H = 16
G = 4
NG = H // G
NP = H // 2
PW = 2 * P
RT = TT * 16
TAPS = 4
PRM = TAPS + 3
DW = L + P
E_ROUTED, E_SHARED = 16, 2
E_ALL = E_ROUTED + E_SHARED
EG = 4
EPG = E_ROUTED // EG
TOPK_GROUP, TOP_K = 2, 4
ROUTED_SCALE = 2.5
EPS = 1e-5
RSQRT_SEED = 1597463007.0
VERY_NEGATIVE = -3.0e38

V_UNITS = TT // 2
C_HEAD = V_UNITS // 2 + B + V_UNITS // 2 + NCH


def c_scores(g, k):
    if isinstance(g, int) and G * g + k == 0:
        return V_UNITS
    if isinstance(g, int) and G * g + k == H - 1:
        return C_HEAD * (H - 1)
    return C_HEAD * G * g + (C_HEAD * G * (k // G) + C_HEAD * (k % G) + V_UNITS // 2)


def c_project(g, k):
    return c_scores(g, k) - V_UNITS // 2


def c_values(g, k):
    return c_scores(g, k) + B


def c_outputs(g, k):
    last = isinstance(g, int) and G * g + k >= H - 2
    return c_scores(g, k) + (B if last else B + V_UNITS // 2)


def head(g, k):
    return (g + k // G if k // G else g), k % G


def units(g, k, per, more=0):
    return g * (G * per) + (k * per + more)


def uses(g, k, ring):
    return g * (G // ring) + (k // ring + 1)


class Steps:

    def __init__(self, eng, sem, body=0):
        self.eng, self.sem, self.n, self.g, self.body = eng, sem, 0, 0, body

    def did(self, ins):
        ins.then_inc(self.sem, 1)
        self.n += 1
        return self.n

    def after(self, n):
        if self.n and n:
            self.eng.wait_ge(self.sem, self.g * self.body + n)

    def enter(self, g):
        self.g, self.start = g, self.n

    def leave(self, rounds):
        assert self.n - self.start == self.body, (self.n - self.start, self.body)
        self.g, self.n = 0, self.n + self.body * (rounds - 1)


def decoder_layer(nc, x_in, ctx_in, xw_in, xb_in, wb_in, bb_in, w_in, prm_in, wv_in, wo_in,
                  rw_in, rb_in, ident_in, tie_in, out):
    obet_rows = nc.dram_tensor("obet_rows", [H, B * DW], F32).ap()
    route_rows = nc.dram_tensor("route_rows", [E_ROUTED, T], F32).ap()

    ctx = ExitStack()
    with ctx:
        def sb(name, cols, dt=F32, parts=P):
            return ctx.enter_context(nc.sbuf_tensor(name, [parts, cols], dt))

        def sem(name):
            return ctx.enter_context(nc.semaphore(name))

        ident = sb("ident", P)
        tie = sb("tie", EG * EG)
        x = sb("x", TT * D)
        xT_hi = sb("xT_hi", KT * T, F32R)
        xT_lo = sb("xT_lo", KT * T, F32R)
        attT = sb("attT", KT * T)
        dmask = sb("dmask", B * DW)
        beta_tok = sb("beta_tok", TT * H)
        w_raw = sb("w_raw", 2 * 3 * D)
        w_hi = sb("w_hi", 2 * 3 * D, F32R)
        w_lo = sb("w_lo", 2 * 3 * D, F32R)
        prm = sb("prm", G * 2 * PRM)
        wv_raw = sb("wv_raw", 2 * KT * PW)
        wv_hi = sb("wv_hi", 2 * KT * PW, F32R)
        wv_lo = sb("wv_lo", 2 * KT * PW, F32R)
        wo_raw = sb("wo_raw", 2 * D)
        wo_hi = sb("wo_hi", 2 * 2 * D, F32R)
        wo_lo = sb("wo_lo", 2 * 2 * D, F32R)
        obet = sb("obet", B * DW)
        raw = sb("raw", 2 * T)
        tap0 = sb("tap0", 2 * T)
        conv = sb("conv", 2 * T)
        tok = sb("tok", 2 * T)
        qk = sb("qk", 2 * T)
        gate = sb("gate", G * T)
        decay = sb("decay", B * DW)
        probs = sb("probs", B * DW)
        gated = sb("gated", T)
        gated_hi = sb("gated_hi", G * T, F32R)
        gated_lo = sb("gated_lo", G * T, F32R)
        values = sb("values", 2 * TT * PW)
        stats = sb("stats", 16 * 6)
        rstd = sb("rstd", 16)
        nmr = sb("nmr", 16)
        s_sum, s_dif, s_var, s_y, s_t = (sb(f"nw{i}", 16) for i in range(5))
        small = sb("small", 3 * TT)
        xT = qk
        ctxT = raw[:, 0:T]
        xw = raw[:, T:T + 2 * P]
        qctx, kctx = conv[:, 0:T], conv[:, T:2 * T]
        att = tok
        x_norm = values[:, 0:TT * D]
        wb = gate[:, 0:KT * H]
        bb = gate[0:H, 64:65]
        xb = gate[:, 66:68]
        betaT = gate[0:H, 3 * T:4 * T]
        obetT = gate[0:H, T:T + B * DW]
        rw = obet[:, 0:KT * H]
        rb = obet[:, 64:64 + H]
        score = obet[:, 128:256]
        choice = obet[:, 256:384]
        masked = obet[:, 384:512]
        weight = obet[:, 640:768]
        gpair = obet[:, 768:768 + 6 * TT * EG]
        gmask = obet[:, 960:960 + TT * EG]
        denom = obet[:, 992:992 + TT]
        more, same, before, tile_start = (raw[:, i * RT:(i + 1) * RT] for i in range(4))
        top8 = raw[:, 4 * RT:4 * RT + 8 * TT]
        rw_hi, rw_lo = wv_hi[:, 0:KT * H], wv_lo[:, 0:KT * H]
        routeT = gate[0:E_ROUTED, T:2 * T]
        scoreT = gate[0:E_ROUTED, 2 * T:3 * T]
        wbc = tap0[:, :]
        silu_g = tok
        prod = conv
        act_w = gate
        act_hi, act_lo = gated_hi[:, 0:T], gated_lo[:, 0:T]
        wb_hi, wb_lo = act_hi[:, 0:KT * H], act_lo[:, 0:KT * H]

        bank = [ctx.enter_context(nc.psum_tensor(f"bank{i}", [P, N], F32)) for i in range(8)]
        a_ring, t_ring, c_ring = bank[0:2], bank[2:6], bank[6:8]
        e_ring, y_acc = bank[0:4], bank[4:8]

        ld = {n: sem("ld_" + n) for n in
              ("const", "tie", "ctx", "beta", "router", "obet", "wo", "obet_rows", "route_rows", "out")}
        ld_x = [sem(f"ld_x{i}") for i in range(NCH)]
        ld_w = [sem(f"ld_w{i}") for i in range(2)]
        ld_prm = [sem(f"ld_prm{i}") for i in range(G)]
        ld_wv = [sem(f"ld_wv{i}") for i in range(2)]
        ld_route = [sem(f"ld_route{i}") for i in range(2)]
        a_full, a_drained = sem("a_full"), sem("a_drained")
        t_full, t_drained = sem("t_full"), sem("t_drained")
        c_full, c_drained = sem("c_full"), sem("c_drained")
        w_hi_ready, w_lo_ready = sem("w_hi_ready"), sem("w_lo_ready")
        wv_hi_ready, wv_lo_ready = sem("wv_hi_ready"), sem("wv_lo_ready")
        down_hi_ready, down_lo_ready = sem("down_hi_ready"), sem("down_lo_ready")
        wo_hi_ready, wo_lo_ready = sem("wo_hi_ready"), sem("wo_lo_ready")
        gated_hi_ready, gated_lo_ready = sem("gated_hi_ready"), sem("gated_lo_ready")
        p_full, p_added = sem("p_full"), sem("p_added")
        taps_done, conv_done, silu_done = sem("taps_done"), sem("conv_done"), sem("silu_done")
        rstd_ready = sem("rstd_ready")
        decay_ready = sem("decay_ready")
        dve_step = sem("dve_step")
        ln_rstd, ln_norm_act, ln_norm_dve = sem("ln_rstd"), sem("ln_norm_act"), sem("ln_norm_dve")
        small_split = sem("small_split")
        ln_full, ln_out, ln_split = sem("ln_full"), sem("ln_out"), sem("ln_split")
        x_qk_full, x_qk_ready = sem("x_qk_full"), sem("x_qk_ready")
        x_energy, x_max, x_exp = sem("x_energy"), sem("x_max"), sem("x_exp")
        x_soft, x_attT_full, x_attT_ready = sem("x_soft"), sem("x_attT_full"), sem("x_attT_ready")
        x_mix_full, x_mixed = sem("x_mix_full"), sem("x_mixed")
        b_full, b_ready, b_tok_full, b_tok_ready = (
            sem("b_full"), sem("b_ready"), sem("b_tok_full"), sem("b_tok_ready"))
        b_lo_ready, r_lo_ready = sem("b_lo_ready"), sem("r_lo_ready")
        obet_ready, dmask_ready = sem("obet_ready"), sem("dmask_ready")
        r_full, r_score = sem("r_full"), sem("r_score")
        r_tok_full, r_tok_ready = sem("r_tok_full"), sem("r_tok_ready")
        r_ready, r_tr_full, r_tr_ready = sem("r_ready"), sem("r_tr_full"), sem("r_tr_ready")
        ones_ready = sem("ones_ready")
        e_full, g_silu, u_prod = sem("e_full"), sem("g_silu"), sem("u_prod")
        e_weighted, e_hi, e_lo = sem("e_weighted"), sem("e_hi"), sem("e_lo")
        e_down = sem("e_down")
        y_full, y_added = sem("y_full"), sem("y_added")

        block = ctx.enter_context(nc.Block())

        @block.sync
        def _(sp):
            sp.dma_start(ctxT, ctx_in).then_inc(ld["ctx"], 16)
            sp.dma_start(xw, xw_in).then_inc(ld["ctx"], 16)
            sp.dma_start(xb, xb_in).then_inc(ld["ctx"], 16)
            for c in range(NCH):
                sp.dma_start(x[:, c * T:(c + 1) * T], x_in[:, c * T:(c + 1) * T]).then_inc(ld_x[c], 16)
            sp.dma_start(ident[:, :], ident_in).then_inc(ld["const"], 16)
            sp.dma_start(wb, wb_in).then_inc(ld["beta"], 16)
            sp.dma_start(bb, bb_in).then_inc(ld["beta"], 16)

            def load_weights(g, k):
                s = k % 2
                if not (isinstance(g, int) and G * g + k < 2):
                    sp.wait_ge(w_hi_ready, units(g, k, 1, -1))
                    sp.wait_ge(w_lo_ready, units(g, k, 1, -1))
                n = G * g + k
                sp.dma_start(w_raw[:, s * 3 * D:(s + 1) * 3 * D],
                             w_in[bass.ds(n, 1), :, :].rearrange("a p c -> (a p) c")).then_inc(ld_w[s], 16)

            def load_params(g, k):
                s = k % G
                if not (isinstance(g, int) and G * g + k < G):
                    sp.wait_ge(t_drained, units(g, k - G + 1, 8))
                n = G * g + k
                sp.dma_start(prm[:, s * 2 * PRM:(s + 1) * 2 * PRM],
                             prm_in[bass.ds(n, 1), :, :].rearrange("a p c -> (a p) c")).then_inc(ld_prm[s], 16)

            def load_obet(g, k):
                if not (isinstance(g, int) and G * g + k < 1):
                    sp.wait_ge(decay_ready, units(g, k, 1))
                n = G * g + k
                sp.dma_start(obet[:, :], obet_rows[bass.ds(n, 1), :].broadcast_to([P, B * DW])
                             ).then_inc(ld["obet"], 16)

            def load_values(pair, s):
                sp.dma_start(wv_raw[:, s * N:(s + 1) * N],
                             wv_in[bass.ds(pair, 1), :, :].rearrange("a p c -> (a p) c")).then_inc(ld_wv[s], 16)

            def load_projection(pair):
                if not (isinstance(pair, int) and pair == 0):
                    sp.wait_ge(wo_lo_ready, pair)
                sp.dma_start(wo_raw[:, :], wo_in[bass.ds(pair, 1), :, :].rearrange("a p c -> (a p) c")
                             ).then_inc(ld["wo"], 16)

            load_weights(0, 0)
            load_params(0, 0)
            load_values(0, 0)
            load_weights(0, 1)
            load_params(0, 1)
            sp.dma_start(tie[:, :], tie_in).then_inc(ld["tie"], 16)
            load_weights(0, 2)
            sp.wait_ge(obet_ready, 2)
            sp.dma_start(obet_rows, obetT).then_inc(ld["obet_rows"], 16)
            sp.wait_ge(ld["obet_rows"], 16)
            load_obet(0, 0)

            def step(g, k):
                n = G * g + k if isinstance(g, int) else None
                if n is None or n + 2 < H:
                    load_params(g, k + 2)
                if k % 2 == 0:
                    if n is None or n + 2 < H:
                        if n != 0:
                            sp.wait_ge(wv_lo_ready, g * 2 + k // 2)
                        load_values(g * 2 + (k // 2 + 1), (k // 2 + 1) % 2)
                    load_projection(g * 2 + k // 2)
                load_weights(g, k + 3)
                if n is None or n + 1 < H:
                    load_obet(g, k + 1)

            step(0, 0)
            step(0, 1)
            with sp.Fori(0, NG - 1) as g:
                for k in (2, 3):
                    step(g, k)
                for k in (0, 1):
                    step(g + 1, k)
            for k in (2, 3):
                step(NG - 1, k)

            def load_expert(n, s):
                m = n + (H - 1)
                sp.dma_start(w_raw[:, s * 3 * D:(s + 1) * 3 * D],
                             w_in[bass.ds(m, 1), :, :].rearrange("a p c -> (a p) c")).then_inc(ld_w[s], 16)

            def expert_split(n):
                sp.wait_ge(down_lo_ready, n - E_SHARED)

            sp.wait_ge(decay_ready, H)
            sp.dma_start(rw, rw_in).then_inc(ld["router"], 16)
            sp.dma_start(rb, rb_in.broadcast_to([P, E_ROUTED])).then_inc(ld["router"], 16)
            sp.wait_ge(w_lo_ready, H + 2)
            load_expert(4, 1)
            sp.wait_ge(r_tr_ready, NCH)
            sp.dma_start(route_rows, routeT).then_inc(ld["route_rows"], 16)
            sp.wait_ge(ld["route_rows"], 16)

            def load_route(e, s, before):
                sp.wait_ge(e_weighted, before)
                sp.dma_start(wbc[:, s * T:(s + 1) * T],
                             route_rows[bass.ds(e, 1), :].broadcast_to([P, T])).then_inc(ld_route[s], 16)

            for s in range(2):
                load_route(s, s, NCH * (s + 1))
            with sp.Fori(0, E_ROUTED // 2 - 1) as r:
                for s in range(2):
                    expert_split(r * 2 + (3 + s))
                    load_expert(r * 2 + (5 + s), s)
                    load_route(r * 2 + (2 + s), s, r * (2 * NCH) + NCH * (3 + s))
            for u in range(TT // 2):
                sp.wait_ge(y_added, u + 1)
                sp.dma_start(out[:, u * N:(u + 1) * N], x[:, u * N:(u + 1) * N]).then_inc(ld["out"], 16)
            sp.wait_ge(ld["out"], 16 * (TT // 2))

        @block.gpsimd
        def _(pool):
            def split_low(g, k):
                s = k % 2
                pool.wait_ge(w_hi_ready, units(g, k, 1, 1))
                if not (isinstance(g, int) and G * g + k < 2):
                    pool.wait_ge(a_full, units(g, k - 1, 6))
                w = slice(s * 3 * D, (s + 1) * 3 * D)
                nc.gpsimd.tensor_tensor(w_lo[:, w], w_raw[:, w], w_hi[:, w].bitcast(F32),
                                        ALU.subtract).then_inc(w_lo_ready, 1)

            def low_values(pair, s):
                w = slice(s * N, (s + 1) * N)
                pool.wait_ge(wv_hi_ready, pair + 1)
                nc.gpsimd.tensor_tensor(wv_lo[:, w], wv_raw[:, w], wv_hi[:, w].bitcast(F32),
                                        ALU.subtract).then_inc(wv_lo_ready, 1)

            def last_tap(g, k):
                for u in range(2 * NCH):
                    pool.wait_ge(taps_done, units(g, k, 4, u + 1))
                    y = conv[:, u * N:(u + 1) * N].rearrange("p (b t) -> p b t", b=BPC)[:, :, TAPS - 1:L]
                    r = tap0[:, u * N:(u + 1) * N].rearrange("p (b t) -> p b t", b=BPC)[:, :, 0:L - TAPS + 1]
                    nc.gpsimd.tensor_tensor(y, r, y, ALU.add).then_inc(conv_done, 1)

            def gated_low(g, k, c):
                cc = slice(k % G * T + c * N, k % G * T + (c + 1) * N)
                pool.wait_ge(gated_hi_ready, units(g, k, NCH, c + 1))
                nc.gpsimd.tensor_tensor(gated_lo[:, cc], gated[:, c * N:(c + 1) * N], gated_hi[:, cc].bitcast(F32),
                                        ALU.subtract).then_inc(gated_lo_ready, 1)

            def low_projection(pair, s):
                w = slice(s * 2 * D, (s + 1) * 2 * D)
                pool.wait_ge(wo_hi_ready, pair + 1)
                nc.gpsimd.tensor_tensor(wo_lo[:, w], wo_raw[:, :], wo_hi[:, w].bitcast(F32),
                                        ALU.subtract).then_inc(wo_lo_ready, 1)

            split_low(0, 0)
            low_values(0, 0)
            split_low(0, 1)
            last_tap(0, 0)
            split_low(0, 2)
            last_tap(0, 1)

            def step(g, k):
                n = G * g + k if isinstance(g, int) else None
                if k % 2:
                    low_projection(g * 2 + k // 2, k // 2)
                elif n is None or n + 2 < H:
                    low_values(g * 2 + (k // 2 + 1), (k // 2 + 1) % 2)
                if n is None or n < H - 1:
                    split_low(*head(g, k + 3))
                if n != 0:
                    gated_low(g, k - 1, 1)
                if n is None or n + 2 < H:
                    last_tap(*head(g, k + 2))
                if n is None or n < H - 1:
                    gated_low(g, k, 0)

            step(0, 0)
            step(0, 1)
            with pool.Fori(0, NG - 1) as g:
                for k in (2, 3):
                    step(g, k)
                for k in (0, 1):
                    step(g + 1, k)
            for k in (2, 3):
                step(NG - 1, k)

            def gate_up_low(n, s):
                w = slice(s * 3 * D, s * 3 * D + 2 * D)
                pool.wait_ge(w_hi_ready, n + H)
                nc.gpsimd.tensor_tensor(w_lo[:, w], w_raw[:, w], w_hi[:, w].bitcast(F32),
                                        ALU.subtract).then_inc(w_lo_ready, 1)

            def down_low(n, s):
                w = slice(s * 3 * D + 2 * D, (s + 1) * 3 * D)
                pool.wait_ge(down_hi_ready, n - E_SHARED)
                nc.gpsimd.tensor_tensor(w_lo[:, w], w_raw[:, w], w_hi[:, w].bitcast(F32),
                                        ALU.subtract).then_inc(down_lo_ready, 1)

            def weigh(n, s, first):
                for c in range(NCH):
                    pool.wait_ge(u_prod, (n - 1) * NCH + c + 1)
                    if not first:
                        pool.wait_ge(e_hi, (n - 2) * NCH + c + 1)
                        pool.wait_ge(e_lo, (n - 2) * NCH + c + 1)
                    cc = slice(c * N, (c + 1) * N)
                    nc.gpsimd.tensor_tensor(act_w[:, cc], prod[:, cc], wbc[:, s * T + c * N:s * T + (c + 1) * N],
                                            ALU.mult).then_inc(e_weighted, 1)

            pool.wait_ge(p_added, TT // 2)
            nc.gpsimd.memset(wbc, 1.0).then_inc(ones_ready, 1)
            pool.wait_ge(ones_ready, 1)
            weigh(1, 0, True)
            gate_up_low(3, 0)
            weigh(2, 1, False)
            gate_up_low(4, 1)
            down_low(3, 0)

            def step(n, s, left=2):
                pool.wait_ge(ld_route[s], (n - 1 - s) * 8)
                weigh(n, s, False)
                if left > 1:
                    gate_up_low(n + 2, s)
                if left > 0:
                    down_low(n + 1, 1 - s)

            with pool.Fori(0, E_ROUTED // 2 - 1) as r:
                for s in range(2):
                    step(r * 2 + (3 + s), s)
            step(E_ALL - 1, 0, 1)
            step(E_ALL, 1, 0)

        @block.scalar
        def _(act):
            def half_norm(i, c):
                act.wait_ge(ln_rstd, NCH * i + c + 1)
                for t in (G * c, G * c + 1):
                    nc.scalar.activation(x_norm[:, t * D:(t + 1) * D], x[:, t * D:(t + 1) * D],
                                         ACT.Identity, scale=rstd[:, t:t + 1],
                                         bias=nmr[:, t:t + 1]).then_inc(ln_norm_act, 1)

            def half_out(i, c, dst):
                for kt in range(KT):
                    act.wait_ge(ln_full, (NCH * i + c) * KT + kt + 1)
                    nc.scalar.activation(dst[:, kt * T + c * N:kt * T + (c + 1) * N],
                                         bank[2 * c + kt][:, :], ACT.Copy).then_inc(ln_out, 1)

            act.wait_ge(ld["ctx"], 48)
            for u in range(2 * NCH):
                act.wait_ge(x_qk_full, u + 1)
                nc.scalar.activation(conv[:, u * N:(u + 1) * N], bank[4 + u][:, :], ACT.Identity,
                                     bias=xb[:, u // NCH:u // NCH + 1]).then_inc(x_qk_ready, 1)
            act.wait_ge(ld["beta"], 32)
            nc.scalar.activation(wb_hi, wb, ACT.Copy).then_inc(small_split, 1)
            for c in range(NCH):
                half_norm(0, c)
            for c in range(NCH):
                half_out(0, c, xT_hi)

            def high(g, k):
                s = k % 2
                w = slice(s * 3 * D, (s + 1) * 3 * D)
                act.wait_ge(ld_w[s], uses(g, k, 2) * 16)
                if not (isinstance(g, int) and G * g + k < 2):
                    act.wait_ge(a_full, units(g, k - 1, 6))
                nc.scalar.activation(w_hi[:, w], w_raw[:, w], ACT.Copy).then_inc(w_hi_ready, 1)

            def high_values(g, k):
                s = (k // 2 + 1) % 2
                w = slice(s * N, (s + 1) * N)
                act.wait_ge(ld_wv[s], g * 16 + (16 if k == 0 else 32))
                if not (isinstance(g, int) and G * g + k == 0):
                    act.wait_ge(c_full, c_scores(g, k - 2) + B)
                nc.scalar.activation(wv_hi[:, w], wv_raw[:, w], ACT.Copy).then_inc(wv_hi_ready, 1)

            def raw_qk(g, k, some=range(2 * NCH)):
                act.wait_ge(ld_prm[k % G], uses(g, k, G) * 16)
                for u in some:
                    act.wait_ge(a_full, units(g, k, 6, u + 1))
                    if not (isinstance(g, int) and G * g + k < 1):
                        act.wait_ge(conv_done, units(g, k - 1, 4, u + 1))
                    o = (k % G) * 2 * PRM + (u // NCH) * PRM
                    nc.scalar.activation(raw[:, u * N:(u + 1) * N], a_ring[u % 2][:, :], ACT.Copy)
                    nc.scalar.activation(tap0[:, u * N:(u + 1) * N], a_ring[u % 2][:, :], ACT.Copy,
                                         scale=prm[:, o:o + 1]).then_inc(a_drained, 1)

            def gates(g, k):
                for c in range(NCH):
                    act.wait_ge(a_full, units(g, k, 6, 4 + c + 1))
                    if not (isinstance(g, int) and G * g + k < G - 1):
                        act.wait_ge(c_full, c_scores(g, k - G + 1) + B)
                    nc.scalar.activation(gate[:, (k % G) * T + c * N:(k % G) * T + (c + 1) * N],
                                         a_ring[c % 2][:, :], ACT.Silu).then_inc(a_drained, 1)

            def silu(g, k, part):
                for u in (2 * part, 2 * part + 1):
                    act.wait_ge(conv_done, units(g, k, 4, u + 1))
                    c = conv[:, u * N:(u + 1) * N]
                    nc.scalar.activation(c, c, ACT.Silu).then_inc(silu_done, 1)

            def normalise(g, k):
                act.wait_ge(rstd_ready, units(g, k, 1, 1))
                for u in range(2 * NCH):
                    act.wait_ge(t_full, units(g, k, 8, u + 1))
                    if not (isinstance(g, int) and G * g + k < 1):
                        act.wait_ge(t_full, units(g, k - 1, 8, 4 + u + 1))
                    for i in range(G):
                        t = u * G + i
                        ins = nc.scalar.activation(tok[:, t * P:(t + 1) * P], t_ring[u][:, i * P:(i + 1) * P],
                                                   ACT.Identity, scale=rstd[:, t:t + 1], bias=nmr[:, t:t + 1])
                    ins.then_inc(t_drained, 1)

            def affine(g, k):
                for u in range(2 * NCH):
                    o = (k % G) * 2 * PRM + (u // NCH) * PRM + TAPS + 1
                    act.wait_ge(t_full, units(g, k, 8, 4 + u + 1))
                    if not (isinstance(g, int) and G * g + k < 1):
                        act.wait_ge(c_full, c_scores(g, k - 1) + B)
                    nc.scalar.activation(qk[:, u * N:(u + 1) * N], t_ring[u][:, :], ACT.Identity,
                                         scale=prm[:, o:o + 1], bias=prm[:, o + 1:o + 2]).then_inc(t_drained, 1)

            def gated_high(g, k, c):
                cc = slice(k % G * T + c * N, k % G * T + (c + 1) * N)
                act.wait_ge(c_drained, c_outputs(g, k) + (c + 1))
                nc.scalar.activation(gated_hi[:, cc], gated[:, c * N:(c + 1) * N],
                                     ACT.Copy).then_inc(gated_hi_ready, 1)

            def high_projection(pair, s):
                w = slice(s * 2 * D, (s + 1) * 2 * D)
                act.wait_ge(ld["wo"], pair * 16 + 16)
                nc.scalar.activation(wo_hi[:, w], wo_raw[:, :], ACT.Copy).then_inc(wo_hi_ready, 1)

            high(0, 0)
            for t in range(TT):
                act.wait_ge(x_max, 2 * (t // 2) + 2)
                nc.scalar.activation(att[:, t * L:(t + 1) * L],
                                     bank[4 + t // 2][:, (t % 2) * L:(t % 2 + 1) * L], ACT.Exp,
                                     bias=small[:, t:t + 1],
                                     accum_out=small[:, TT + t:TT + t + 1]).then_inc(x_exp, 1)
            raw_qk(0, 0, (0, 1))
            for c in range(NCH):
                act.wait_ge(b_full, c + 1)
                nc.scalar.activation(betaT[:, c * N:(c + 1) * N], bank[2 + c][0:H, :], ACT.Sigmoid,
                                     bias=bb).then_inc(b_ready, 1)
            raw_qk(0, 0, (2, 3))
            act.wait_ge(ld_wv[0], 16)
            nc.scalar.activation(wv_hi[:, 0:N], wv_raw[:, 0:N], ACT.Copy).then_inc(wv_hi_ready, 1)
            high(0, 1)
            gates(0, 0)
            silu(0, 0, 0)
            silu(0, 0, 1)
            high(0, 2)
            raw_qk(0, 1)
            normalise(0, 0)
            act.wait_ge(ld["obet_rows"], 16)
            gates(0, 1)
            silu(0, 1, 0)

            def step(g, k):
                n = G * g + k if isinstance(g, int) else None
                if k % 2:
                    high_projection(g * 2 + k // 2, k // 2)
                affine(g, k)
                if n is None or n + 1 < H:
                    if n is None or n + 2 < H:
                        raw_qk(*head(g, k + 2), (0,))
                    silu(*head(g, k + 1), 1)
                if n is None or n + 2 < H:
                    raw_qk(*head(g, k + 2), (1, 2, 3))
                    if k % 2 == 0:
                        high_values(g, k)
                if n is None or n < H - 1:
                    high(*head(g, k + 3))
                if n != 0:
                    gated_high(g, k - 1, 1)
                if n is None or n + 1 < H:
                    normalise(*head(g, k + 1))
                if n is None or n + 2 < H:
                    gates(*head(g, k + 2))
                    silu(*head(g, k + 2), 0)
                if n is None or n < H - 1:
                    gated_high(g, k, 0)

            step(0, 0)
            step(0, 1)
            with act.Fori(0, NG - 1) as g:
                for k in (2, 3):
                    step(g, k)
                for k in (0, 1):
                    step(g + 1, k)
            for k in (2, 3):
                step(NG - 1, k)

            def gate_up_high(n, s):
                act.wait_ge(ld_w[s], n * 8 + (8 * (H - 1 - s) + 16))
                act.wait_ge(e_full, n * 4 - 8)
                w = slice(s * 3 * D, s * 3 * D + 2 * D)
                nc.scalar.activation(w_hi[:, w], w_raw[:, w], ACT.Copy).then_inc(w_hi_ready, 1)

            def down_high(n, s):
                act.wait_ge(ld_w[s], n * 8 + (8 * (H - 1 - s) + 16))
                act.wait_ge(e_down, n - 2)
                w = slice(s * 3 * D + 2 * D, (s + 1) * 3 * D)
                nc.scalar.activation(w_hi[:, w], w_raw[:, w], ACT.Copy).then_inc(down_hi_ready, 1)

            def gate_silu(n, first):
                for c in range(NCH):
                    act.wait_ge(e_full, (n - 1) * 4 + 2 * c + 1)
                    if not first:
                        act.wait_ge(u_prod, (n - 2) * NCH + c + 1)
                    cc = slice(c * N, (c + 1) * N)
                    nc.scalar.activation(silu_g[:, cc], e_ring[2 * c][:, :], ACT.Silu).then_inc(g_silu, 1)

            def act_high(n, first):
                for c in range(NCH):
                    act.wait_ge(e_weighted, (n - 1) * NCH + c + 1)
                    if not first:
                        act.wait_ge(e_down, n - 1)
                    cc = slice(c * N, (c + 1) * N)
                    nc.scalar.activation(act_hi[:, cc], act_w[:, cc], ACT.Copy).then_inc(e_hi, 1)

            act.wait_ge(ld["router"], 32)
            nc.scalar.activation(rw_hi, rw, ACT.Copy).then_inc(small_split, 1)
            for i, dst in ((1, xT), (2, xT_hi)):
                for c in range(NCH):
                    half_norm(i, c)
                for c in range(NCH):
                    half_out(i, c, dst)
            for c in range(NCH):
                act.wait_ge(r_full, c + 1)
                nc.scalar.activation(scoreT[:, c * N:(c + 1) * N], bank[4 + c][0:E_ROUTED, :],
                                     ACT.Sigmoid).then_inc(r_score, 1)
            act.wait_ge(r_tok_full, 1)
            nc.scalar.activation(score, bank[4][:, 0:TT * E_ROUTED], ACT.Copy).then_inc(r_tok_ready, 1)
            gate_silu(1, True)
            gate_up_high(3, 0)
            act_high(1, True)
            gate_silu(2, False)
            gate_up_high(4, 1)
            act_high(2, False)
            down_high(3, 0)

            for c in range(NCH):
                act.wait_ge(r_tr_full, c + 1)
                nc.scalar.activation(routeT[:, c * N:(c + 1) * N], e_ring[2 + c][0:E_ROUTED, :],
                                     ACT.Copy).then_inc(r_tr_ready, 1)

            def step(n, s, left=2):
                gate_silu(n, False)
                if left > 1:
                    gate_up_high(n + 2, s)
                act_high(n, False)
                if left > 0:
                    down_high(n + 1, 1 - s)

            with act.Fori(0, E_ROUTED // 2 - 1) as r:
                for s in range(2):
                    step(r * 2 + (3 + s), s)
            step(E_ALL - 1, 0, 1)
            step(E_ALL, 1, 0)

        @block.vector
        def _(dve):
            steps = Steps(dve, dve_step, body=G * 23)

            def norm_factors(tiles, width):
                st = stats[:, 0:6 * tiles].rearrange("p (t s) -> p s t", s=6)
                me, m2e, mo, m2o = st[:, 1, :], st[:, 2, :], st[:, 4, :], st[:, 5, :]
                c = slice(0, tiles)
                dif = steps.did(nc.vector.tensor_tensor(s_dif[:, c], me, mo, ALU.subtract))
                nc.vector.tensor_tensor(s_sum[:, c], me, mo, ALU.add)
                nc.vector.tensor_tensor(s_var[:, c], m2e, m2o, ALU.add)
                steps.after(dif)
                a = steps.did(nc.vector.tensor_tensor(s_t[:, c], s_dif[:, c], s_dif[:, c], ALU.mult))
                steps.after(a)
                a = steps.did(nc.vector.scalar_tensor_tensor(
                    out=s_var[:, c], in0=s_t[:, c], scalar=width / 4.0, in1=s_var[:, c],
                    op0=ALU.mult, op1=ALU.add))
                steps.after(a)
                a = steps.did(nc.vector.tensor_scalar(s_var[:, c], s_var[:, c], 1.0 / width, EPS,
                                                      ALU.mult, ALU.add))
                steps.after(a)
                a = steps.did(nc.vector.tensor_scalar(
                    s_y[:, c].bitcast(I32), s_var[:, c].bitcast(I32), -0.5, RSQRT_SEED,
                    ALU.mult, ALU.add))
                for i in range(3):
                    steps.after(a)
                    a = steps.did(nc.vector.tensor_tensor(s_t[:, c], s_y[:, c], s_y[:, c], ALU.mult))
                    steps.after(a)
                    a = steps.did(nc.vector.scalar_tensor_tensor(
                        out=s_t[:, c], in0=s_t[:, c], scalar=-0.5, in1=s_var[:, c],
                        op0=ALU.mult, op1=ALU.mult))
                    steps.after(a)
                    y = rstd if i == 2 else s_y
                    a = steps.did(nc.vector.scalar_tensor_tensor(
                        out=y[:, c], in0=s_t[:, c], scalar=1.5, in1=s_y[:, c],
                        op0=ALU.add, op1=ALU.mult))
                steps.after(a)
                return nc.vector.scalar_tensor_tensor(
                    out=nmr[:, c], in0=s_sum[:, c], scalar=-0.5, in1=rstd[:, c],
                    op0=ALU.mult, op1=ALU.mult)

            def x_stats(t):
                return nc.vector.bn_stats(stats[:, 6 * t:6 * t + 6], x[:, t * D:(t + 1) * D])

            def half_norm(i, c):
                dve.wait_ge(ln_rstd, NCH * i + c + 1)
                for t in (G * c + 2, G * c + 3):
                    nc.vector.tensor_scalar(x_norm[:, t * D:(t + 1) * D], x[:, t * D:(t + 1) * D],
                                            rstd[:, t:t + 1], nmr[:, t:t + 1], ALU.mult,
                                            ALU.add).then_inc(ln_norm_dve, 1)

            def half_low(i, c):
                for kt in range(KT):
                    cc = slice(kt * T + c * N, kt * T + (c + 1) * N)
                    dve.wait_ge(ln_out, (NCH * i + c) * KT + kt + 1)
                    nc.vector.tensor_tensor(xT_lo[:, cc], bank[2 * c + kt][:, :], xT_hi[:, cc].bitcast(F32),
                                            ALU.subtract).then_inc(ln_split, 1)

            obet_zero = steps.did(nc.vector.memset(obetT, 0.0))
            a = steps.did(nc.vector.memset(dmask[:, :], 0.0))
            for t in range(TT):
                dve.wait_ge(ld_x[t // G], 16)
                ins = x_stats(t)
            steps.after(steps.did(ins))
            norm_factors(TT, D).then_inc(ln_rstd, NCH)
            for c in range(NCH):
                half_norm(0, c)
            dve.wait_ge(ld["const"], 16)
            steps.after(a)
            dm = dmask[:, :].rearrange("p (b c) -> p b c", b=B)
            for b in range(B):
                nc.vector.tensor_copy(dm[:, b, 0:P], ident[:, :])
                ins = nc.vector.tensor_copy(dm[:, b, L:L + P], ident[:, :])
            ins.then_inc(dmask_ready, 1)
            dve.wait_ge(small_split, 1)
            nc.vector.tensor_tensor(wb_lo, wb, wb_hi.bitcast(F32), ALU.subtract).then_inc(b_lo_ready, 1)
            for c in range(NCH):
                half_low(0, c)
            for t in range(TT):
                dve.wait_ge(x_energy, t // 2 + 1)
                nc.vector.tensor_reduce(small[:, t:t + 1], bank[4 + t // 2][:, (t % 2) * L:(t % 2 + 1) * L],
                                        op=ALU.max, axis=AX.X, negate=True).then_inc(x_max, 1)
            dve.wait_ge(x_exp, TT)
            a = steps.did(nc.vector.reciprocal(small[:, 2 * TT:3 * TT], small[:, TT:2 * TT]))
            steps.after(a)
            for t in range(TT):
                nc.vector.tensor_scalar(att[:, t * L:(t + 1) * L], att[:, t * L:(t + 1) * L],
                                        small[:, 2 * TT + t:2 * TT + t + 1], None, ALU.mult).then_inc(x_soft, 1)
            bt_v = beta_tok[:, :].rearrange("p (t h) -> p t h", t=TT)

            def scale_values(at, h, s, units):
                for i, u in enumerate(units):
                    dve.wait_ge(c_full, at + (i + 1))
                    o = s * TT * PW + u * N
                    nc.vector.tensor_tensor(
                        values[:, o:o + N].rearrange("p (t h c) -> p t h c", t=2, h=2),
                        c_ring[i % 2][:, :].rearrange("p (t h c) -> p t h c", t=2, h=2),
                        bt_v[:, 2 * u:2 * u + 2, bass.ds(h, 2)].unsqueeze(3).broadcast_to([P, 2, 2, P]),
                        ALU.mult).then_inc(c_drained, 1)

            def head_decay(g, k):
                dve.wait_ge(ld["obet"], units(g, k, 16, 16))
                if not (isinstance(g, int) and G * g + k < 1):
                    dve.wait_ge(c_drained, c_scores(g, k - 1) + B)
                nc.vector.tensor_tensor_scan(decay[:, :], obet[:, :],
                                             dmask[:, :], 0.0, ALU.mult, ALU.add).then_inc(decay_ready, 1)

            def head_factors(g, k):
                for u in range(2 * NCH):
                    dve.wait_ge(t_full, units(g, k, 8, u + 1))
                    for i in range(G):
                        t = u * G + i
                        ins = nc.vector.bn_stats(stats[:, 6 * t:6 * t + 6], t_ring[u][:, i * P:(i + 1) * P])
                steps.after(steps.did(ins))
                if not (isinstance(g, int) and G * g + k < 1):
                    dve.wait_ge(t_drained, units(g, k - 1, 8, 4))
                norm_factors(2 * TT, P).then_inc(rstd_ready, 1)

            tapped = {}

            def taps(g, k, part, backs=range(TAPS - 1), only=None):
                o = (k % G) * 2 * PRM + part * PRM
                if part == 0 and 0 in backs:
                    dve.wait_ge(ld_prm[k % G], uses(g, k, G) * 16)
                for back in backs:
                    for u in ((2 * part, 2 * part + 1) if only is None else (only,)):
                        if back == 0:
                            dve.wait_ge(a_drained, units(g, k, 6, u + 1))
                            if not (isinstance(g, int) and G * g + k < 1):
                                dve.wait_ge(t_full, units(g, k - 1, 8, u + 1))
                            tapped[u] = steps.did(nc.vector.tensor_scalar(
                                conv[:, u * N:(u + 1) * N], raw[:, u * N:(u + 1) * N],
                                prm[:, o + 3:o + 4], prm[:, o + 4:o + 5], ALU.mult, ALU.add))
                            continue
                        y = conv[:, u * N:(u + 1) * N].rearrange("p (b t) -> p b t", b=BPC)[:, :, back:L]
                        r = raw[:, u * N:(u + 1) * N].rearrange("p (b t) -> p b t", b=BPC)[:, :, 0:L - back]
                        steps.after(tapped[u])
                        ins = nc.vector.scalar_tensor_tensor(
                            out=y, in0=r, scalar=prm[:, o + 3 - back:o + 4 - back], in1=y,
                            op0=ALU.mult, op1=ALU.add)
                        if back == TAPS - 2:
                            ins.then_inc(taps_done, 1)
                        else:
                            tapped[u] = steps.did(ins)

            def decayed(g, k, part):
                dve.wait_ge(decay_ready, units(g, k, 1, 1))
                for b in (2 * part, 2 * part + 1):
                    dve.wait_ge(c_full, c_scores(g, k) + (b + 1))
                    bb_ = slice(b * DW, (b + 1) * DW)
                    nc.vector.tensor_tensor(probs[:, bb_], c_ring[b % 2][:, 0:DW], decay[:, bb_],
                                            ALU.mult).then_inc(c_drained, 1)

            def gated_out(g, k, c):
                dve.wait_ge(a_drained, units(g, k, 6, 6))
                dve.wait_ge(c_full, c_outputs(g, k) + (c + 1))
                if not (isinstance(g, int) and G * g + k < 1):
                    dve.wait_ge(gated_lo_ready, units(g, k, NCH, c - 1))
                nc.vector.tensor_tensor(gated[:, c * N:(c + 1) * N], c_ring[c % 2][:, :],
                                        gate[:, k * T + c * N:k * T + (c + 1) * N],
                                        ALU.mult).then_inc(c_drained, 1)

            def add_projection(at, i, u):
                dve.wait_ge(c_full, at + (i + 1))
                xs = x[:, u * N:(u + 1) * N]
                nc.vector.tensor_tensor(xs, c_ring[u % 2][:, :], xs, ALU.add).then_inc(c_drained, 1)

            taps(0, 0, 0)
            dve.wait_ge(b_ready, NCH)
            steps.after(obet_zero)
            bt = betaT.rearrange("h (b t) -> h b t", b=B)
            ob = obetT.rearrange("h (b c) -> h b c", b=B)
            nc.vector.tensor_scalar(ob[:, :, 1:L], bt[:, :, 1:L], -1.0, 1.0, ALU.mult,
                                    ALU.add).then_inc(obet_ready, 1)
            nc.vector.tensor_scalar(ob[:, :, L + 1:DW], bt[:, :, P + 1:L], -1.0, 1.0, ALU.mult,
                                    ALU.add).then_inc(obet_ready, 1)
            taps(0, 0, 1, (0, 1))
            for u in (2, 3, 0, 1):
                dve.wait_ge(x_attT_full, u + 1)
                nc.vector.tensor_copy(attT[:, u * N:(u + 1) * N], bank[4 + u][:, :]).then_inc(x_attT_ready, 1)
            dve.wait_ge(b_tok_full, 1)
            nc.vector.tensor_copy(beta_tok[:, :], bank[2][:, 0:TT * H]).then_inc(b_tok_ready, 1)
            dve.wait_ge(b_tok_ready, 1)
            taps(0, 0, 1, (2,))
            scale_values(0, 0, 0, range(V_UNITS))
            head_factors(0, 0)
            taps(0, 1, 0)
            taps(0, 1, 1)
            head_decay(0, 0)

            def step(g, k):
                n = G * g + k if isinstance(g, int) else None
                if n is None or n + 1 < H:
                    head_factors(*head(g, k + 1))
                more = n is None or n + 2 < H
                project = n is None or n > 1
                at = c_project(g, k)
                if project:
                    add_projection(at, 0, 2 * (k % 2))
                if more:
                    taps(*head(g, k + 2), 0, (0,))
                if project:
                    add_projection(at, 1, 2 * (k % 2) + 1)
                if more:
                    taps(*head(g, k + 2), 0, (1,))
                decayed(g, k, 0)
                decayed(g, k, 1)
                if more:
                    taps(*head(g, k + 2), 0, (2,))
                    scale_values(c_values(g, k), g * G + (k // 2 + 1) * 2, (k // 2 + 1) % 2,
                                 (2 * (k % 2), 2 * (k % 2) + 1))
                    taps(*head(g, k + 2), 1, (0,))
                gated_out(g, k, 0)
                if more:
                    taps(*head(g, k + 2), 1, (1,), 2)
                gated_out(g, k, 1)
                if more:
                    taps(*head(g, k + 2), 1, (2,), 2)
                    taps(*head(g, k + 2), 1, (1, 2), 3)
                if n is None or n + 1 < H:
                    head_decay(*head(g, k + 1))

            dve.wait_ge(c_drained, V_UNITS)
            step(0, 0)
            step(0, 1)
            with dve.Fori(0, NG - 1) as g:
                steps.enter(g)
                for k in (2, 3):
                    step(g, k)
                for k in (0, 1):
                    step(g + 1, k)
            steps.leave(NG - 1)
            for k in (2, 3):
                step(NG - 1, k)

            def add_and_norm(i, full, banks, drained):
                def add(u):
                    dve.wait_ge(full, u + 1)
                    xs = x[:, u * N:(u + 1) * N]
                    nc.vector.tensor_tensor(xs, banks[u][:, :], xs, ALU.add).then_inc(drained, 1)

                add(0)
                for u in range(TT // 2):
                    if u + 1 < TT // 2:
                        add(u + 1)
                    dve.wait_ge(drained, u + 1)
                    for t in (2 * u, 2 * u + 1):
                        ins = x_stats(t)
                steps.after(steps.did(ins))
                norm_factors(TT, D).then_inc(ln_rstd, NCH)
                for c in range(NCH):
                    half_norm(i, c)

            dve.wait_ge(small_split, 2)
            nc.vector.tensor_tensor(rw_lo, rw, rw_hi.bitcast(F32), ALU.subtract).then_inc(r_lo_ready, 1)
            add_and_norm(1, p_full, bank[0:4], p_added)
            add_and_norm(2, x_mix_full, bank[4:8], x_mixed)
            for c in range(NCH):
                half_low(2, c)

            def u_times(n, first=False, chunks=range(NCH)):
                for c in chunks:
                    dve.wait_ge(e_full, (n - 1) * 4 + 2 * c + 2)
                    dve.wait_ge(g_silu, (n - 1) * NCH + c + 1)
                    if not first:
                        dve.wait_ge(e_weighted, (n - 2) * NCH + c + 1)
                    cc = slice(c * N, (c + 1) * N)
                    nc.vector.tensor_tensor(prod[:, cc], e_ring[2 * c + 1][:, :], silu_g[:, cc],
                                            ALU.mult).then_inc(u_prod, 1)

            def act_low(n):
                for c in range(NCH):
                    dve.wait_ge(e_hi, (n - 1) * NCH + c + 1)
                    cc = slice(c * N, (c + 1) * N)
                    nc.vector.tensor_tensor(act_lo[:, cc], act_w[:, cc], act_hi[:, cc].bitcast(F32),
                                            ALU.subtract).then_inc(e_lo, 1)

            def by_tile(ap):
                return ap.rearrange("p (t e) -> p t e", t=TT)

            def spread(ap, n):
                return ap.unsqueeze(2).broadcast_to([P, TT, n])

            def op(*instructions):
                steps.after(steps.did(instructions[-1]))

            op(nc.vector.memset(tile_start, 1.0))
            nc.vector.memset(by_tile(tile_start)[:, :, 0:1], 0.0)
            dve.wait_ge(r_tok_ready, 1)
            dve.wait_ge(ld["router"], 32)
            dve.wait_ge(ld["tie"], 16)
            op(nc.vector.tensor_tensor(by_tile(choice), by_tile(score),
                                       rb.unsqueeze(1).broadcast_to([P, TT, E_ROUTED]), ALU.add))
            c4 = choice.rearrange("p (q e) -> p e q", e=EPG)
            hi1, lo1, hi2, lo2, top, sec = (gpair[:, i * TT * EG:(i + 1) * TT * EG] for i in range(6))
            op(nc.vector.tensor_tensor(hi1, c4[:, 0, :], c4[:, 1, :], ALU.max),
               nc.vector.tensor_tensor(lo1, c4[:, 0, :], c4[:, 1, :], ALU.min),
               nc.vector.tensor_tensor(hi2, c4[:, 2, :], c4[:, 3, :], ALU.max),
               nc.vector.tensor_tensor(lo2, c4[:, 2, :], c4[:, 3, :], ALU.min))
            op(nc.vector.tensor_tensor(top, hi1, hi2, ALU.max),
               nc.vector.tensor_tensor(sec, hi1, hi2, ALU.min),
               nc.vector.tensor_tensor(lo1, lo1, lo2, ALU.max))
            op(nc.vector.tensor_tensor(sec, sec, lo1, ALU.max))
            op(nc.vector.tensor_tensor(top, top, sec, ALU.add))

            u_times(1, True, (0,))
            v = by_tile(top)
            other = v.unsqueeze(2).broadcast_to([P, TT, EG, EG])
            own = v.unsqueeze(3).broadcast_to([P, TT, EG, EG])
            m4, s4 = (a.rearrange("p (t e f) -> p t e f", t=TT, e=EG) for a in (more, same))
            lower = tie.rearrange("p (e f) -> p e f", e=EG).unsqueeze(1).broadcast_to([P, TT, EG, EG])
            op(nc.vector.tensor_tensor(m4, other, own, ALU.is_gt),
               nc.vector.tensor_tensor(s4, other, own, ALU.is_equal))
            op(nc.vector.tensor_tensor(s4, s4, lower, ALU.mult))
            op(nc.vector.tensor_tensor(m4, m4, s4, ALU.add))
            op(nc.vector.tensor_reduce(by_tile(gmask), m4, op=ALU.add, axis=AX.X))
            op(nc.vector.tensor_scalar(gmask, gmask, TOPK_GROUP - 0.5, None, ALU.is_lt))
            u_times(1, True, (1,))
            gm4 = gmask.unsqueeze(2).broadcast_to([P, TT * EG, EPG])
            k4 = masked.rearrange("p (q e) -> p q e", e=EPG)
            op(nc.vector.tensor_tensor(k4, choice.rearrange("p (q e) -> p q e", e=EPG), gm4, ALU.mult))
            op(nc.vector.tensor_scalar(gmask, gmask, -VERY_NEGATIVE, VERY_NEGATIVE, ALU.mult, ALU.add))
            op(nc.vector.tensor_tensor(k4, k4, gm4, ALU.add))
            act_low(1)
            u_times(2, chunks=(0,))
            for t in range(TT):
                ins = nc.vector.max(out=top8[:, t * 8:(t + 1) * 8],
                                    in_=masked[:, t * E_ROUTED:(t + 1) * E_ROUTED])
            op(ins)
            least = spread(by_tile(top8)[:, :, TOP_K - 1], E_ROUTED)
            op(nc.vector.tensor_tensor(by_tile(more), by_tile(masked), least, ALU.is_gt),
               nc.vector.tensor_tensor(by_tile(same), by_tile(masked), least, ALU.is_equal))
            above = gpair[:, 0:TT]
            op(nc.vector.tensor_reduce(above, by_tile(more), op=ALU.add, axis=AX.X),
               nc.vector.tensor_tensor_scan(before, tile_start, same, 0.0, ALU.mult, ALU.add))
            u_times(2, chunks=(1,))
            op(nc.vector.tensor_tensor(by_tile(before), by_tile(before), spread(above, E_ROUTED), ALU.add))
            op(nc.vector.tensor_scalar(before, before, TOP_K + 0.5, None, ALU.is_lt))
            op(nc.vector.tensor_tensor(same, same, before, ALU.mult))
            op(nc.vector.tensor_tensor(same, same, more, ALU.add))
            op(nc.vector.tensor_tensor(weight, same, score, ALU.mult))
            dn = denom[:, 0:TT]
            op(nc.vector.tensor_reduce(dn, by_tile(weight), op=ALU.add, axis=AX.X))
            op(nc.vector.tensor_scalar(dn, dn, 1e-20, None, ALU.add))
            op(nc.vector.reciprocal(dn, dn))
            op(nc.vector.tensor_scalar(dn, dn, ROUTED_SCALE, None, ALU.mult))
            nc.vector.tensor_tensor(by_tile(weight), by_tile(weight), spread(dn, E_ROUTED),
                                    ALU.mult).then_inc(r_ready, 1)

            act_low(2)
            with dve.Fori(0, E_ROUTED // 2) as r:
                for s in range(2):
                    u_times(r * 2 + (3 + s))
                    act_low(r * 2 + (3 + s))
            for u in range(TT // 2):
                dve.wait_ge(y_full, u + 1)
                xs = x[:, u * N:(u + 1) * N]
                nc.vector.tensor_tensor(xs, y_acc[u][:, :], xs, ALU.add).then_inc(y_added, 1)

        @block.tensor
        def _(pe):
            def mm(o, l, r, start, stop):
                return nc.tensor.matmul(o, l, r, start=start, stop=stop)

            def mm3(o, l_hi, l_lo, r_hi, r_lo, start, stop, loose=False):
                nc.tensor.matmul(o, l_hi, r_lo, start=start, stop=False, skip_group_check=loose)
                nc.tensor.matmul(o, l_lo, r_hi, start=False, stop=False, skip_group_check=loose)
                return nc.tensor.matmul(o, l_hi, r_hi, start=False, stop=stop, skip_group_check=loose)

            def half_transpose(i, c):
                pe.wait_ge(ln_norm_act, 2 * (NCH * i + c + 1))
                pe.wait_ge(ln_norm_dve, 2 * (NCH * i + c + 1))
                for kt in range(KT):
                    for j in range(G):
                        t = c * G + j
                        ins = nc.tensor.transpose(bank[2 * c + kt][:, j * P:(j + 1) * P],
                                                  x_norm[:, t * D + kt * P:t * D + (kt + 1) * P], ident[:, :])
                    ins.then_inc(ln_full, 1)

            pe.wait_ge(ld["ctx"], 48)
            for u in range(2 * NCH):
                s, c = divmod(u, NCH)
                mm(bank[4 + u][:, :], xw[:, s * P:(s + 1) * P], ctxT[:, c * N:(c + 1) * N],
                   True, True).then_inc(x_qk_full, 1)

            def energies(some):
                for t in some:
                    b = t // KT
                    ins = mm(bank[4 + t // 2][:, (t % 2) * L:(t % 2 + 1) * L], qctx[:, t * P:(t + 1) * P],
                             kctx[:, b * L:(b + 1) * L], True, True)
                    if t % 2:
                        ins.then_inc(x_energy, 1)

            pe.wait_ge(x_qk_ready, 2 * NCH)
            energies(range(TT // 2))
            pe.wait_ge(ld["const"], 16)
            for c in range(NCH):
                half_transpose(0, c)
            energies(range(TT // 2, TT))

            def context_weights():
                pe.wait_ge(x_soft, TT)
                for u in range(KT * NCH):
                    nt, c = divmod(u, NCH)
                    for j in range(G):
                        t = c * G + j
                        ins = nc.tensor.transpose(bank[4 + u][:, j * P:(j + 1) * P],
                                                  att[:, t * L + nt * P:t * L + (nt + 1) * P], ident[:, :])
                    ins.then_inc(x_attT_full, 1)

            def beta_logits():
                pe.wait_ge(b_lo_ready, 1)
                for c in range(NCH):
                    for kt in range(KT):
                        w = slice(kt * H, (kt + 1) * H)
                        ins = mm3(bank[2 + c][0:H, :], wb_hi[:, w], wb_lo[:, w],
                                  xs_(xT_hi, kt, c * N, (c + 1) * N), xs_(xT_lo, kt, c * N, (c + 1) * N),
                                  kt == 0, kt == KT - 1)
                    ins.then_inc(b_full, 1)

            def beta_tokens():
                pe.wait_ge(b_ready, NCH)
                for t in range(TT):
                    ins = nc.tensor.transpose(bank[2][:, t * H:(t + 1) * H], betaT[:, t * P:(t + 1) * P],
                                              ident[0:H, 0:H])
                ins.then_inc(b_tok_full, 1)

            def xs_(t_, kt, a, b):
                return t_[:, kt * T + a:kt * T + b]

            def values_of(at, s, units, split):
                pe.wait_ge(wv_lo_ready, split)
                for i, u in enumerate(units):
                    if not (isinstance(at, int) and at + i < 2):
                        pe.wait_ge(c_drained, at + (i - 1))
                    for j in range(2):
                        t = 2 * u + j
                        for kt in range(KT):
                            w = slice(s * N + kt * PW, s * N + (kt + 1) * PW)
                            ins = mm3(c_ring[i % 2][:, j * PW:(j + 1) * PW], xs_(xT_hi, kt, t * P, (t + 1) * P),
                                      xs_(xT_lo, kt, t * P, (t + 1) * P), wv_hi[:, w], wv_lo[:, w],
                                      kt == 0, kt == KT - 1)
                    ins.then_inc(c_full, 1)

            def project_in(g, k, what, chunks=range(NCH)):
                s = k % 2
                if what == 0:
                    pe.wait_ge(w_lo_ready, units(g, k, 1, 1))
                for c in chunks:
                    u = what * NCH + c
                    if not (isinstance(g, int) and G * g + k < 1 and u < 2):
                        pe.wait_ge(a_drained, units(g, k, 6, u - 1))
                    for kt in range(KT):
                        o = s * 3 * D + what * D + kt * P
                        ins = mm3(a_ring[c % 2][:, :], w_hi[:, o:o + P], w_lo[:, o:o + P],
                                  xs_(xT_hi, kt, c * N, (c + 1) * N), xs_(xT_lo, kt, c * N, (c + 1) * N),
                                  kt == 0, kt == KT - 1)
                    ins.then_inc(a_full, 1)

            def to_tokens(g, k):
                for u in range(2 * NCH):
                    pe.wait_ge(silu_done, units(g, k, 4, u + 1))
                    if not (isinstance(g, int) and G * g + k < 1):
                        pe.wait_ge(t_drained, units(g, k, 8, u - 3))
                    for i in range(G):
                        t = u * G + i
                        ins = nc.tensor.transpose(t_ring[u][:, i * P:(i + 1) * P], conv[:, t * P:(t + 1) * P],
                                                  ident[:, :])
                    ins.then_inc(t_full, 1)

            def to_features(g, k):
                for u in range(2 * NCH):
                    pe.wait_ge(t_drained, units(g, k, 8, u + 1))
                    for i in range(G):
                        t = u * G + i
                        ins = nc.tensor.transpose(t_ring[u][:, i * P:(i + 1) * P], tok[:, t * P:(t + 1) * P],
                                                  ident[:, :])
                    ins.then_inc(t_full, 1)

            def scores(g, k, part):
                if part == 0:
                    pe.wait_ge(t_drained, units(g, k, 8, 8))
                for b in (2 * part, 2 * part + 1):
                    pe.wait_ge(c_drained, c_scores(g, k) + (b - 1))
                    q0, k0 = b * L, T + b * L
                    mm(c_ring[b % 2][:, 0:L], qk[:, k0:k0 + P], qk[:, q0:q0 + L], True, True)
                    mm(c_ring[b % 2][:, L:DW], qk[:, k0 + P:k0 + L], qk[:, q0 + P:q0 + L],
                       True, True).then_inc(c_full, 1)

            def outputs(g, k):
                for c in range(NCH):
                    pe.wait_ge(c_drained, c_outputs(g, k) + (c - 1))
                    for i in range(BPC):
                        b = c * BPC + i
                        v = (k // 2) * TT * PW + 2 * b * PW + (k % 2) * P
                        v0, v1 = values[:, v:v + P], values[:, v + PW:v + PW + P]
                        o = c_ring[c % 2]
                        mm(o[:, i * L:(i + 1) * L], v0, probs[:, b * DW:b * DW + L], True, False)
                        ins = mm(o[:, i * L + P:(i + 1) * L], v1, probs[:, b * DW + L:(b + 1) * DW], False, True)
                    ins.then_inc(c_full, 1)

            def project_out(g, k):
                s = (k // 2 + 1) % 2
                pe.wait_ge(wo_lo_ready, g * 2 + k // 2)
                pe.wait_ge(gated_lo_ready, units(g, k, NCH, -1 - k % 2))
                for i in range(2):
                    pe.wait_ge(c_drained, c_project(g, k) + (i - 1))
                    for j in range(2):
                        t = 4 * (k % 2) + 2 * i + j
                        for h in range(2):
                            hh = 2 * s + h
                            gt, w = slice(hh * T + t * P, hh * T + (t + 1) * P), slice(hh * D, (hh + 1) * D)
                            ins = mm3(c_ring[i][:, j * D:(j + 1) * D], gated_hi[:, gt], gated_lo[:, gt],
                                      wo_hi[:, w], wo_lo[:, w], h == 0, h == 1)
                    ins.then_inc(c_full, 1)

            def project_last(h, u):
                hh = 2 * ((NP - 1) % 2) + h
                for j in range(2):
                    t = 2 * u + j
                    o = bank[u][:, j * D:(j + 1) * D]
                    gt, w = slice(hh * T + t * P, hh * T + (t + 1) * P), slice(hh * D, (hh + 1) * D)
                    if h == 0:
                        mm3(o, gated_hi[:, gt], gated_lo[:, gt], wo_hi[:, w], wo_lo[:, w], j == 0, False,
                            loose=True)
                    else:
                        ins = nc.tensor.matmul(o, gated[:, t * P:(t + 1) * P], wo_raw[:, D:2 * D],
                                               start=False, stop=True, skip_group_check=True)
                        if j:
                            ins.then_inc(p_full, 1)

            pe.wait_ge(ln_split, KT * NCH)
            project_in(0, 0, 0)
            beta_logits()
            project_in(0, 0, 1)
            beta_tokens()
            context_weights()
            project_in(0, 0, 2)
            pe.wait_ge(x_attT_ready, KT * NCH)
            values_of(0, 0, range(V_UNITS), 1)
            pe.wait_ge(b_tok_ready, 1)
            to_tokens(0, 0)
            for what in range(3):
                project_in(0, 1, what)

            def step(g, k):
                n = G * g + k if isinstance(g, int) else None
                to_features(g, k)
                if n is None or n + 2 < H:
                    project_in(*head(g, k + 2), 0)
                if n is None or n + 1 < H:
                    to_tokens(*head(g, k + 1))
                if n is None or n + 2 < H:
                    project_in(*head(g, k + 2), 1)
                if n is None or n > 1:
                    project_out(g, k)
                if n == H - 1:
                    pe.wait_ge(wo_lo_ready, NP)
                    pe.wait_ge(gated_lo_ready, NCH * n - 1)
                    for u in (0, 1):
                        project_last(0, u)
                if n is None or n + 2 < H:
                    project_in(*head(g, k + 2), 2, (0,))
                scores(g, k, 0)
                if n is None or n + 2 < H:
                    project_in(*head(g, k + 2), 2, (1,))
                scores(g, k, 1)
                if n is None or n + 2 < H:
                    values_of(c_values(g, k), (k // 2 + 1) % 2, (2 * (k % 2), 2 * (k % 2) + 1),
                              g * 2 + (k // 2 + 2))
                if n == H - 1:
                    pe.wait_ge(gated_lo_ready, NCH * n)
                    for u in (2, 3):
                        project_last(0, u)
                outputs(g, k)

            step(0, 0)
            step(0, 1)
            with pe.Fori(0, NG - 1) as g:
                for k in (2, 3):
                    step(g, k)
                for k in (0, 1):
                    step(g + 1, k)
            for k in (2, 3):
                step(NG - 1, k)

            for u in range(TT // 2):
                pe.wait_ge(c_drained, c_outputs(NG - 1, G - 1) + (u // 2 + 1))
                project_last(1, u)

            for c in range(NCH):
                half_transpose(1, c)
            for c in range(NCH):
                pe.wait_ge(ln_out, (NCH + c + 1) * KT)
                for u in (2 * c, 2 * c + 1):
                    for i in range(2):
                        t = 2 * u + i
                        for nt in range(KT):
                            ins = mm(bank[4 + u][:, i * D:(i + 1) * D],
                                     xT[:, nt * T + t * P:nt * T + (t + 1) * P],
                                     attT[:, nt * T + (t // KT) * L:nt * T + (t // KT + 1) * L],
                                     nt == 0, nt == KT - 1)
                    ins.then_inc(x_mix_full, 1)

            def router_logits(c):
                pe.wait_ge(r_lo_ready, 1)
                for kt in range(KT):
                    w = slice(kt * H, (kt + 1) * H)
                    ins = mm3(bank[4 + c][0:E_ROUTED, :], rw_hi[:, w], rw_lo[:, w],
                              xs_(xT_hi, kt, c * N, (c + 1) * N), xs_(xT_lo, kt, c * N, (c + 1) * N),
                              kt == 0, kt == KT - 1)
                ins.then_inc(r_full, 1)

            def gate_up(n, s, first=False, chunks=range(NCH)):
                pe.wait_ge(w_lo_ready, n + H)
                for c in chunks:
                    for j in range(2):
                        if not first:
                            pe.wait_ge(g_silu if j == 0 else u_prod, (n - 2) * NCH + c + 1)
                        for kt in range(KT):
                            o = s * 3 * D + j * D + kt * P
                            ins = mm3(e_ring[2 * c + j][:, :], w_hi[:, o:o + P], w_lo[:, o:o + P],
                                      xs_(xT_hi, kt, c * N, (c + 1) * N), xs_(xT_lo, kt, c * N, (c + 1) * N),
                                      kt == 0, kt == KT - 1)
                        ins.then_inc(e_full, 1)

            def down(n, s, first, last):
                if not (isinstance(n, int) and n <= E_SHARED):
                    pe.wait_ge(down_lo_ready, n - E_SHARED)
                o = s * 3 * D + 2 * D
                for t in range(TT):
                    if t % G == 0:
                        pe.wait_ge(e_lo, (n - 1) * NCH + t // G + 1)
                    tt = slice(t * P, (t + 1) * P)
                    ins = mm3(y_acc[t // 2][:, (t % 2) * D:(t % 2 + 1) * D], act_hi[:, tt], act_lo[:, tt],
                              w_hi[:, o:o + D], w_lo[:, o:o + D], first and t % 2 == 0, last, loose=True)
                    if last and t % 2:
                        ins.then_inc(y_full, 1)
                if not last:
                    ins.then_inc(e_down, 1)

            for c in range(NCH):
                half_transpose(2, c)
            for c in range(NCH):
                pe.wait_ge(ln_split, KT * NCH + (c + 1) * KT)
                router_logits(c)
            gate_up(1, 0, True, (0,))
            pe.wait_ge(r_score, NCH)
            for t in range(TT):
                ins = nc.tensor.transpose(bank[4][:, t * E_ROUTED:(t + 1) * E_ROUTED],
                                          scoreT[:, t * P:(t + 1) * P], ident[0:E_ROUTED, 0:E_ROUTED])
            ins.then_inc(r_tok_full, 1)
            gate_up(1, 0, True, (1,))
            gate_up(2, 1)
            pe.wait_ge(r_tok_ready, 1)
            down(1, 0, True, False)
            gate_up(3, 0, chunks=(0,))
            pe.wait_ge(r_ready, 1)
            pe.wait_ge(g_silu, 2 * NCH)
            pe.wait_ge(u_prod, 2 * NCH)
            for c in range(NCH):
                for j in range(G):
                    t = c * G + j
                    ins = nc.tensor.transpose(e_ring[2 + c][0:E_ROUTED, j * P:(j + 1) * P],
                                              weight[:, t * E_ROUTED:(t + 1) * E_ROUTED], ident[:, :])
                ins.then_inc(r_tr_full, 1)
            pe.wait_ge(r_tr_ready, NCH)
            gate_up(3, 0, chunks=(1,))
            down(2, 1, False, False)
            gate_up(4, 1)
            down(3, 0, False, False)
            with pe.Fori(0, E_ROUTED // 2 - 1) as r:
                for s in range(2):
                    gate_up(r * 2 + (5 + s), s)
                    down(r * 2 + (4 + s), 1 - s, False, False)
            down(E_ALL, 1, False, True)


def kernel(**inputs):
    import numpy as np
    import concourse.bacc as bacc
    from concourse.bass_utils import run_bass_kernel_spmd

    a = {k: np.asarray(v) for k, v in inputs.items()}

    def tiles(w):
        return w.reshape(KT, P, -1).transpose(1, 0, 2)

    def tokens(v):
        return v.reshape(TT, P, D).transpose(1, 0, 2).reshape(P, TT * D)

    heads = [tiles(a[f"L0_attn_{n}"]).reshape(P, KT, H, P).transpose(2, 0, 1, 3) for n in ("Wq", "Wk", "Wg")]
    wh = np.stack(heads, axis=2).reshape(H, P, 3 * D)
    prm = []
    for n in "qk":
        cw = a[f"L0_attn_{n}conv_w"].reshape(H, P, TAPS)
        cb = a[f"L0_attn_{n}conv_b"].reshape(H, P, 1)
        nw, nb = (np.broadcast_to(a[f"L0_attn_{n}n_{s}"].reshape(1, P, 1), (H, P, 1)) for s in "wb")
        prm += [cw, cb, nw, nb]
    prm = np.concatenate(prm, axis=2)
    wv = tiles(a["L0_attn_Wv"]).reshape(P, KT, NP, PW).transpose(2, 0, 1, 3).reshape(NP, P, KT * PW)
    wo = a["L0_attn_Wo"].reshape(NP, 2, P, D).transpose(0, 2, 1, 3).reshape(NP, P, 2 * D)

    def up(w):
        return w.reshape(-1, P, KT, P).transpose(0, 3, 2, 1).reshape(-1, P, D)

    gw = np.concatenate([up(a["L0_ffn_sh_gate_w"]), up(a["L0_ffn_gate_w"])])
    uw = np.concatenate([up(a["L0_ffn_sh_up_w"]), up(a["L0_ffn_up_w"])])
    dw = np.concatenate([a["L0_ffn_sh_down_w"].reshape(D, E_SHARED, P).transpose(1, 2, 0),
                         a["L0_ffn_down_w"].transpose(0, 2, 1)])
    we = np.concatenate([gw, uw, dw], axis=2)
    lower = np.broadcast_to(np.tril(np.ones((EG, EG), np.float32), -1).reshape(1, EG * EG), (P, EG * EG))
    arrays = {
        "x": tokens(a["x"]),
        "ctx": a["ctx_1024"].reshape(T, P).T,
        "xw": np.concatenate([a["L0_xattn_Wq"].T, a["L0_xattn_Wk"].T], axis=1),
        "xb": np.stack([a["L0_xattn_bq"], a["L0_xattn_bk"]], axis=1),
        "wb": tiles(a["L0_attn_Wb"]).reshape(P, KT * H),
        "bb": a["L0_attn_bb"].reshape(H, 1),
        "w": np.concatenate([wh, we]), "prm": prm, "wv": wv, "wo": wo,
        "rw": tiles(a["L0_ffn_gate_weight"].T).reshape(P, KT * E_ROUTED),
        "rb": a["L0_ffn_e_score_correction_bias"].reshape(1, E_ROUTED),
        "ident": np.eye(P, dtype=np.float32),
        "tie": lower,
    }
    arrays = {f"in_{k}": np.ascontiguousarray(v) for k, v in arrays.items()}
    nc = bacc.Bacc("TRN2", target_bir_lowering=False, num_devices=1)
    args = [nc.dram_tensor(k, v.shape, mybir.dt.from_np(v.dtype), kind="ExternalInput").ap()
            for k, v in arrays.items()]
    out = nc.dram_tensor("out_x", [P, TT * D], F32, kind="ExternalOutput").ap()
    decoder_layer(nc, *args, out)
    r = run_bass_kernel_spmd(nc, [arrays], core_ids=[0])
    got = np.asarray(r.results[0]["out_x"])
    return got.reshape(P, TT, D).transpose(1, 0, 2).reshape(B, L, D)
```
